# Optimizing a Trainium2 kernel written in Bass

```python
import numpy as np
import jax
import jax.numpy as jnp

def _softmax(x, axis=-1):
    return jax.nn.softmax(x, axis=axis)

def _gelu(x):
    return jax.nn.gelu(x, approximate=True)

def _silu(x):
    return jax.nn.silu(x)

def _sigmoid(x):
    return jax.nn.sigmoid(x)

def _layernorm(x, axis=-1, eps=1e-05):
    m = jnp.mean(x, axis=axis, keepdims=True)
    v = jnp.var(x, axis=axis, keepdims=True)
    return (x - m) / jnp.sqrt(v + eps)

def _scatter_add(tgt, idx, src, axis=0):
    return tgt.at[idx].add(src)

def _segment_sum(src, seg, n):
    return jax.ops.segment_sum(src, seg, n)
kernel_name = 'mk_gnn_resnorm_d2_gnn_r32_91091a'

def setup_inputs(seed: int=0):
    np.random.seed(seed)
    _w = jnp.asarray

    def _rec_inputs():
        import jax
        import jax.numpy as jnp
        _gk = jax.random.key(seed)
        x = -0.000202 + 1 * jax.random.normal(jax.random.fold_in(_gk, 1), (50000, 128), jnp.float32)
        src = jax.random.randint(jax.random.fold_in(_gk, 2), (25000,), 0, 50000, jnp.int32)
        dst = jax.random.randint(jax.random.fold_in(_gk, 3), (25000,), 0, 50000, jnp.int32)
        _o = jnp.argsort(dst, stable=True)
        src = src[_o]
        dst = dst[_o]
        edge_attr_64 = 0.000196303 + 1.00016 * jax.random.normal(jax.random.fold_in(_gk, 13), (25000, 64), jnp.float32)
        return (x, src, dst, edge_attr_64)
    x, src, dst, edge_attr_64 = _rec_inputs()

    def _L0_gnn_setup():
        import jax, jax.numpy as jnp
        import numpy as np
        N_NODES = 50000
        N_EDGES = 25000
        IN_FEATS = 128
        OUT_FEATS = 128
        key = jax.random.key(seed)
        k1, k2, k3, k4, k5, k6 = jax.random.split(key, 6)
        features = jax.random.normal(k1, (N_NODES, IN_FEATS), dtype=jnp.float32)
        norm = jax.random.uniform(k2, (N_NODES, 1), dtype=jnp.float32)
        W = jax.random.normal(k3, (OUT_FEATS, IN_FEATS), dtype=jnp.float32) * (1.0 / np.sqrt(IN_FEATS))
        b = jax.random.normal(k4, (OUT_FEATS,), dtype=jnp.float32) * 0.01
        src = jax.random.randint(k5, (N_EDGES,), 0, N_NODES, dtype=jnp.int32)
        dst = jax.random.randint(k6, (N_EDGES,), 0, N_NODES, dtype=jnp.int32)
        return {'features': features, 'norm': norm, 'W': W, 'b': b, 'src': src, 'dst': dst}
    _L0_gnn_all = _L0_gnn_setup()
    _L0_gnn_in = {k: v for k, v in _L0_gnn_all.items() if k in ('W', 'b')}
    del _L0_gnn_all

    def _L1_gnn_setup():
        import jax, jax.numpy as jnp
        import numpy as np
        N, E = (50000, 12500)
        NODE_DIM, EDGE_DIM = (128, 64)
        MSG_IN = 2 * NODE_DIM + EDGE_DIM
        key = jax.random.key(seed)
        ks = jax.random.split(key, 12)
        h = jax.random.normal(ks[0], (N, NODE_DIM), dtype=jnp.float32)
        edge_index = jax.random.randint(ks[1], (2, E), 0, N, dtype=jnp.int64)
        e = jax.random.normal(ks[2], (E, EDGE_DIM), dtype=jnp.float32)

        def lin(k, fan_in, fan_out):
            bound = 1.0 / np.sqrt(fan_in)
            k1, k2 = jax.random.split(k)
            w = jax.random.uniform(k1, (fan_in, fan_out), minval=-bound, maxval=bound, dtype=jnp.float32)
            b = jax.random.uniform(k2, (fan_out,), minval=-bound, maxval=bound, dtype=jnp.float32)
            return (w, b)
        w1, b1 = lin(ks[3], MSG_IN, NODE_DIM)
        w2, b2 = lin(ks[4], NODE_DIM, NODE_DIM)
        wg, bg = lin(ks[5], MSG_IN, NODE_DIM)
        wu, bu = lin(ks[6], 2 * NODE_DIM, NODE_DIM)
        return {'h': h, 'edge_index': edge_index, 'e': e, 'w1': w1, 'b1': b1, 'w2': w2, 'b2': b2, 'wg': wg, 'bg': bg, 'wu': wu, 'bu': bu}
    _L1_gnn_all = _L1_gnn_setup()
    _L1_gnn_in = {k: v for k, v in _L1_gnn_all.items() if k in ('w1', 'b1', 'w2', 'b2', 'wg', 'bg', 'wu', 'bu')}
    del _L1_gnn_all
    return {'x': x, 'src': src, 'dst': dst, 'edge_attr_64': edge_attr_64, 'L0_gnn_W': _L0_gnn_in['W'], 'L0_gnn_b': _L0_gnn_in['b'], 'L1_gnn_w1': _L1_gnn_in['w1'], 'L1_gnn_b1': _L1_gnn_in['b1'], 'L1_gnn_w2': _L1_gnn_in['w2'], 'L1_gnn_b2': _L1_gnn_in['b2'], 'L1_gnn_wg': _L1_gnn_in['wg'], 'L1_gnn_bg': _L1_gnn_in['bg'], 'L1_gnn_wu': _L1_gnn_in['wu'], 'L1_gnn_bu': _L1_gnn_in['bu']}

def reference(x, src, dst, edge_attr_64, L0_gnn_W, L0_gnn_b, L1_gnn_w1, L1_gnn_b1, L1_gnn_w2, L1_gnn_b2, L1_gnn_wg, L1_gnn_bg, L1_gnn_wu, L1_gnn_bu):
    import jax
    import jax.numpy as jnp

    def _L0_gnn_ref(features, norm, W, b, src, dst):
        import jax, jax.numpy as jnp
        import numpy as np
        N_NODES = 50000
        N_EDGES = 25000
        IN_FEATS = 128
        OUT_FEATS = 128
        msg = features[src] * norm[src]
        agg = jax.ops.segment_sum(msg, dst, num_segments=N_NODES) * norm
        h = jnp.tanh(agg @ W.T + b)
        return h

    def _L1_gnn_ref(h, edge_index, e, w1, b1, w2, b2, wg, bg, wu, bu):
        import jax, jax.numpy as jnp
        import numpy as np
        N, E = (50000, 12500)
        NODE_DIM, EDGE_DIM = (128, 64)
        MSG_IN = 2 * NODE_DIM + EDGE_DIM
        src, dst = (edge_index[0], edge_index[1])
        msg_in = jnp.concatenate([h[src], h[dst], e], axis=-1)
        messages = jax.nn.silu(msg_in @ w1 + b1) @ w2 + b2
        gates = jax.nn.sigmoid(msg_in @ wg + bg)
        messages = messages * gates
        n = h.shape[0]
        agg = jax.ops.segment_sum(messages, dst, num_segments=n)
        deg = jax.ops.segment_sum(jnp.ones((dst.shape[0],), h.dtype), dst, num_segments=n)
        agg = agg / jnp.maximum(deg, 1.0)[:, None]
        h_new = jax.nn.silu(jnp.concatenate([h, agg], axis=-1) @ wu + bu)
        return h_new
    edge_index = jnp.stack([src, dst])
    deg = jnp.maximum(jax.ops.segment_sum(jnp.ones(dst.shape, jnp.float32), dst, num_segments=50000), 1.0)
    deg_isqrt = deg ** (-0.5)
    x = _layernorm(x + _L0_gnn_ref(x, deg_isqrt[:, None], L0_gnn_W, L0_gnn_b, src, dst), axis=-1)
    x = _layernorm(x + _L1_gnn_ref(x, edge_index, edge_attr_64, L1_gnn_w1, L1_gnn_b1, L1_gnn_w2, L1_gnn_b2, L1_gnn_wg, L1_gnn_bg, L1_gnn_wu, L1_gnn_bu), axis=-1)
    return x

_drawn_inputs = setup_inputs


def setup_inputs(seed=0):
    import zlib

    import numpy as np

    out = dict(_drawn_inputs(seed))
    spreads = {}
    factors = {'edge_attr_64': 8.0,
     'L0_gnn_b': 6.399,
     'L1_gnn_w1': 4.822,
     'L1_gnn_b1': 22.464,
     'L1_gnn_w2': 4.684,
     'L1_gnn_b2': 26.678,
     'L1_gnn_wg': 8.0,
     'L1_gnn_bg': 26.133,
     'L1_gnn_bu': 3.293}
    for name, (base, spread) in spreads.items():
        noise = np.random.default_rng([zlib.crc32(name.encode()), seed]).standard_normal(out[name].shape)
        drawn = base * np.exp(spread * noise) if base else spread * noise
        out[name] = jnp.asarray(drawn.astype(out[name].dtype))
    for name, factor in factors.items():
        out[name] = (out[name] * factor).astype(out[name].dtype)
    return out
```

```python
import numpy as np
import concourse.bass as bass
from concourse import mybir
from contextlib import ExitStack

F32, I32, F16, BF16 = mybir.dt.float32, mybir.dt.int32, mybir.dt.float16, mybir.dt.bfloat16
ALU, ACT = mybir.AluOpType, mybir.ActivationFunctionType


def gnn_kernel(nc, x, src, dst, edge_attr, W, b, w1, b1, w2, b2, wg, bg, wu, bu, out):
    P = 128
    N, D = x.shape
    E = src.shape[0]
    DE = edge_attr.shape[1]
    K = P - 2
    GT = 4
    T_REAL = -(-E // K)
    T = -(-T_REAL // (2 * GT)) * 2 * GT
    G = T // GT
    STEPS = G // 2
    SLOTS = T * P
    LAST_ROWS = E - (T_REAL - 1) * K
    NODE_GROUP = GT * P
    NG = -(-N // NODE_GROUP)
    NG_LAST_P = (N - (NG - 1) * NODE_GROUP) // GT
    PAIRS = NG // 2
    assert NG % 2 == 0 and 2 * (STEPS - 1) == PAIRS - 1 and (N - (NG - 1) * NODE_GROUP) % GT == 0
    HI = -(-N // P)
    HC = -(-HI // P)
    NO_KEY = 65535.0
    SKIP = 70000.0
    FAR = 1.0e6
    EPS = 1e-5
    C1_TILES = T_REAL - P

    def dram(name, shape, dt):
        return nc.dram_tensor(name, shape, dt, kind="Internal").ap()

    key_rows = dram("key_rows", (T, P), F32)
    node_tab = dram("node_tab", (HI * P, 2), F32)
    src_feat = dram("src_feat", (SLOTS, D), F32)
    messages = dram("messages", (SLOTS, D), F32)
    x1_tab = dram("x1_tab", (SLOTS + N, D), F32)

    def slots_of(tab, g):
        return tab[bass.ds(g * (GT * P), GT * P), :].rearrange("(t s) d -> s t d", s=P)

    def nodes_of(tab, g, base=0, parts=P):
        return tab[bass.ds(g * NODE_GROUP + base, parts * GT), :].rearrange("(p j) d -> p (j d)", j=GT)

    ctx = ExitStack()
    with ctx:
        def sb(name, shape, dt=F32):
            return ctx.enter_context(nc.sbuf_tensor(name, shape, dt))

        def sem(name):
            return ctx.enter_context(nc.semaphore(name))

        bank = [ctx.enter_context(nc.psum_tensor(f"bank{i}", [P, 512], F32)) for i in range(8)]

        ident = sb("ident", [P, P])
        before = sb("before", [P, P])
        ones = sb("ones", [P, 512])
        onesb = sb("onesb", [P, P], BF16)
        zerosb = sb("zerosb", [P, 512], BF16)
        neg_half = sb("neg_half", [P, HI])
        iota_i = sb("iota_i", [P, HI], I32)
        iota_h = sb("iota_h", [P, HI], F16)
        node_i = sb("node_i", [P, HI], I32)
        edge_i = sb("edge_i", [P, 2, K], I32)
        third_m = sb("third_m", [P, 3])
        Wsb, WT = sb("Wsb", [P, D]), sb("WT", [P, D])
        w1s, w1d, w1e = sb("w1s", [P, D]), sb("w1d", [P, D]), sb("w1e", [DE, D])
        wgs, wgd, wge = sb("wgs", [P, D]), sb("wgd", [P, D]), sb("wge", [DE, D])
        w2sb, wux, wua = sb("w2sb", [P, D]), sb("wux", [P, D]), sb("wua", [P, D])
        b1c = sb("b1c", [P, 1])
        bias_in = sb("bias_in", [P, 4, D])
        bias_rest = sb("bias_rest", [P, 4, D])
        bias_part = sb("bias_part", [P, 4, D], BF16)
        bias3 = sb("bias3", [P, 4, D], BF16)
        plain_h = sb("plain_h", [P, D])
        B_B, B_B2, B_BG, B_BU = range(4)

        dst_i, src_i = sb("dst_i", [P, 2, K], I32), sb("src_i", [P, 2, K], I32)
        prev_i, next_i = sb("prev_i", [P, 2], I32), sb("next_i", [P, 2], I32)
        prev_f, next_f = sb("prev_f", [P, 2]), sb("next_f", [P, 2])
        QK, QS, QD, QB, QF, QL = range(6)
        rows = sb("rows", [P, 6, 2, P])
        edge_f = sb("edge_f", [P, 2, K])
        run_last = sb("run_last", [P, 2, K])
        scan_in, scan_lo, scan_hi = sb("scan_in", [P, 2, K]), sb("scan_lo", [P, 2, K]), sb("scan_hi", [P, 2, K])
        scan_in2 = sb("scan_in2", [P, 2, K])
        tile_flags = sb("tile_flags", [P, 2, 2])
        line = sb("line", [1, 4, 2 * P])
        line_sc, line_ex = sb("line_sc", [1, 2, 2 * P]), sb("line_ex", [1, 2, 2 * P])
        run_carry = sb("run_carry", [P, 2, 2])
        linked, whole = sb("linked", [P, 2 * P]), sb("whole", [P, 2 * P])
        cols = sb("cols", [P, 4, T])
        firstlast = sb("firstlast", [P, T, 2])
        valid, tmp_c = sb("valid", [P, T]), sb("tmp_c", [P, T])
        idx_src, idx_dst = sb("idx_src", [P, T], I32), sb("idx_dst", [P, T], I32)
        idx_out, idx_x1 = sb("idx_out", [P, T], I32), sb("idx_x1", [P, T], I32)
        rdst, weight0, weight1 = sb("rdst", [P, T]), sb("weight0", [P, T]), sb("weight1", [P, T])
        hi_i, hi_f, lo_f = sb("hi_i", [P, T], I32), sb("hi_f", [P, T]), sb("lo_f", [P, T])
        hot_lo, hot_hi = sb("hot_lo", [P, 2, GT, P], F16), sb("hot_hi", [P, 2, GT, HI], F16)
        tab_flat = sb("tab_flat", [P, 8 * HI])
        tab = tab_flat[:, :].rearrange("p (a h) -> p a h", a=8)
        tab_i = sb("tab_i", [P, HI], I32)
        tab_out = sb("tab_out", [P, HC, P, 2])
        part = sb("part", [P, 2, T])
        chain_a, chain_b = sb("chain_a", [P, 2, T]), sb("chain_b", [P, 2, T])
        carry = sb("carry", [P, 2, 2 * P])
        carry_rows = sb("carry_rows", [P, 2, 2, P])

        s_consts, s_mask0, s_load, s_idx_ld, s_chain = (sem(n) for n in ("s_consts", "s_mask0", "s_load", "s_idx_ld", "s_chain"))
        s_prefill, s_pe0, s_act0, s_pow0 = (sem(n) for n in ("s_prefill", "s_pe0", "s_act0", "s_pow0"))
        s_wt = sem("s_wt")
        s_keys, s_tab = sem("s_keys"), sem("s_tab")
        s_hot, s_hot_used = sem("s_hot"), sem("s_hot_used")
        s_pool_turn = sem("s_pool_turn")
        s_act_turn = sem("s_act_turn")

        mark = {}

        xs = sb("xs", [P, 2, GT, D])
        tabs = sb("tabs", [P, 2, GT, 2])
        ids_a, ids_b, ids_c, ids_d = (sb(f"ids_{n}", [P, 2, GT], I32) for n in "abcd")
        flw = sb("flw", [P, 2, GT, 2])
        nx = sb("nx", [P, 2, 2 * GT, D])
        nz, nx1 = sb("nz", [P, 2, 2 * GT, D]), sb("nx1", [P, 2, 2 * GT, D])
        nx1T, nh = sb("nx1T", [P, 2, GT * P]), sb("nh", [P, 2, 2 * GT, D])
        nz2, nout = nh, sb("nout", [P, 2, 2 * GT, D])

        class Norm:
            def __init__(self, name, n):
                self.st = sb(name + "_st", [P, 2, n, 6])
                self.tmp = sb(name + "_tmp", [P, 2, 4, n])
                self.mean, self.var, self.rstd = (sb(name + s, [P, 2, n]) for s in ("_mean", "_var", "_rstd"))
                self.s_var, self.s_rstd = sem("s_" + name + "_var"), sem("s_" + name + "_rstd")
                self.n = n

        norm1, norm2 = Norm("norm1", 2 * GT), Norm("norm2", 2 * GT)
        normb, normd = Norm("normb", GT), Norm("normd", GT)

        sA = {n: sem("a_" + n) for n in ("ids", "flw", "part", "partev", "z1", "x1", "T", "Tev", "O", "h", "z2", "out", "xs_free")}
        sA_xs, sA_tab, sA_st = ([sem(f"a_{n}{u}") for u in range(2)] for n in ("xs", "tab", "xst"))
        sA_nx, sA_x1st, sA_outst = ([sem(f"a_{n}{q}") for q in range(2)] for n in ("nx", "x1st", "outst"))
        s_carry0, s_carry1, s_cst0, s_cst1, s_cpe0, s_cpe1 = (sem(n) for n in ("s_carry0", "s_carry1", "s_cst0", "s_cst1", "s_cpe0", "s_cpe1"))

        bxs, bkey, bS = sb("bxs", [P, 2, GT, D]), sb("bkey", [P, 2, GT * P]), sb("bS", [P, 2, GT, P])
        bxd, baT = sb("bxd", [P, 2, GT, D]), sb("baT", [P, 2, GT * P])
        bh, bz, bx1 = sb("bh", [P, 2, GT, D]), sb("bz", [P, 2, GT, D]), sb("bx1", [P, 2, GT, D])
        sB = {n: sem("b_" + n) for n in ("ids", "S", "A", "Aev", "O", "h", "z", "x1")}
        sB_xs, sB_key, sB_xd, sB_st = ([sem(f"b_{n}{u}") for u in range(2)] for n in ("xs", "key", "xd", "st"))

        cxs, cxd, cea = sb("cxs", [P, 2, GT, D]), sb("cxd", [P, 2, GT, D]), sb("cea", [P, 2, GT, DE])
        csT, cdT, ceT = sb("csT", [P, 2, GT * P]), sb("cdT", [P, 2, GT * P]), sb("ceT", [DE, 2, GT * P])
        per = 2 * GT * P
        chT = tab_flat[:, 0:per].rearrange("p (u e) -> p u e", u=2)
        cg, cm = (tab_flat[:, n * per:(n + 1) * per].rearrange("p (u t d) -> p u t d", u=2, t=GT) for n in (1, 2))
        cfl = sb("cfl", [P, 2, GT, 2])
        sC = {n: sem("c_" + n) for n in ("ids", "cfl", "T", "sT", "dT", "eT", "H", "h", "G", "g", "M", "m", "part", "partev")}
        sC_xs, sC_xd, sC_ea, sC_st = ([sem(f"c_{n}{u}") for u in range(2)] for n in ("xs", "xd", "ea", "st"))

        dms, dkey, dS, dxd, daT, dh, dz, dout = bxs, bkey, bS, bxd, baT, bh, bz, bx1
        dxT = csT
        sD = {n: sem("d_" + n) for n in ("ids", "S", "A", "Aev", "T", "Tev", "O", "h", "z", "out")}
        sD_ms, sD_key, sD_xd, sD_st = ([sem(f"d_{n}{u}") for u in range(2)] for n in ("ms", "key", "xd", "st"))

        block = ctx.enter_context(nc.Block())

        def steps(eng, body, count=STEPS):
            body(0)
            with eng.Fori(1, count - 1) as s:
                body(s)
            body(count - 1)

        def first(s):
            return isinstance(s, int) and s == 0

        class Chain:

            def __init__(self, eng, semaphore, share=0):
                self.eng, self.semaphore, self.share, self.base, self.used = eng, semaphore, share, 0, 0

            def begin(self, s):
                self.base, self.used = s * self.share, 0

            def link(self, ins):
                self.used += 1
                ins.then_inc(self.semaphore, 1)
                self.eng.wait_ge(self.semaphore, self.base + self.used)

            def end(self):
                assert self.used <= self.share, self.used
                if self.used < self.share:
                    self.eng.sem_inc(self.semaphore, self.share - self.used)

        @block.vector
        def _(v):
            prep = Chain(v, s_chain)
            link = prep.link
            nc.vector.memset(dst_i[:, :, :], int(NO_KEY))
            nc.vector.memset(src_i[:, :, :], 0)
            nc.vector.memset(next_i[:, :], int(NO_KEY))
            link(nc.vector.memset(prev_i[:, :], int(NO_KEY)))
            nc.vector.memset(prev_i[0:1, 0:1], -1).then_inc(s_prefill, 1)
            nc.vector.memset(cea[:, :, :, :], 0.0)
            nc.vector.memset(onesb[:, :], 1.0)
            nc.vector.memset(zerosb[:, :], 0.0)
            nc.vector.memset(weight0[:, :], 1.0)
            nc.vector.memset(carry[:, :, :], 0.0)
            link(nc.vector.memset(rows[:, :, :, :], 0.0))
            mark["fills"] = prep.used
            v.wait_ge(s_idx_ld, 16 * 10)
            key = rows[:, QK, :, :]
            nc.vector.tensor_copy(rows[:, QS, :, 0:K], src_i[:, :, :])
            nc.vector.tensor_copy(prev_f[:, :], prev_i[:, :])
            nc.vector.tensor_copy(next_f[:, :], next_i[:, :])
            link(nc.vector.tensor_copy(key[:, :, 0:K], dst_i[:, :, :]))
            nc.vector.tensor_copy(key[:, :, K:K + 1], key[:, :, 0:1])
            link(nc.vector.tensor_copy(key[:, :, K + 1:P], key[:, :, K - 1:K]))
            mark["keys"] = prep.used
            v.wait_ge(s_consts, 1)
            nc.vector.tensor_copy(iota_h[:, :], iota_i[:, :])
            link(nc.vector.tensor_copy(edge_f[:, :, :], edge_i[:, :, :]))
            nc.vector.tensor_tensor(rows[:, QB, :, 0:1], key[:, :, 0:1], prev_f[:, :].unsqueeze(2), ALU.not_equal)
            nc.vector.tensor_tensor(rows[:, QB, :, 1:K], key[:, :, 1:K], key[:, :, 0:K - 1], ALU.not_equal)
            nc.vector.tensor_tensor(run_last[:, :, K - 1:K], key[:, :, K - 1:K], next_f[:, :].unsqueeze(2), ALU.not_equal)
            link(nc.vector.tensor_tensor(run_last[:, :, 0:K - 1], key[:, :, 0:K - 1], key[:, :, 1:K], ALU.not_equal))
            nc.vector.tensor_tensor(scan_in[:, :, :], rows[:, QB, :, 0:K], edge_f[:, :, :], ALU.mult)
            link(nc.vector.scalar_tensor_tensor(scan_in2[:, :, :], edge_f[:, :, :], 1.0 - FAR, run_last[:, :, :], ALU.add, ALU.mult))
            link(nc.vector.tensor_scalar(scan_in2[:, :, :], scan_in2[:, :, :], FAR, None, ALU.add))
            for c in range(2):
                nc.vector.tensor_tensor_scan(scan_lo[:, c, :], scan_in[:, c, :], scan_in[:, c, :], 0.0, ALU.max, ALU.max)
                nc.vector.tensor_tensor_scan(scan_hi[:, c, ::-1], scan_in2[:, c, ::-1], scan_in2[:, c, ::-1], FAR, ALU.min, ALU.min)
                nc.vector.tensor_scalar(rows[:, QF, c, 0:K], key[:, c, 0:K], key[:, c, 0:1], None, ALU.is_equal)
                nc.vector.tensor_scalar(rows[:, QL, c, 0:K], key[:, c, 0:K], key[:, c, K - 1:K], None, ALU.is_equal)
            nc.vector.tensor_tensor(tile_flags[:, :, 0:1], key[:, :, 0:1], prev_f[:, :].unsqueeze(2), ALU.is_equal)
            link(nc.vector.tensor_tensor(tile_flags[:, :, 1:2], key[:, :, 0:1], key[:, :, K - 1:K], ALU.is_equal))
            mark["scans"] = prep.used
            v.wait_ge(s_pe0, 1)
            nc.vector.tensor_copy(line[0:1, 0:2, :], bank[0][0:1, 0:512].rearrange("o (a b) -> o a b", a=2))
            link(nc.vector.tensor_copy(line[0:1, 2:4, :], bank[1][0:1, 0:512].rearrange("o (a b) -> o a b", a=2)))
            nc.vector.tensor_tensor_scan(line_sc[:, 0, :], line[:, 0, :], line[:, 0, :], 0.0, ALU.max, ALU.max)
            nc.vector.memset(line_ex[:, 0, 0:1], 0.0)
            nc.vector.memset(line_ex[:, 1, 2 * P - 1:2 * P], FAR)
            link(nc.vector.tensor_tensor_scan(line_sc[:, 1, ::-1], line[:, 1, ::-1], line[:, 1, ::-1], FAR, ALU.min, ALU.min))
            nc.vector.tensor_copy(line_ex[:, 0, 1:2 * P], line_sc[:, 0, 0:2 * P - 1])
            link(nc.vector.tensor_copy(line_ex[:, 1, 0:2 * P - 1], line_sc[:, 1, 1:2 * P]))
            mark["lines"] = prep.used
            v.wait_ge(s_pe0, 2)
            nc.vector.tensor_copy(linked[:, :], bank[3][:, 0:2 * P])
            nc.vector.tensor_copy(whole[:, :], bank[3][:, 2 * P:4 * P])
            link(nc.vector.tensor_copy(run_carry[:, :, :], bank[2][:, 0:4].rearrange("p (a c) -> p a c", a=2)))
            for c in range(2):
                nc.vector.tensor_scalar(scan_lo[:, c, :], scan_lo[:, c, :], run_carry[:, 0, c:c + 1], None, ALU.max)
                ins = nc.vector.tensor_scalar(scan_hi[:, c, :], scan_hi[:, c, :], run_carry[:, 1, c:c + 1], None, ALU.min)
            link(ins)
            nc.vector.memset(rows[:, QD, :, K:P], 0.5)
            link(nc.vector.tensor_tensor(rows[:, QD, :, 0:K], scan_hi[:, :, :], scan_lo[:, :, :], ALU.subtract))
            mark["rows"] = prep.used
            v.wait_ge(s_pe0, 3)
            for n in (QK, QS, QD, QB):
                nc.vector.tensor_copy(cols[:, n, :], bank[n][:, 0:T])
            nc.vector.tensor_copy(firstlast[:, :, 0], bank[QF][:, 0:T])
            link(nc.vector.tensor_copy(firstlast[:, :, 1], bank[QL][:, 0:T]))
            mark["cols"] = prep.used
            ckey = cols[:, QK, :]
            nc.vector.tensor_copy(idx_src[:, :], cols[:, QS, :])
            nc.vector.tensor_scalar(hi_i[:, :], ckey, 0.5 - P / 2, 1.0 / P, ALU.add, ALU.mult)
            nc.vector.reciprocal(weight1[:, :], cols[:, QD, :])
            nc.vector.tensor_scalar(tmp_c[:, :], cols[:, QD, :], 1.0, None, ALU.max)
            link(nc.vector.tensor_scalar(valid[:, :], ckey, 60000.0, None, ALU.is_lt))
            mark["deg"] = prep.used
            nc.vector.tensor_tensor(idx_dst[:, :], ckey, valid[:, :], ALU.mult)
            nc.vector.tensor_tensor(cols[:, QB, :], cols[:, QB, :], valid[:, :], ALU.mult)
            nc.vector.tensor_copy(hi_f[:, :], hi_i[:, :])
            link(nc.vector.scalar_tensor_tensor(weight1[:, :], weight1[:, :], 0.5, valid[:, :], ALU.mult, ALU.mult))
            link(nc.vector.scalar_tensor_tensor(lo_f[:, :], hi_f[:, :], -float(P), ckey, ALU.mult, ALU.add))
            link(nc.vector.scalar_tensor_tensor(cols[:, QB, :], ckey, -SKIP, cols[:, QB, :], ALU.add, ALU.mult))
            nc.vector.tensor_scalar(idx_out[:, :], cols[:, QB, :], SKIP, None, ALU.add)
            v.wait_ge(s_pow0, 1)
            link(nc.vector.tensor_tensor(rdst[:, :], rdst[:, :], valid[:, :], ALU.mult))
            mark["idx"] = prep.used

            def step_hot(s):
                for u in range(2):
                    g = s * 2 + u
                    if not first(s):
                        v.wait_ge(s_hot_used, g - 1)
                    for t in range(GT):
                        at = g * GT + t
                        nc.vector.tensor_scalar(hot_lo[:, u, t, :], iota_h[:, 0:P], lo_f[:, bass.ds(at, 1)], None, ALU.is_equal)
                        ins = nc.vector.tensor_scalar(hot_hi[:, u, t, :], iota_h[:, :], hi_f[:, bass.ds(at, 1)], None, ALU.is_equal)
                    ins.then_inc(s_hot, 1)

            steps(v, step_hot)

            v.wait_ge(s_pe0, 4)
            link(nc.vector.tensor_copy(tab[:, 0, :], bank[7][:, 0:HI]))
            mark["counts"] = prep.used
            nc.vector.tensor_scalar(tab[:, 4, :], tab[:, 0, :], 1.0, None, ALU.max)
            link(nc.vector.tensor_scalar(tab[:, 7, :], node_i[:, :], float(SLOTS), None, ALU.add))
            mark["tabdeg"] = prep.used
            v.wait_ge(s_pe0, 5)
            link(nc.vector.tensor_copy(tab[:, 1, :], bank[1][:, 0:HI]))
            link(nc.vector.tensor_tensor_scan(tab[:, 2, :], ones[:, 0:HI], tab[:, 1, :], 0.0, ALU.mult, ALU.add))
            link(nc.vector.tensor_tensor(tab[:, 3, :], tab[:, 2, :], tab[:, 1, :], ALU.subtract))
            link(nc.vector.tensor_tensor(tab[:, 3, :], tab[:, 3, :], bank[0][:, 0:HI], ALU.add))
            link(nc.vector.tensor_scalar(tab_i[:, :], tab[:, 3, :], 0.5 - K / 2, 1.0 / K, ALU.add, ALU.mult))
            link(nc.vector.tensor_copy(tab[:, 6, :], tab_i[:, :]))
            link(nc.vector.scalar_tensor_tensor(tab[:, 3, :], tab[:, 6, :], float(P - K), tab[:, 3, :], ALU.mult, ALU.add))
            link(nc.vector.tensor_tensor(tab[:, 6, :], tab[:, 3, :], tab[:, 7, :], ALU.subtract))
            link(nc.vector.scalar_tensor_tensor(tab[:, 6, :], tab[:, 0, :], 0.0, tab[:, 6, :], ALU.is_gt, ALU.mult))
            link(nc.vector.tensor_tensor(tab[:, 6, :], tab[:, 6, :], tab[:, 7, :], ALU.add))
            mark["tab"] = prep.used
            v.wait_ge(s_pe0, 6)
            full = HC - 1
            rest = HI - full * P
            for w in range(2):
                nc.vector.tensor_copy(tab_out[:, 0:full, :, w], bank[4 + w][:, 0:full * P].rearrange("p (c l) -> p c l", c=full))
                ins = nc.vector.tensor_copy(tab_out[0:rest, full, :, w], bank[4 + w][0:rest, full * P:HC * P])
            link(ins)
            mark["tabout"] = prep.used

            v.wait_ge(s_load, 16 * 15)
            link(nc.vector.tensor_copy(bias_part[:, :, :], bias_in[:, :, :]))
            nc.vector.tensor_scalar(bias3[:, :, :], bias_part[:, :, :], third_m[:, 0:1], None, ALU.mult)
            link(nc.vector.tensor_tensor(bias_rest[:, :, :], bias_in[:, :, :], bias_part[:, :, :], ALU.subtract))
            for n in (1, 2):
                link(nc.vector.tensor_copy(bias_part[:, :, :], bias_rest[:, :, :]))
                for w in range(4):
                    nc.vector.scalar_tensor_tensor(bias3[:, w, :], bias_part[:, w, :], third_m[:, n:n + 1], bias3[:, w, :], ALU.mult, ALU.add)
                link(nc.vector.tensor_tensor(bias_rest[:, :, :], bias_rest[:, :, :], bias_part[:, :, :], ALU.subtract))
            v.wait_ge(s_wt, 1)
            link(nc.vector.tensor_copy(WT[:, :], bank[6][:, 0:P]))
            mark["weights"] = prep.used
            v.wait_ge(s_act0, 1)

            def statistics(chain, nm, z, q, s_z=None):
                for t in range(nm.n):
                    ins = nc.vector.bn_stats(nm.st[:, q, t, :], z[:, t, :])
                chain.link(ins)
                tmp, st = nm.tmp[:, q, :, :], nm.st[:, q, :, :]
                nc.vector.tensor_tensor(tmp[:, 0, :], st[:, :, 1], st[:, :, 4], ALU.add)
                nc.vector.tensor_tensor(tmp[:, 1, :], st[:, :, 1], st[:, :, 4], ALU.subtract)
                chain.link(nc.vector.tensor_tensor(tmp[:, 2, :], st[:, :, 2], st[:, :, 5], ALU.add))
                nc.vector.tensor_scalar(nm.mean[:, q, :], tmp[:, 0, :], 0.5, None, ALU.mult)
                chain.link(nc.vector.scalar_tensor_tensor(tmp[:, 3, :], tmp[:, 1, :], D / 4.0, tmp[:, 1, :], ALU.mult, ALU.mult))
                chain.link(nc.vector.tensor_tensor(tmp[:, 3, :], tmp[:, 3, :], tmp[:, 2, :], ALU.add))
                nc.vector.tensor_scalar(nm.var[:, q, :], tmp[:, 3, :], 1.0 / D, EPS, ALU.mult, ALU.add).then_inc(nm.s_var, 1)

            def normalize(nm, dest, z, q):
                for t in range(nm.n):
                    ins = nc.vector.tensor_scalar(dest[:, t, :], z[:, t, :], nm.mean[:, q, t:t + 1], nm.rstd[:, q, t:t + 1],
                                                  ALU.subtract, ALU.mult)
                return ins

            chain = Chain(v, sem("s_chain_a"), share=22)

            def step_a(s):
                chain.begin(s)
                last = isinstance(s, int) and s == STEPS - 1
                for q in range(2):
                    k, g = s * 2 + q, s * 2 + q
                    here, there = not (last and q == 1), not (first(s) and q == 0)
                    o = 1 - q
                    if here:
                        v.wait_ge(sA_nx[q], 32 * (s + 1))
                        chain.link(nc.vector.tensor_tensor(nz[:, q, :, :], nx[:, q, :, :],
                                                           plain_h[:, :].unsqueeze(1).to_broadcast([P, 2 * GT, D]), ALU.add))
                        v.sem_inc(sA["z1"], 1)
                        statistics(chain, norm1, nz[:, q, :, :], q)
                    if there:
                        v.wait_ge(sA["h"], 2 * k)
                        chain.link(nc.vector.tensor_tensor(nz2[:, o, :, :], nx1[:, o, :, :], nh[:, o, :, :], ALU.add))
                        v.sem_inc(sA["z2"], 1)
                        statistics(chain, norm2, nz2[:, o, :, :], o)
                    v.wait_ge(sA_tab[q], 64 * (s + 1))
                    if not first(s):
                        v.wait_ge(sA["part"], g - 1)
                    nc.vector.tensor_copy(idx_x1[:, bass.ds(g * GT, GT)], tabs[:, q, :, 1])
                    chain.link(nc.vector.tensor_tensor(weight0[0:K, bass.ds(g * GT, GT)], tabs[0:K, q, :, 0],
                                                       rdst[0:K, bass.ds(g * GT, GT)], ALU.mult))
                    nc.vector.tensor_tensor(flw[:, q, :, :], firstlast[:, bass.ds(g * GT, GT), :],
                                            weight0[:, bass.ds(g * GT, GT)].unsqueeze(2).to_broadcast([P, GT, 2]),
                                            ALU.mult).then_inc(sA["flw"], 1)
                    if here:
                        v.wait_ge(norm1.s_rstd, k + 1)
                        if not first(s):
                            v.wait_ge(sA_x1st[q], 32 * s)
                        normalize(norm1, nx1[:, q, :, :], nz[:, q, :, :], q).then_inc(sA["x1"], 1)
                    if there:
                        v.wait_ge(norm2.s_rstd, k)
                        if not (first(s) or (isinstance(s, int) and s == 1 and q == 0)):
                            n = s if q == 1 else s - 1
                            v.wait_ge(sA_outst[o], 32 * n)
                        normalize(norm2, nout[:, o, :, :], nz2[:, o, :, :], o).then_inc(sA["out"], 1)
                chain.end()

            step_a(0)
            step_a(1)
            with v.Fori(2, STEPS - 1) as s:
                step_a(s)
            step_a(STEPS - 1)

            def carries(s_partev, s_cpe, s_carry):
                v.wait_ge(s_partev, G)
                lk, wh = linked[:, 1:T], whole
                nc.vector.tensor_tensor(chain_a[:, 0, 1:T], lk, wh[:, 0:T - 1], ALU.mult)
                nc.vector.tensor_tensor(chain_b[:, 0, 1:T], lk, part[:, 1, 0:T - 1], ALU.mult)
                nc.vector.tensor_tensor(chain_a[:, 1, 0:T - 1], lk, wh[:, 1:T], ALU.mult)
                link(nc.vector.tensor_tensor(chain_b[:, 1, 0:T - 1], lk, part[:, 0, 1:T], ALU.mult))
                nc.vector.tensor_tensor_scan(carry[:, 0, 1:T], chain_a[:, 0, 1:T], chain_b[:, 0, 1:T], 0.0, ALU.mult, ALU.add)
                link(nc.vector.tensor_tensor_scan(carry[:, 1, 0:T - 1][:, ::-1], chain_a[:, 1, 0:T - 1][:, ::-1],
                                                  chain_b[:, 1, 0:T - 1][:, ::-1], 0.0, ALU.mult, ALU.add))
                v.sem_inc(s_cpe, 1)
                v.wait_ge(s_cpe, 2)
                nc.vector.tensor_copy(carry_rows[:, :, :, :].rearrange("p a c d -> p (a c d)"), bank[6][:, :]).then_inc(s_carry, 1)

            prep.base, prep.used = mark["weights"], 0
            carries(sA["partev"], s_cpe0, s_carry0)

            chain = Chain(v, sem("s_chain_b"), share=10)

            def select(S, keys, weights, s, u, s_key, s_used, s_out):
                g = s * 2 + u
                v.wait_ge(s_key[u], 16 * (s + 1))
                if not first(s):
                    v.wait_ge(s_used, g - 1)
                for t in range(GT):
                    at = g * GT + t
                    ins = nc.vector.tensor_scalar(S[:, u, t, :], keys[:, u, t * P:(t + 1) * P], cols[:, QK, bass.ds(at, 1)],
                                                  weights[:, bass.ds(at, 1)], ALU.is_equal, ALU.mult)
                ins.then_inc(s_out, 1)

            def sum_b(g, u, waits=()):
                v.wait_ge(sB_xd[u], 64 * waits)
                v.wait_ge(sB["h"], g + 1)
                chain.link(nc.vector.tensor_tensor(bz[:, u, :, :], bxd[:, u, :, :], bh[:, u, :, :], ALU.add))
                v.sem_inc(sB["z"], 1)
                statistics(chain, normb, bz[:, u, :, :], u)

            def norm_b(g, u, stored):
                v.wait_ge(normb.s_rstd, g + 1)
                if stored is not None:
                    v.wait_ge(sB_st[u], 16 * stored)
                normalize(normb, bx1[:, u, :, :], bz[:, u, :, :], u).then_inc(sB["x1"], 1)

            def step_b(s):
                chain.begin(s)
                for u in range(2):
                    g = s * 2 + u
                    select(bS, bkey, weight0, s, u, sB_key, sB["A"], sB["S"])
                    if not (first(s) and u == 0):
                        sum_b(g - 1, 1 - u, s if u == 0 else s + 1)
                    if not first(s):
                        norm_b(g - 2, u, None if isinstance(s, int) and s == 1 else s - 1)
                chain.end()

            step_b(0)
            step_b(1)
            with v.Fori(2, STEPS) as s:
                step_b(s)
            chain.begin(STEPS)
            v.wait_ge(sB["x1"], G - 2)
            sum_b(G - 1, 1, STEPS)
            for u in range(2):
                norm_b(G - 2 + u, u, STEPS - 1)

            def product_c(g, u, n):
                v.wait_ge(sC["M"], g + 1)
                v.wait_ge(sC["g"], g + 1)
                if n is not None:
                    v.wait_ge(sC_st[u], 16 * n)
                nc.vector.scalar_tensor_tensor(cm[:, u, :, :].rearrange("p t d -> p (t d)"), cg[:, u, :, :].rearrange("p t d -> p (t d)"),
                                               1.0, bank[5][:, :], ALU.add, ALU.mult).then_inc(sC["m"], 1)

            def step_c(s):
                for u in range(2):
                    g = s * 2 + u
                    if not first(s):
                        v.wait_ge(sC["part"], g - 1)
                    nc.vector.tensor_tensor(cfl[:, u, :, :], firstlast[:, bass.ds(g * GT, GT), :],
                                            weight1[:, bass.ds(g * GT, GT)].unsqueeze(2).to_broadcast([P, GT, 2]),
                                            ALU.mult).then_inc(sC["cfl"], 1)
                    v.wait_ge(sC["T"], g + 1)
                    if not first(s):
                        v.wait_ge(sC["G"], g - 1)
                    nc.vector.tensor_copy(cdT[:, u, :], bank[1][:, :]).then_inc(sC["dT"], 1)
                    if not (first(s) and u == 0):
                        n = s if u == 1 else s - 1
                        early = first(s) or (isinstance(s, int) and s == 1 and u == 0)
                        product_c(g - 1, 1 - u, None if early else n)

            step_c(0)
            step_c(1)
            with v.Fori(2, STEPS) as s:
                step_c(s)
            product_c(G - 1, 1, STEPS - 1)
            carries(sC["partev"], s_cpe1, s_carry1)

            chain = Chain(v, sem("s_chain_d"), share=10)

            def sum_d(g, u, n):
                v.wait_ge(sD_xd[u], 16 * n)
                v.wait_ge(sD["h"], g + 1)
                chain.link(nc.vector.tensor_tensor(dz[:, u, :, :], dxd[:, u, :, :], dh[:, u, :, :], ALU.add))
                v.sem_inc(sD["z"], 1)
                statistics(chain, normd, dz[:, u, :, :], u)

            def norm_d(g, u, stored):
                v.wait_ge(normd.s_rstd, g + 1)
                if stored is not None:
                    v.wait_ge(sD_st[u], 64 * stored)
                normalize(normd, dout[:, u, :, :], dz[:, u, :, :], u).then_inc(sD["out"], 1)

            def step_d(s):
                chain.begin(s)
                for u in range(2):
                    g = s * 2 + u
                    select(dS, dkey, weight1, s, u, sD_key, sD["A"], sD["S"])
                    if not (first(s) and u == 0):
                        sum_d(g - 1, 1 - u, s if u == 0 else s + 1)
                    if not first(s):
                        norm_d(g - 2, u, None if isinstance(s, int) and s == 1 else s - 1)
                chain.end()

            step_d(0)
            step_d(1)
            with v.Fori(2, STEPS) as s:
                step_d(s)
            chain.begin(STEPS)
            v.wait_ge(sD["out"], G - 2)
            sum_d(G - 1, 1, STEPS)
            for u in range(2):
                norm_d(G - 2 + u, u, STEPS - 1)

        @block.scalar
        def _(act):
            def turn():
                act.sem_inc(s_act_turn, 1)

            act.wait_ge(s_load, 16 * 15)
            nc.scalar.activation(plain_h[:, :], bias_in[:, B_B, :], ACT.Tanh).then_inc(s_act0, 1)

            def keep_part(g, u, s_part, s_partev, b0):
                act.wait_ge(s_part, g + 1)
                turn()
                nc.scalar.activation(part[:, :, bass.ds(g * GT, GT)].rearrange("p a t -> p t a"),
                                     bank[b0 + u][:, 0:2 * GT].rearrange("p (t a) -> p t a", a=2), ACT.Copy).then_inc(s_partev, 1)

            def step_a(s):
                last = isinstance(s, int) and s == STEPS - 1
                for q in range(2):
                    k = s * 2 + q
                    if not (last and q == 1):
                        for w in range(2):
                            n = 2 * k + w
                            act.wait_ge(sA["T"], n + 1)
                            if not (first(s) and q == 0):
                                act.wait_ge(sA["O"], n - 1)
                            nc.scalar.activation(nx1T[:, w, :], bank[w][:, :], ACT.Copy).then_inc(sA["Tev"], 1)
                        for w in range(2):
                            n = 2 * k + w
                            act.wait_ge(sA["O"], n + 1)
                            if not first(s) and w == 0:
                                act.wait_ge(sA["z2"], k - 1)
                            nc.scalar.activation(nh[:, q, w * GT:(w + 1) * GT, :].rearrange("p t d -> p (t d)"), bank[2 + w][:, :],
                                                 ACT.Silu).then_inc(sA["h"], 1)
                    keep_part(s * 2 + q, q, sA["part"], sA["partev"], 4)

            steps(act, step_a)

            def tanh_b(g, u):
                act.wait_ge(sB["O"], g + 1)
                if not (isinstance(g, int) and g < 2):
                    act.wait_ge(sB["z"], g - 1)
                nc.scalar.activation(bh[:, u, :, :].rearrange("p t d -> p (t d)"), bank[2 + u][:, :], ACT.Tanh).then_inc(sB["h"], 1)

            def step_b(s):
                for u in range(2):
                    g = s * 2 + u
                    act.wait_ge(sB["A"], g + 1)
                    if not first(s):
                        act.wait_ge(sB["O"], g - 1)
                    nc.scalar.activation(baT[:, u, :], bank[u][:, :], ACT.Copy).then_inc(sB["Aev"], 1)
                    if not (first(s) and u == 0):
                        tanh_b(g - 1, 1 - u)

            step_b(0)
            step_b(1)
            with act.Fori(2, STEPS) as s:
                step_b(s)
            tanh_b(G - 1, 1)

            def gates_c(g, u):
                early = isinstance(g, int) and g < 2
                act.wait_ge(sC["H"], g + 1)
                if not early:
                    act.wait_ge(sC["M"], g - 1)
                nc.scalar.activation(chT[:, u, :], bank[3][:, :], ACT.Silu, bias=b1c[:, 0:1]).then_inc(sC["h"], 1)
                act.wait_ge(sC["G"], g + 1)
                if not early:
                    act.wait_ge(sC["m"], g - 1)
                nc.scalar.activation(cg[:, u, :, :].rearrange("p t d -> p (t d)"), bank[4][:, :], ACT.Tanh, scale=0.5).then_inc(sC["g"], 1)

            def step_c(s):
                for u in range(2):
                    g = s * 2 + u
                    act.wait_ge(sC["T"], g + 1)
                    if not first(s):
                        act.wait_ge(sC["G"], g - 1)
                    nc.scalar.activation(csT[:, u, :], bank[0][:, :], ACT.Copy).then_inc(sC["sT"], 1)
                    nc.scalar.activation(ceT[:, u, :], bank[2][0:DE, :], ACT.Copy).then_inc(sC["eT"], 1)
                    if not (first(s) and u == 0):
                        gates_c(g - 1, 1 - u)
                    if not first(s):
                        keep_part(g - 2, u, sC["part"], sC["partev"], 6)

            step_c(0)
            step_c(1)
            with act.Fori(2, STEPS) as s:
                step_c(s)
            gates_c(G - 1, 1)
            for u in range(2):
                keep_part(G - 2 + u, u, sC["part"], sC["partev"], 6)

            def silu_d(g, u):
                act.wait_ge(sD["O"], g + 1)
                if not (isinstance(g, int) and g < 2):
                    act.wait_ge(sD["z"], g - 1)
                nc.scalar.activation(dh[:, u, :, :].rearrange("p t d -> p (t d)"), bank[4 + u][:, :], ACT.Silu).then_inc(sD["h"], 1)

            def step_d(s):
                for u in range(2):
                    g = s * 2 + u
                    if not first(s):
                        act.wait_ge(sD["O"], g - 1)
                    act.wait_ge(sD["T"], g + 1)
                    nc.scalar.activation(dxT[:, u, :], bank[2 + u][:, :], ACT.Copy).then_inc(sD["Tev"], 1)
                    act.wait_ge(sD["A"], g + 1)
                    nc.scalar.activation(daT[:, u, :], bank[u][:, :], ACT.Copy).then_inc(sD["Aev"], 1)
                    if not (first(s) and u == 0):
                        silu_d(g - 1, 1 - u)

            step_d(0)
            step_d(1)
            with act.Fori(2, STEPS) as s:
                step_d(s)
            silu_d(G - 1, 1)

        @block.tensor
        def _(pe):
            mm = nc.tensor.matmul

            def transpose(dest, src_, parts=P):
                return nc.tensor.transpose(dest, src_, ident[0:parts, 0:parts])

            pe.wait_ge(s_consts, 1)
            pe.wait_ge(s_load, 16 * 15)
            transpose(bank[6][:, 0:P], Wsb[:, :]).then_inc(s_wt, 1)
            pe.wait_ge(s_chain, mark["scans"])
            for c in range(2):
                for n, col in enumerate((scan_lo[:, c, K - 1:K], scan_hi[:, c, 0:1], tile_flags[:, c, 0:1], tile_flags[:, c, 1:2])):
                    at = (n % 2) * 2 * P + c * P
                    ins = transpose(bank[n // 2][0:1, at:at + P], col)
            ins.then_inc(s_pe0, 1)
            pe.wait_ge(s_chain, mark["lines"])
            for a in range(2):
                for c in range(2):
                    transpose(bank[2][:, 2 * a + c:2 * a + c + 1], line_ex[0:1, a, c * P:(c + 1) * P], 1)
            mm(bank[3][:, :], ones[0:1, 0:P], line[0:1, 2:4, :].rearrange("o a b -> o (a b)"), start=True, stop=True).then_inc(s_pe0, 1)
            pe.wait_ge(s_chain, mark["rows"])
            for n in range(6):
                transpose(bank[n][:, 0:P], rows[:, n, 0, :])
                ins = transpose(bank[n][:, P:T], rows[0:T - P, n, 1, :], T - P)
            ins.then_inc(s_pe0, 1)

            mm(bank[7][:, 0:HI], zerosb[:, 0:P], zerosb[:, 0:HI], start=True, stop=False)

            def step_hot(s):
                for u in range(2):
                    pe.wait_ge(s_hot, s * 2 + u + 1)
                    for t in range(GT):
                        ins = mm(bank[7][:, 0:HI], hot_lo[0:K, u, t, :], hot_hi[0:K, u, t, :], start=False, stop=False)
                    ins.then_inc(s_hot_used, 1)

            steps(pe, step_hot)
            mm(bank[7][:, 0:HI], zerosb[:, 0:P], zerosb[:, 0:HI], start=False, stop=True).then_inc(s_pe0, 1)
            pe.wait_ge(s_chain, mark["counts"])
            mm(bank[0][:, 0:HI], before[:, :], tab[:, 0, :], start=True, stop=True)
            mm(bank[1][:, 0:HI], ones[:, 0:P], tab[:, 0, :], start=True, stop=True).then_inc(s_pe0, 1)
            pe.wait_ge(s_pow0, 2)
            pe.wait_ge(s_chain, mark["tab"])
            for c in range(HC):
                n = min(P, HI - c * P)
                for w, q in enumerate((5, 6)):
                    ins = transpose(bank[4 + w][0:n, c * P:(c + 1) * P], tab[:, q, c * P:c * P + n])
            ins.then_inc(s_pe0, 1)
            pe.wait_ge(s_chain, mark["weights"])

            def bias_mm(dest, n):
                return mm(dest, onesb[:, :], bias3[:, n, :].unsqueeze(1).to_broadcast([P, GT, D]), start=True, stop=False)

            def tile_at(t):
                return slice(t * P, (t + 1) * P)

            def step_a(s):
                last = isinstance(s, int) and s == STEPS - 1
                for q in range(2):
                    k = s * 2 + q
                    early = first(s) and q == 0
                    if not (last and q == 1):
                        pe.wait_ge(sA["x1"], k + 1)
                        for w in range(2):
                            n = 2 * k + w
                            if not early:
                                pe.wait_ge(sA["Tev"], n - 1)
                            for t in range(GT):
                                ins = transpose(bank[w][:, tile_at(t)], nx1[:, q, w * GT + t, :])
                            ins.then_inc(sA["T"], 1)
                        for w in range(2):
                            n = 2 * k + w
                            pe.wait_ge(sA["Tev"], n + 1)
                            if not early:
                                pe.wait_ge(sA["h"], n - 1)
                            bias_mm(bank[2 + w][:, :], B_BU)
                            for t in range(GT):
                                ins = mm(bank[2 + w][:, tile_at(t)], nx1T[:, w, tile_at(t)], wux[:, :], start=False, stop=t == GT - 1)
                            ins.then_inc(sA["O"], 1)
                    g = s * 2 + q
                    pe.wait_ge(sA_xs[q], 64 * (s + 1))
                    pe.wait_ge(sA["flw"], g + 1)
                    if not first(s):
                        pe.wait_ge(sA["partev"], g - 1)
                    for t in range(GT):
                        ins = mm(bank[4 + q][:, 2 * t:2 * t + 2], xs[:, q, t, :], flw[:, q, t, :], start=t == 0, stop=t == GT - 1)
                    ins.then_inc(sA["part"], 1)

            steps(pe, step_a)

            def carry_mm(s_cpe):
                pe.wait_ge(s_cpe, 1)
                for a in range(2):
                    for c in range(2):
                        ins = transpose(bank[6][:, (2 * a + c) * P:(2 * a + c + 1) * P], carry[:, a, c * P:(c + 1) * P])
                ins.then_inc(s_cpe, 1)

            carry_mm(s_cpe0)

            def out_b(g, u):
                pe.wait_ge(sB["Aev"], g + 1)
                if not (isinstance(g, int) and g < 2):
                    pe.wait_ge(sB["h"], g - 1)
                bias_mm(bank[2 + u][:, :], B_B)
                for t in range(GT):
                    ins = mm(bank[2 + u][:, tile_at(t)], baT[:, u, tile_at(t)], WT[:, :], start=False, stop=t == GT - 1)
                ins.then_inc(sB["O"], 1)

            def step_b(s):
                for u in range(2):
                    g = s * 2 + u
                    pe.wait_ge(sB_xs[u], 16 * (s + 1))
                    pe.wait_ge(sB["S"], g + 1)
                    if not first(s):
                        pe.wait_ge(sB["Aev"], g - 1)
                    for t in range(GT):
                        ins = mm(bank[u][:, tile_at(t)], bxs[:, u, t, :], bS[:, u, t, :], start=t == 0, stop=t == GT - 1)
                    ins.then_inc(sB["A"], 1)
                    if not (first(s) and u == 0):
                        out_b(g - 1, 1 - u)

            step_b(0)
            step_b(1)
            with pe.Fori(2, STEPS) as s:
                step_b(s)
            out_b(G - 1, 1)
            pe.wait_ge(sB["h"], G)
            pe.wait_ge(s_carry0, 1)

            def transposes_c(s, u):
                g = s * 2 + u
                pe.wait_ge(sC_xd[u], 16 * (s + 1))
                short = isinstance(g, int) and g == G - 1
                pe.wait_ge(sC_ea[u], 16 * (s + 1) + (16 if short else 0))
                pe.wait_ge(sC_xs[u], 64 * (s + 1))
                if not (first(s) and u == 0):
                    for n in ("sT", "dT", "eT"):
                        pe.wait_ge(sC[n], g)
                for t in range(GT):
                    transpose(bank[0][:, tile_at(t)], cxs[:, u, t, :])
                for t in range(GT):
                    transpose(bank[1][:, tile_at(t)], cxd[:, u, t, :])
                for t in range(GT):
                    ins = transpose(bank[2][0:DE, tile_at(t)], cea[:, u, t, :])
                ins.then_inc(sC["T"], 1)

            def messages_c(g, u):
                for n in ("sT", "dT", "eT"):
                    pe.wait_ge(sC[n], g + 1)
                later = not (isinstance(g, int) and g == 0)
                if later:
                    pe.wait_ge(sC["h"], g)
                mm(bank[3][:, :], w1s[:, :], csT[:, u, :], start=True, stop=False)
                mm(bank[3][:, :], w1d[:, :], cdT[:, u, :], start=False, stop=False)
                mm(bank[3][:, :], w1e[:, :], ceT[:, u, :], start=False, stop=True).then_inc(sC["H"], 1)
                if later:
                    pe.wait_ge(sC["g"], g)
                bias_mm(bank[4][:, :], B_BG)
                for t in range(GT):
                    mm(bank[4][:, tile_at(t)], csT[:, u, tile_at(t)], wgs[:, :], start=False, stop=False)
                    mm(bank[4][:, tile_at(t)], cdT[:, u, tile_at(t)], wgd[:, :], start=False, stop=False)
                    ins = mm(bank[4][:, tile_at(t)], ceT[:, u, tile_at(t)], wge[:, :], start=False, stop=t == GT - 1)
                ins.then_inc(sC["G"], 1)
                if later:
                    pe.wait_ge(sC["m"], g)
                pe.wait_ge(sC["h"], g + 1)
                bias_mm(bank[5][:, :], B_B2)
                for t in range(GT):
                    ins = mm(bank[5][:, tile_at(t)], chT[:, u, tile_at(t)], w2sb[:, :], start=False, stop=t == GT - 1)
                ins.then_inc(sC["M"], 1)

            def part_c(g, u):
                pe.wait_ge(sC["m"], g + 1)
                pe.wait_ge(sC["cfl"], g + 1)
                if not (isinstance(g, int) and g < 2):
                    pe.wait_ge(sC["partev"], g - 1)
                for t in range(GT):
                    ins = mm(bank[6 + u][:, 2 * t:2 * t + 2], cm[:, u, t, :], cfl[:, u, t, :], start=t == 0, stop=t == GT - 1)
                ins.then_inc(sC["part"], 1)

            def step_c(s):
                for u in range(2):
                    g = s * 2 + u
                    transposes_c(s, u)
                    if not first(s):
                        part_c(g - 2, u)
                    if not (first(s) and u == 0):
                        messages_c(g - 1, 1 - u)

            step_c(0)
            step_c(1)
            with pe.Fori(2, STEPS - 1) as s:
                step_c(s)
            step_c(STEPS - 1)
            part_c(G - 2, 0)
            messages_c(G - 1, 1)
            part_c(G - 1, 1)
            pe.wait_ge(sC["partev"], G)
            carry_mm(s_cpe1)

            def out_d(g, u):
                pe.wait_ge(sD["Tev"], g + 1)
                pe.wait_ge(sD["Aev"], g + 1)
                if not (isinstance(g, int) and g < 2):
                    pe.wait_ge(sD["h"], g - 1)
                bias_mm(bank[4 + u][:, :], B_BU)
                for t in range(GT):
                    mm(bank[4 + u][:, tile_at(t)], dxT[:, u, tile_at(t)], wux[:, :], start=False, stop=False)
                    ins = mm(bank[4 + u][:, tile_at(t)], daT[:, u, tile_at(t)], wua[:, :], start=False, stop=t == GT - 1)
                ins.then_inc(sD["O"], 1)

            def step_d(s):
                for u in range(2):
                    g = s * 2 + u
                    pe.wait_ge(sD_xd[u], 16 * (s + 1))
                    if not first(s):
                        pe.wait_ge(sD["Tev"], g - 1)
                    for t in range(GT):
                        ins = transpose(bank[2 + u][:, tile_at(t)], dxd[:, u, t, :])
                    ins.then_inc(sD["T"], 1)
                    pe.wait_ge(sD_ms[u], 16 * (s + 1))
                    pe.wait_ge(sD["S"], g + 1)
                    if not first(s):
                        pe.wait_ge(sD["Aev"], g - 1)
                    for t in range(GT):
                        ins = mm(bank[u][:, tile_at(t)], dms[:, u, t, :], dS[:, u, t, :], start=t == 0, stop=t == GT - 1)
                    ins.then_inc(sD["A"], 1)
                    if not (first(s) and u == 0):
                        out_d(g - 1, 1 - u)

            step_d(0)
            step_d(1)
            with pe.Fori(2, STEPS) as s:
                step_d(s)
            out_d(G - 1, 1)

        @block.sync
        def _(sp):
            sp.wait_ge(s_prefill, 1)
            for lst, tile in ((dst, dst_i), (src, src_i)):
                sp.dma_start(tile[:, 0, :], lst[0:P * K].rearrange("(t i) -> t i", i=K)).then_inc(s_idx_ld, 16)
                sp.dma_start(tile[0:C1_TILES - 1, 1, :],
                             lst[P * K:(T_REAL - 1) * K].rearrange("(t i) -> t i", i=K)).then_inc(s_idx_ld, 16)
                sp.dma_start(tile[C1_TILES - 1:C1_TILES, 1, 0:LAST_ROWS],
                             lst[(T_REAL - 1) * K:E].rearrange("(t i) -> t i", t=1)).then_inc(s_idx_ld, 16)
            with nc.allow_non_contiguous_dma(reason="one key per tile"):
                pairs = ((prev_i[1:P, 0:1], K - 1, P - 1), (prev_i[0:C1_TILES, 1:2], P * K - 1, C1_TILES),
                         (next_i[:, 0:1], K, P), (next_i[0:C1_TILES - 1, 1:2], (P + 1) * K, C1_TILES - 1))
                for tile, at, n in pairs:
                    sp.dma_start(tile, dst[at:at + (n - 1) * K + 1].unsqueeze(1)[::K, :]).then_inc(s_idx_ld, 16)
            for tile, ap in ((Wsb[:, :], W), (w1s[:, :], w1[0:D, :]), (w1d[:, :], w1[D:2 * D, :]), (w1e[:, :], w1[2 * D:, :]),
                             (wgs[:, :], wg[0:D, :]), (wgd[:, :], wg[D:2 * D, :]), (wge[:, :], wg[2 * D:, :]),
                             (w2sb[:, :], w2), (wux[:, :], wu[0:D, :]), (wua[:, :], wu[D:, :]),
                             (b1c[:, :], b1.unsqueeze(1))):
                sp.dma_start(tile, ap).then_inc(s_load, 16)
            for n, ap in ((B_B, b), (B_B2, b2), (B_BG, bg), (B_BU, bu)):
                sp.dma_start(bias_in[:, n, :], ap.unsqueeze(0).to_broadcast([P, D])).then_inc(s_load, 16)
            sp.wait_ge(s_chain, mark["keys"])
            sp.dma_start(key_rows[0:P, :], rows[:, QK, 0, :]).then_inc(s_keys, 16)
            sp.dma_start(key_rows[P:T, :], rows[0:T - P, QK, 1, :]).then_inc(s_keys, 16)

            def load_nodes(k, q):
                for v in range(2):
                    g = k * 2 + v
                    parts = NG_LAST_P if isinstance(g, int) and g == NG - 1 else P
                    sp.dma_start(nx[0:parts, q, v * GT:(v + 1) * GT, :].rearrange("p j d -> p (j d)"),
                                 nodes_of(x, g, 0, parts)).then_inc(sA_nx[q], 16)

            def store_nodes(k, q, tile, tab_, base, sems):
                for v in range(2):
                    g = k * 2 + v
                    parts = NG_LAST_P if isinstance(g, int) and g == NG - 1 else P
                    sp.dma_start(nodes_of(tab_, g, base, parts),
                                 tile[0:parts, q, v * GT:(v + 1) * GT, :].rearrange("p j d -> p (j d)")).then_inc(sems[q], 16)

            load_nodes(0, 0)
            load_nodes(1, 1)
            sp.wait_ge(s_chain, mark["tabout"])
            full = HC - 1
            sp.dma_start(node_tab[0:full * P * P, :].rearrange("(c p l) w -> p c (l w)", p=P, l=P),
                         tab_out[:, 0:full, :, :].rearrange("p c l w -> p c (l w)")).then_inc(s_tab, 16)
            sp.dma_start(node_tab[full * P * P:HI * P, :].rearrange("(p l) w -> p (l w)", l=P),
                         tab_out[0:HI - full * P, full, :, :].rearrange("p l w -> p (l w)")).then_inc(s_tab, 16)

            def step_a(s):
                last = isinstance(s, int) and s == STEPS - 1
                for u in range(2):
                    k = s * 2 + u
                    if not last:
                        sp.wait_ge(sA["z1"], k + 1)
                        if not (isinstance(s, int) and s == STEPS - 2 and u == 1):
                            load_nodes(k + 2, u)
                    if not (last and u == 1):
                        sp.wait_ge(sA["x1"], k + 1)
                        store_nodes(k, u, nx1, x1_tab, SLOTS, sA_x1st)
                    if not (first(s) and u == 0):
                        sp.wait_ge(sA["out"], k)
                        store_nodes(k - 1, 1 - u, nout, out, 0, sA_outst)
                    g = s * 2 + u
                    sp.wait_ge(sA_xs[u], 64 * (s + 1))
                    sp.dma_start(slots_of(src_feat, g), xs[:, u, :, :]).then_inc(sA_st[u], 16)

            step_a(0)
            with sp.Fori(1, STEPS - 2) as s:
                step_a(s)
            step_a(STEPS - 2)
            step_a(STEPS - 1)

            for u in range(2):
                sp.wait_ge(sA_st[u], 16 * STEPS)
            sp.wait_ge(s_carry0, 1)
            for side in range(2):
                for c, n in ((0, P), (1, T - P)):
                    sp.dma_start(src_feat.rearrange("(t s) d -> t s d", s=P)[c * P:c * P + n, K + side, :],
                                 carry_rows[0:n, side, c, :]).then_inc(s_cst0, 16)
            sp.wait_ge(s_cst0, 64)
            sp.wait_ge(s_keys, 32)

            def load_b(s, u):
                g = s * 2 + u
                if not first(s):
                    sp.wait_ge(sB["S"], g - 1)
                sp.dma_start(bkey[:, u, :], key_rows[bass.ds(g * GT, GT), :].rearrange("t s -> (t s)").unsqueeze(0)
                             .to_broadcast([P, GT * P])).then_inc(sB_key[u], 16)
                if not first(s):
                    sp.wait_ge(sB["A"], g - 1)
                sp.dma_start(bxs[:, u, :, :], slots_of(src_feat, g)).then_inc(sB_xs[u], 16)

            def step_b(s):
                for u in range(2):
                    if not (isinstance(s, int) and s == STEPS - 1):
                        load_b(s + 1, u)
                    g = s * 2 + u
                    sp.wait_ge(sB["x1"], g + 1)
                    sp.dma_start(slots_of(x1_tab, g), bx1[:, u, :, :]).then_inc(sB_st[u], 16)

            for u in range(2):
                load_b(0, u)
            steps(sp, step_b)

            for u in range(2):
                sp.wait_ge(sB_st[u], 16 * STEPS)

            def load_c(s, u):
                g = s * 2 + u
                if not first(s):
                    sp.wait_ge(sC["T"], g - 1)
                sp.dma_start(cxd[:, u, :, :], slots_of(x1_tab, g)).then_inc(sC_xd[u], 16)
                at = g * (GT * K)
                if isinstance(g, int) and g == G - 1:
                    full = T_REAL - 1 - g * GT
                    sp.dma_start(cea[0:K, u, 0:full, :],
                                 edge_attr[at:at + full * K, :].rearrange("(t i) d -> i t d", i=K)).then_inc(sC_ea[u], 16)
                    sp.dma_start(cea[0:LAST_ROWS, u, full, :], edge_attr[at + full * K:E, :]).then_inc(sC_ea[u], 16)
                else:
                    sp.dma_start(cea[0:K, u, :, :],
                                 edge_attr[bass.ds(at, GT * K), :].rearrange("(t i) d -> i t d", i=K)).then_inc(sC_ea[u], 16)

            def step_c(s):
                for u in range(2):
                    if not (isinstance(s, int) and s == STEPS - 1):
                        load_c(s + 1, u)
                    g = s * 2 + u
                    sp.wait_ge(sC["m"], g + 1)
                    sp.dma_start(slots_of(messages, g), cm[:, u, :, :]).then_inc(sC_st[u], 16)

            for u in range(2):
                load_c(0, u)
            step_c(0)
            with sp.Fori(1, STEPS - 2) as s:
                step_c(s)
            step_c(STEPS - 2)
            step_c(STEPS - 1)

            for u in range(2):
                sp.wait_ge(sC_st[u], 16 * STEPS)
            sp.wait_ge(s_carry1, 1)
            for side in range(2):
                for c, n in ((0, P), (1, T - P)):
                    sp.dma_start(messages.rearrange("(t s) d -> t s d", s=P)[c * P:c * P + n, K + side, :],
                                 carry_rows[0:n, side, c, :]).then_inc(s_cst1, 16)
            sp.wait_ge(s_cst1, 64)

            def load_d(s, u):
                g = s * 2 + u
                if not first(s):
                    sp.wait_ge(sD["S"], g - 1)
                sp.dma_start(dkey[:, u, :], key_rows[bass.ds(g * GT, GT), :].rearrange("t s -> (t s)").unsqueeze(0)
                             .to_broadcast([P, GT * P])).then_inc(sD_key[u], 16)
                if not first(s):
                    sp.wait_ge(sD["A"], g - 1)
                sp.dma_start(dms[:, u, :, :], slots_of(messages, g)).then_inc(sD_ms[u], 16)
                if not first(s):
                    sp.wait_ge(sD["z"], g - 1)
                sp.dma_start(dxd[:, u, :, :], slots_of(x1_tab, g)).then_inc(sD_xd[u], 16)

            for u in range(2):
                load_d(0, u)

            def step_d(s):
                for u in range(2):
                    load_d(s + 1, u)

            step_d(0)
            with sp.Fori(1, STEPS - 1) as s:
                step_d(s)
            for u in range(2):
                sp.wait_ge(sD_st[u], 64 * STEPS)

        @block.gpsimd
        def _(pool):
            nc.gpsimd.iota(iota_i[:, :], pattern=[[1, HI]], base=0, channel_multiplier=0)
            nc.gpsimd.iota(node_i[:, :], pattern=[[P, HI]], base=0, channel_multiplier=1)
            nc.gpsimd.iota(edge_i[:, :, :], pattern=[[P * K, 2], [1, K]], base=0, channel_multiplier=K)
            nc.gpsimd.memset(ones[:, :], 1.0)
            nc.gpsimd.memset(neg_half[:, :], -0.5).then_inc(s_mask0, 1)
            pool.wait_ge(s_mask0, 1)
            nc.gpsimd.affine_select(out=ident[:, :], in_=ones[:, 0:P], pattern=[[-1, P]], compare_op=ALU.is_equal,
                                    fill=0.0, base=0, channel_multiplier=1)
            nc.gpsimd.affine_select(out=third_m[:, :], in_=ones[:, 0:3], pattern=[[-1, 3]], compare_op=ALU.is_equal,
                                    fill=0.0, base=0, channel_multiplier=1)
            nc.gpsimd.affine_select(out=before[:, :], in_=ones[:, 0:P], pattern=[[1, P]], compare_op=ALU.is_gt,
                                    fill=0.0, base=0, channel_multiplier=-1).then_inc(s_consts, 1)
            pool.wait_ge(s_chain, mark["deg"])
            nc.gpsimd.tensor_tensor(rdst[:, :], tmp_c[:, :], neg_half[:, 0:T], ALU.pow).then_inc(s_pow0, 1)
            pool.wait_ge(s_chain, mark["tabdeg"])
            nc.gpsimd.tensor_tensor(tab[:, 5, :], tab[:, 4, :], neg_half[:, :], ALU.pow).then_inc(s_pow0, 1)

            def turn():
                pool.sem_inc(s_pool_turn, 1)

            def take_ids(ids, idx, s, u, s_ids):
                g = s * 2 + u
                nc.gpsimd.tensor_copy(ids[:, u, :], idx[:, bass.ds(g * GT, GT)]).then_inc(s_ids, 1)
                pool.wait_ge(s_ids, g + 1)
                turn()

            def gather(dest, table, ids, u, t, s_done):
                nc.gpsimd.indirect_dma_start(dest, None, table, bass.IndirectOffsetOnAxis(ap=ids[:, u, t:t + 1], axis=0)
                                             ).then_inc(s_done, 16)

            def powers(nm, k, q):
                pool.wait_ge(nm.s_var, k + 1)
                nc.gpsimd.tensor_tensor(nm.rstd[:, q, :], nm.var[:, q, :], neg_half[:, 0:nm.n], ALU.pow
                                        ).then_inc(nm.s_rstd, 1)

            pool.wait_ge(s_tab, 32)

            def step_a(s):
                for u in range(2):
                    if not first(s):
                        pool.wait_ge(sA_st[u], 16 * s)
                        pool.wait_ge(sA["part"], s * 2 + u - 1)
                        pool.wait_ge(sA["flw"], s * 2 + u - 1)
                        turn()
                    take_ids(ids_a, idx_src, s, u, sA["ids"])
                    for t in range(GT):
                        gather(xs[:, u, t, :], x[:, :], ids_a, u, t, sA_xs[u])
                    for t in range(GT):
                        gather(tabs[:, u, t, :], node_tab[:, :], ids_a, u, t, sA_tab[u])
                    k = s * 2 + u
                    if not (isinstance(s, int) and s == STEPS - 1 and u == 1):
                        powers(norm1, k, u)
                    if not (first(s) and u == 0):
                        powers(norm2, k - 1, 1 - u)

            steps(pool, step_a)

            def step_b(s):
                for u in range(2):
                    if not first(s):
                        pool.wait_ge(sB["z"], s * 2 + u - 1)
                        turn()
                    take_ids(ids_b, idx_dst, s, u, sB["ids"])
                    for t in range(GT):
                        gather(bxd[:, u, t, :], x[:, :], ids_b, u, t, sB_xd[u])
                    if not (first(s) and u == 0):
                        powers(normb, s * 2 + u - 1, 1 - u)

            steps(pool, step_b)
            powers(normb, G - 1, 1)

            for u in range(2):
                pool.wait_ge(sB_st[u], 16 * STEPS)
            for q, n in ((0, PAIRS // 2 + 1), (1, PAIRS // 2)):
                pool.wait_ge(sA_x1st[q], 32 * n)

            def step_c(s):
                for u in range(2):
                    if not first(s):
                        pool.wait_ge(sC["T"], s * 2 + u - 1)
                        turn()
                    take_ids(ids_c, idx_x1, s, u, sC["ids"])
                    for t in range(GT):
                        gather(cxs[:, u, t, :], x1_tab[:, :], ids_c, u, t, sC_xs[u])

            steps(pool, step_c)

            for q, n in ((0, PAIRS // 2 + 1), (1, PAIRS // 2)):
                pool.wait_ge(sA_outst[q], 32 * n)

            def scatter_d(s, u):
                g = s * 2 + u
                if not first(s):
                    pool.wait_ge(sD_st[u], 64 * s)
                    turn()
                take_ids(ids_d, idx_out, s, u, sD["ids"])
                pool.wait_ge(sD["out"], g + 1)
                turn()
                for t in range(GT):
                    nc.gpsimd.indirect_dma_start(out[:, :], bass.IndirectOffsetOnAxis(ap=ids_d[:, u, t:t + 1], axis=0),
                                                 dout[:, u, t, :], None, bounds_check=N - 1, oob_is_err=False
                                                 ).then_inc(sD_st[u], 16)

            def step_d(s):
                for u in range(2):
                    powers(normd, s * 2 + u, u)
                    if u == 1:
                        scatter_d(s, 0)
                    elif not first(s):
                        scatter_d(s - 1, 1)

            step_d(0)
            step_d(1)
            with pool.Fori(2, STEPS) as s:
                step_d(s)
            scatter_d(STEPS - 1, 1)


_INS = ["x", "src", "dst", "edge_attr_64", "L0_gnn_W", "L0_gnn_b", "L1_gnn_w1", "L1_gnn_b1", "L1_gnn_w2", "L1_gnn_b2",
        "L1_gnn_wg", "L1_gnn_bg", "L1_gnn_wu", "L1_gnn_bu"]


def kernel(**inputs):
    import concourse.bacc as _bacc
    from concourse.bass_utils import run_bass_kernel_spmd as _run

    nc = _bacc.Bacc("TRN2", target_bir_lowering=False, num_devices=1)
    arrays, args = {}, []
    for name in _INS:
        a = np.ascontiguousarray(inputs[name])
        arrays[f"in_{name}_dram"] = a
        args.append(nc.dram_tensor(f"in_{name}_dram", a.shape, mybir.dt.from_np(a.dtype), kind="ExternalInput").ap())
    shape = inputs["x"].shape
    args.append(nc.dram_tensor("out_dram", shape, F32, kind="ExternalOutput").ap())
    gnn_kernel(nc, *args)
    r = _run(nc, [arrays], core_ids=[0])
    return r.results[0]["out_dram"]
```

```python
import numpy as np
import concourse.bass as bass
from concourse import mybir
from contextlib import ExitStack

F32, I32, F16, BF16 = mybir.dt.float32, mybir.dt.int32, mybir.dt.float16, mybir.dt.bfloat16
ALU, ACT = mybir.AluOpType, mybir.ActivationFunctionType


def gnn_kernel(nc, x, src, dst, edge_attr, W, b, w1, b1, w2, b2, wg, bg, wu, bu, out):
    P = 128
    N, D = x.shape
    E = src.shape[0]
    DE = edge_attr.shape[1]
    K = P - 2
    GT = 4
    T_REAL = -(-E // K)
    T = -(-T_REAL // (2 * GT)) * 2 * GT
    G = T // GT
    STEPS = G // 2
    R = 5
    RSTEPS = G // R
    assert RSTEPS * R == G
    SLOTS = T * P
    LAST_ROWS = E - (T_REAL - 1) * K
    NODE_GROUP = GT * P
    NG = -(-N // NODE_GROUP)
    NG_LAST_P = (N - (NG - 1) * NODE_GROUP) // GT
    PAIRS = NG // 2
    assert NG % 2 == 0 and 2 * STEPS == PAIRS + 1 and (N - (NG - 1) * NODE_GROUP) % GT == 0
    HI = -(-N // P)
    HC = -(-HI // P)
    NO_KEY = 65535.0
    SKIP = 70000.0
    FAR = 1.0e6
    EPS = 1e-5
    C1_TILES = T_REAL - P

    def dram(name, shape, dt):
        return nc.dram_tensor(name, shape, dt, kind="Internal").ap()

    key_rows = dram("key_rows", (T, P), F32)
    node_tab = dram("node_tab", (HI * P, 2), F32)
    src_feat = dram("src_feat", (SLOTS, D), F32)
    messages = dram("messages", (SLOTS, D), F32)
    x1_tab = dram("x1_tab", (SLOTS + N, D), F32)

    def slots_of(tab, g):
        return tab[bass.ds(g * (GT * P), GT * P), :].rearrange("(t s) d -> s t d", s=P)

    def nodes_of(tab, g, base=0, parts=P):
        return tab[bass.ds(g * NODE_GROUP + base, parts * GT), :].rearrange("(p j) d -> p (j d)", j=GT)

    ctx = ExitStack()
    with ctx:
        def sb(name, shape, dt=F32):
            return ctx.enter_context(nc.sbuf_tensor(name, shape, dt))

        def sem(name):
            return ctx.enter_context(nc.semaphore(name))

        bank = [ctx.enter_context(nc.psum_tensor(f"bank{i}", [P, 512], F32)) for i in range(8)]

        ident = sb("ident", [P, P])
        before = sb("before", [P, P])
        ones = sb("ones", [P, 512])
        onesb = sb("onesb", [P, P], BF16)
        zerosb = sb("zerosb", [P, 512], BF16)
        iota_i = sb("iota_i", [P, HI], I32)
        iota_h = sb("iota_h", [P, HI], F16)
        node_i = sb("node_i", [P, HI], I32)
        edge_i = sb("edge_i", [P, 2, K], I32)
        third_m = sb("third_m", [P, 3])
        Wsb, WT = sb("Wsb", [P, D]), sb("WT", [P, D])
        w1s, w1d, w1e = sb("w1s", [P, D]), sb("w1d", [P, D]), sb("w1e", [DE, D])
        wgs, wgd, wge = sb("wgs", [P, D]), sb("wgd", [P, D]), sb("wge", [DE, D])
        w2sb, wux, wua = sb("w2sb", [P, D]), sb("wux", [P, D]), sb("wua", [P, D])
        b1c = sb("b1c", [P, 1])
        bias_in = sb("bias_in", [P, 4, D])
        bias_rest = sb("bias_rest", [P, 4, D])
        bias_part = sb("bias_part", [P, 4, D], BF16)
        bias3 = sb("bias3", [P, 4, D], BF16)
        plain_h = sb("plain_h", [P, D])
        B_B, B_B2, B_BG, B_BU = range(4)

        dst_i, src_i = sb("dst_i", [P, 2, K], I32), sb("src_i", [P, 2, K], I32)
        prev_i, next_i = sb("prev_i", [P, 2], I32), sb("next_i", [P, 2], I32)
        prev_f, next_f = sb("prev_f", [P, 2]), sb("next_f", [P, 2])
        QK, QS, QD, QB, QF, QL = range(6)
        rows = sb("rows", [P, 6, 2, P])
        edge_f = sb("edge_f", [P, 2, K])
        run_last = sb("run_last", [P, 2, K])
        scan_in, scan_lo, scan_hi = sb("scan_in", [P, 2, K]), sb("scan_lo", [P, 2, K]), sb("scan_hi", [P, 2, K])
        scan_in2 = sb("scan_in2", [P, 2, K])
        tile_flags = sb("tile_flags", [P, 2, 2])
        line = sb("line", [1, 4, 2 * P])
        line_sc, line_ex = sb("line_sc", [1, 2, 2 * P]), sb("line_ex", [1, 2, 2 * P])
        run_carry = sb("run_carry", [P, 2, 2])
        linked, whole = sb("linked", [P, 2 * P]), sb("whole", [P, 2 * P])
        cols = sb("cols", [P, 4, T])
        firstlast = sb("firstlast", [P, T, 2])
        valid, tmp_c = sb("valid", [P, T]), sb("tmp_c", [P, T])
        idx_src, idx_dst = sb("idx_src", [P, T], I32), sb("idx_dst", [P, T], I32)
        idx_out, idx_x1 = sb("idx_out", [P, T], I32), sb("idx_x1", [P, T], I32)
        rdst, weight0, weight1 = sb("rdst", [P, T]), sb("weight0", [P, T]), sb("weight1", [P, T])
        half_c, scr_c = sb("half_c", [P, T]), sb("scr_c", [P, T])
        hi_i, hi_f, lo_f = sb("hi_i", [P, T], I32), sb("hi_f", [P, T]), sb("lo_f", [P, T])
        hot_lo, hot_hi = sb("hot_lo", [P, 2, GT, P], F16), sb("hot_hi", [P, 2, GT, HI], F16)
        tab_flat = sb("tab_flat", [P, 9 * HI])
        tab = tab_flat[:, :].rearrange("p (a h) -> p a h", a=9)
        tab_i = sb("tab_i", [P, HI], I32)
        tab_out = sb("tab_out", [P, HC, P, 2])
        part = sb("part", [P, 2, T])
        chain_a, chain_b = sb("chain_a", [P, 2, T]), sb("chain_b", [P, 2, T])
        carry = sb("carry", [P, 2, 2 * P])
        carry_rows = sb("carry_rows", [P, 2, 2, P])

        s_consts, s_mask0, s_load, s_idx_ld, s_chain = (sem(n) for n in ("s_consts", "s_mask0", "s_load", "s_idx_ld", "s_chain"))
        s_prefill, s_pe0, s_act0 = (sem(n) for n in ("s_prefill", "s_pe0", "s_act0"))
        s_wt = sem("s_wt")
        s_keys, s_tab = sem("s_keys"), sem("s_tab")
        s_hot, s_hot_used = sem("s_hot"), sem("s_hot_used")
        s_pool_turn = sem("s_pool_turn")
        s_act_turn = sem("s_act_turn")

        mark = {}

        room = sb("room", [P, 38 * GT * D])
        taken = [0, 0]

        def view(area, slots, *shape):
            lo = taken[area]
            taken[area] += slots
            assert taken[area] <= 38
            v_ = room[:, lo * GT * D:(lo + slots) * GT * D]
            if shape[0] == "rows":
                return v_.rearrange("p (u e) -> p u e", u=slots)
            if shape[0] == "tiles":
                return v_.rearrange("p (t d) -> p t d", d=D)
            return v_.rearrange("p (u t d) -> p u t d", u=slots, t=GT)

        xs, axs = view(0, 2, "groups"), view(0, 2, "groups")
        tabs = sb("tabs", [P, 2, GT, 2])
        ids_h, ids_a, ids_c = (sb(f"ids_{n}", [P, 2, GT], I32) for n in "hac")
        ids_b, ids_d = (sb(f"ids_{n}", [P, R, GT], I32) for n in "bd")
        flw = sb("flw", [P, 2, GT, 2])
        PT = 2 * GT
        nx, nz, nx1, nh, nout = (view(0, 2, "tiles") for _ in range(5))
        nx1T = view(0, 2, "rows")

        class Norm:
            def __init__(self, name, n):
                self.st = sb(name + "_st", [P, n, 6])
                self.tmp = sb(name + "_tmp", [P, 4, n])
                self.mean, self.var, self.mhalf, self.rstd = (sb(name + t, [P, n]) for t in ("_mean", "_var", "_mhalf", "_rstd"))

        norm_n, norm_e = Norm("norm_n", 2 * PT), Norm("norm_e", R * GT)

        sN = {n: sem("n_" + n) for n in ("nx", "z1", "x1", "T", "Tev", "O", "h", "z2", "out", "x1st", "outst")}
        sH_xs, sH_st = ([sem(f"h_{n}{u}") for u in range(2)] for n in ("xs", "st"))
        s_hids = sem("h_ids")
        sA = {n: sem("a_" + n) for n in ("ids", "flw", "part", "partev")}
        sA_xs, sA_tab = ([sem(f"a_{n}{u}") for u in range(2)] for n in ("xs", "tab"))
        s_carry0, s_carry1, s_cst0, s_cst1, s_cpe0, s_cpe1 = (sem(n) for n in ("s_carry0", "s_carry1", "s_cst0", "s_cst1", "s_cpe0", "s_cpe1"))

        AT = (0, 1, 0, 1, 2)
        bx1, bz, bh = view(1, R, "groups"), view(1, R, "groups"), view(1, R, "groups")
        baT = view(1, 3, "rows")
        bS, bxs, bxd = view(1, R, "groups"), view(1, R, "groups"), view(1, R, "groups")
        bkey = view(1, R, "rows")
        sB = {n: sem("b_" + n) for n in ("ids", "S", "A", "Aev", "O", "h", "z", "x1")}
        sB_xs, sB_key, sB_xd, sB_st = ([sem(f"b_{n}{u}") for u in range(R)] for n in ("xs", "key", "xd", "st"))

        cxs, cxd, cea = sb("cxs", [P, 2, GT, D]), sb("cxd", [P, 2, GT, D]), sb("cea", [P, 2, GT, DE])
        turned = sb("turned", [P, 4, GT * P])
        csT, cdT, ceT = turned[:, 0:2, :], turned[:, 2:4, :], sb("ceT", [DE, 2, GT * P])
        per = 2 * GT * P
        chT = tab_flat[:, 0:per].rearrange("p (u e) -> p u e", u=2)
        cg, cm = (tab_flat[:, n * per:(n + 1) * per].rearrange("p (u t d) -> p u t d", u=2, t=GT) for n in (1, 2))
        cfl = sb("cfl", [P, 2, GT, 2])
        sC = {n: sem("c_" + n) for n in ("ids", "cfl", "T", "sT", "dT", "eT", "H", "h", "G", "g", "M", "m", "part", "partev")}
        sC_xs, sC_xd, sC_ea, sC_st = ([sem(f"c_{n}{u}") for u in range(2)] for n in ("xs", "xd", "ea", "st"))

        dms, dkey, dS, dxd, daT, dh, dz, dout = bxs, bkey, bS, bxd, baT, bh, bz, bx1
        dxT = turned[:, 0:3, :]
        sD = {n: sem("d_" + n) for n in ("ids", "S", "A", "Aev", "T", "Tev", "O", "h", "z", "out")}
        sD_ms, sD_key, sD_xd, sD_st = ([sem(f"d_{n}{u}") for u in range(R)] for n in ("ms", "key", "xd", "st"))

        block = ctx.enter_context(nc.Block())

        def steps(eng, body, count=STEPS):
            body(0)
            with eng.Fori(1, count - 1) as s:
                body(s)
            body(count - 1)

        def first(s):
            return isinstance(s, int) and s == 0

        def free(eng, semaphore, g, back):
            if not (isinstance(g, int) and g < back):
                eng.wait_ge(semaphore, g - back + 1)

        def back3(u):
            return next(d for d in range(1, R + 1) if AT[(u - d) % R] == AT[u])

        class Chain:

            def __init__(self, eng, semaphore, share=0):
                self.eng, self.semaphore, self.share, self.base, self.used = eng, semaphore, share, 0, 0

            def begin(self, s):
                self.base, self.used = s * self.share, 0

            def link(self, ins):
                self.used += 1
                ins.then_inc(self.semaphore, 1)
                self.eng.wait_ge(self.semaphore, self.base + self.used)

            def end(self):
                assert self.used <= self.share, self.used
                if self.used < self.share:
                    self.eng.sem_inc(self.semaphore, self.share - self.used)

        def inv_sqrt(chain, y, v_, mhalf, tmp):
            nc.vector.tensor_scalar(mhalf, v_, -0.5, None, ALU.mult)
            chain.link(nc.vector.tensor_scalar(y.bitcast(I32), v_.bitcast(I32), -0.5, float(0x5F3759DF), ALU.mult, ALU.add))
            for _ in range(3):
                chain.link(nc.vector.tensor_tensor(tmp, y, y, ALU.mult))
                chain.link(nc.vector.tensor_tensor(tmp, tmp, mhalf, ALU.mult))
                chain.link(nc.vector.scalar_tensor_tensor(y, tmp, 1.5, y, ALU.add, ALU.mult))

        @block.vector
        def _(v):
            prep = Chain(v, s_chain)
            link = prep.link
            nc.vector.memset(dst_i[:, :, :], int(NO_KEY))
            nc.vector.memset(src_i[:, :, :], 0)
            nc.vector.memset(next_i[:, :], int(NO_KEY))
            link(nc.vector.memset(prev_i[:, :], int(NO_KEY)))
            nc.vector.memset(prev_i[0:1, 0:1], -1).then_inc(s_prefill, 1)
            nc.vector.memset(cea[:, :, :, :], 0.0)
            nc.vector.memset(onesb[:, :], 1.0)
            nc.vector.memset(zerosb[:, :], 0.0)
            nc.vector.memset(weight0[:, :], 1.0)
            nc.vector.memset(carry[:, :, :], 0.0)
            link(nc.vector.memset(rows[:, :, :, :], 0.0))
            mark["fills"] = prep.used
            v.wait_ge(s_idx_ld, 16 * 10)
            key = rows[:, QK, :, :]
            nc.vector.tensor_copy(rows[:, QS, :, 0:K], src_i[:, :, :])
            nc.vector.tensor_copy(prev_f[:, :], prev_i[:, :])
            nc.vector.tensor_copy(next_f[:, :], next_i[:, :])
            link(nc.vector.tensor_copy(key[:, :, 0:K], dst_i[:, :, :]))
            nc.vector.tensor_copy(key[:, :, K:K + 1], key[:, :, 0:1])
            link(nc.vector.tensor_copy(key[:, :, K + 1:P], key[:, :, K - 1:K]))
            mark["keys"] = prep.used
            v.wait_ge(s_consts, 1)
            nc.vector.tensor_copy(iota_h[:, :], iota_i[:, :])
            link(nc.vector.tensor_copy(edge_f[:, :, :], edge_i[:, :, :]))
            nc.vector.tensor_tensor(rows[:, QB, :, 0:1], key[:, :, 0:1], prev_f[:, :].unsqueeze(2), ALU.not_equal)
            nc.vector.tensor_tensor(rows[:, QB, :, 1:K], key[:, :, 1:K], key[:, :, 0:K - 1], ALU.not_equal)
            nc.vector.tensor_tensor(run_last[:, :, K - 1:K], key[:, :, K - 1:K], next_f[:, :].unsqueeze(2), ALU.not_equal)
            link(nc.vector.tensor_tensor(run_last[:, :, 0:K - 1], key[:, :, 0:K - 1], key[:, :, 1:K], ALU.not_equal))
            nc.vector.tensor_tensor(scan_in[:, :, :], rows[:, QB, :, 0:K], edge_f[:, :, :], ALU.mult)
            link(nc.vector.scalar_tensor_tensor(scan_in2[:, :, :], edge_f[:, :, :], 1.0 - FAR, run_last[:, :, :], ALU.add, ALU.mult))
            link(nc.vector.tensor_scalar(scan_in2[:, :, :], scan_in2[:, :, :], FAR, None, ALU.add))
            for c in range(2):
                nc.vector.tensor_tensor_scan(scan_lo[:, c, :], scan_in[:, c, :], scan_in[:, c, :], 0.0, ALU.max, ALU.max)
                nc.vector.tensor_tensor_scan(scan_hi[:, c, ::-1], scan_in2[:, c, ::-1], scan_in2[:, c, ::-1], FAR, ALU.min, ALU.min)
                nc.vector.tensor_scalar(rows[:, QF, c, 0:K], key[:, c, 0:K], key[:, c, 0:1], None, ALU.is_equal)
                nc.vector.tensor_scalar(rows[:, QL, c, 0:K], key[:, c, 0:K], key[:, c, K - 1:K], None, ALU.is_equal)
            nc.vector.tensor_tensor(tile_flags[:, :, 0:1], key[:, :, 0:1], prev_f[:, :].unsqueeze(2), ALU.is_equal)
            link(nc.vector.tensor_tensor(tile_flags[:, :, 1:2], key[:, :, 0:1], key[:, :, K - 1:K], ALU.is_equal))
            mark["scans"] = prep.used
            v.wait_ge(s_pe0, 1)
            nc.vector.tensor_copy(line[0:1, 0:2, :], bank[0][0:1, 0:512].rearrange("o (a b) -> o a b", a=2))
            link(nc.vector.tensor_copy(line[0:1, 2:4, :], bank[1][0:1, 0:512].rearrange("o (a b) -> o a b", a=2)))
            nc.vector.tensor_tensor_scan(line_sc[:, 0, :], line[:, 0, :], line[:, 0, :], 0.0, ALU.max, ALU.max)
            nc.vector.memset(line_ex[:, 0, 0:1], 0.0)
            nc.vector.memset(line_ex[:, 1, 2 * P - 1:2 * P], FAR)
            link(nc.vector.tensor_tensor_scan(line_sc[:, 1, ::-1], line[:, 1, ::-1], line[:, 1, ::-1], FAR, ALU.min, ALU.min))
            nc.vector.tensor_copy(line_ex[:, 0, 1:2 * P], line_sc[:, 0, 0:2 * P - 1])
            link(nc.vector.tensor_copy(line_ex[:, 1, 0:2 * P - 1], line_sc[:, 1, 1:2 * P]))
            mark["lines"] = prep.used
            v.wait_ge(s_pe0, 2)
            nc.vector.tensor_copy(linked[:, :], bank[3][:, 0:2 * P])
            nc.vector.tensor_copy(whole[:, :], bank[3][:, 2 * P:4 * P])
            link(nc.vector.tensor_copy(run_carry[:, :, :], bank[2][:, 0:4].rearrange("p (a c) -> p a c", a=2)))
            for c in range(2):
                nc.vector.tensor_scalar(scan_lo[:, c, :], scan_lo[:, c, :], run_carry[:, 0, c:c + 1], None, ALU.max)
                ins = nc.vector.tensor_scalar(scan_hi[:, c, :], scan_hi[:, c, :], run_carry[:, 1, c:c + 1], None, ALU.min)
            link(ins)
            nc.vector.memset(rows[:, QD, :, K:P], 0.5)
            link(nc.vector.tensor_tensor(rows[:, QD, :, 0:K], scan_hi[:, :, :], scan_lo[:, :, :], ALU.subtract))
            mark["rows"] = prep.used
            v.wait_ge(s_pe0, 3)
            for n in (QK, QS, QD, QB):
                nc.vector.tensor_copy(cols[:, n, :], bank[n][:, 0:T])
            nc.vector.tensor_copy(firstlast[:, :, 0], bank[QF][:, 0:T])
            link(nc.vector.tensor_copy(firstlast[:, :, 1], bank[QL][:, 0:T]))
            mark["cols"] = prep.used
            ckey = cols[:, QK, :]
            nc.vector.tensor_copy(idx_src[:, :], cols[:, QS, :])
            nc.vector.tensor_scalar(hi_i[:, :], ckey, 0.5 - P / 2, 1.0 / P, ALU.add, ALU.mult)
            nc.vector.reciprocal(weight1[:, :], cols[:, QD, :])
            nc.vector.tensor_scalar(tmp_c[:, :], cols[:, QD, :], 1.0, None, ALU.max)
            link(nc.vector.tensor_scalar(valid[:, :], ckey, NO_KEY, None, ALU.is_lt))
            mark["deg"] = prep.used
            nc.vector.tensor_tensor(idx_dst[:, :], ckey, valid[:, :], ALU.mult)
            nc.vector.tensor_tensor(cols[:, QB, :], cols[:, QB, :], valid[:, :], ALU.mult)
            nc.vector.tensor_copy(hi_f[:, :], hi_i[:, :])
            link(nc.vector.scalar_tensor_tensor(weight1[:, :], weight1[:, :], 0.5, valid[:, :], ALU.mult, ALU.mult))
            link(nc.vector.scalar_tensor_tensor(lo_f[:, :], hi_f[:, :], -float(P), ckey, ALU.mult, ALU.add))
            link(nc.vector.scalar_tensor_tensor(cols[:, QB, :], ckey, -SKIP, cols[:, QB, :], ALU.add, ALU.mult))
            nc.vector.tensor_scalar(idx_out[:, :], cols[:, QB, :], SKIP, None, ALU.add)
            inv_sqrt(prep, rdst[:, :], tmp_c[:, :], half_c[:, :], scr_c[:, :])
            link(nc.vector.tensor_tensor(rdst[:, :], rdst[:, :], valid[:, :], ALU.mult))
            mark["idx"] = prep.used

            v.wait_ge(s_load, 16 * 15)
            link(nc.vector.tensor_copy(bias_part[:, :, :], bias_in[:, :, :]))
            nc.vector.tensor_scalar(bias3[:, :, :], bias_part[:, :, :], third_m[:, 0:1], None, ALU.mult)
            link(nc.vector.tensor_tensor(bias_rest[:, :, :], bias_in[:, :, :], bias_part[:, :, :], ALU.subtract))
            for n in (1, 2):
                link(nc.vector.tensor_copy(bias_part[:, :, :], bias_rest[:, :, :]))
                for w in range(4):
                    nc.vector.scalar_tensor_tensor(bias3[:, w, :], bias_part[:, w, :], third_m[:, n:n + 1], bias3[:, w, :], ALU.mult, ALU.add)
                link(nc.vector.tensor_tensor(bias_rest[:, :, :], bias_rest[:, :, :], bias_part[:, :, :], ALU.subtract))
            v.wait_ge(s_wt, 1)
            link(nc.vector.tensor_copy(WT[:, :], bank[6][:, 0:P]))
            mark["weights"] = prep.used
            v.wait_ge(s_act0, 1)


            def sums(nm, lo, hi):
                tmp, st = nm.tmp, nm.st
                nc.vector.tensor_tensor(tmp[:, 0, lo:hi], st[:, lo:hi, 1], st[:, lo:hi, 4], ALU.add)
                nc.vector.tensor_tensor(tmp[:, 1, lo:hi], st[:, lo:hi, 1], st[:, lo:hi, 4], ALU.subtract)
                chain.link(nc.vector.tensor_tensor(tmp[:, 2, lo:hi], st[:, lo:hi, 2], st[:, lo:hi, 5], ALU.add))
                nc.vector.tensor_scalar(nm.mean[:, lo:hi], tmp[:, 0, lo:hi], 0.5, None, ALU.mult)
                chain.link(nc.vector.scalar_tensor_tensor(tmp[:, 3, lo:hi], tmp[:, 1, lo:hi], D / 4.0, tmp[:, 1, lo:hi], ALU.mult, ALU.mult))
                chain.link(nc.vector.tensor_tensor(tmp[:, 3, lo:hi], tmp[:, 3, lo:hi], tmp[:, 2, lo:hi], ALU.add))
                chain.link(nc.vector.tensor_scalar(nm.var[:, lo:hi], tmp[:, 3, lo:hi], 1.0 / D, EPS, ALU.mult, ALU.add))
                inv_sqrt(chain, nm.rstd[:, lo:hi], nm.var[:, lo:hi], nm.mhalf[:, lo:hi], tmp[:, 0, lo:hi])

            def stats(nm, at, z, n):
                for t in range(n):
                    ins = nc.vector.bn_stats(nm.st[:, at + t, :], z[:, t, :])
                return ins

            def normalize(nm, at, dest, z, n):
                for t in range(n):
                    ins = nc.vector.tensor_scalar(dest[:, t, :], z[:, t, :], nm.mean[:, at + t:at + t + 1],
                                                  nm.rstd[:, at + t:at + t + 1], ALU.subtract, ALU.mult)
                return ins

            def nodes(k, k_first=False, k_last=False):
                here, there = not k_last, not k_first
                if here:
                    v.wait_ge(sN["nx"], 32 * (k + 1))
                    if there:
                        v.wait_ge(sN["x1"], k)
                    chain.link(nc.vector.tensor_tensor(nz[:, :, :], nx[:, :, :],
                                                       plain_h[:, :].unsqueeze(1).to_broadcast([P, PT, D]), ALU.add))
                    v.sem_inc(sN["z1"], 1)
                    last = stats(norm_n, 0, nz, PT)
                if there:
                    v.wait_ge(sN["h"], 2 * k)
                    if not (isinstance(k, int) and k == 1):
                        v.wait_ge(sN["out"], k - 1)
                    chain.link(nc.vector.tensor_tensor(nh[:, :, :], nx1[:, :, :], nh[:, :, :], ALU.add))
                    last = stats(norm_n, PT, nh, PT)
                chain.link(last)
                sums(norm_n, 0 if here else PT, 2 * PT if there else PT)
                if here:
                    if there:
                        v.wait_ge(sN["x1st"], 32 * k)
                    normalize(norm_n, 0, nx1, nz, PT).then_inc(sN["x1"], 1)
                if there:
                    if not (isinstance(k, int) and k == 1):
                        v.wait_ge(sN["outst"], 32 * (k - 1))
                    normalize(norm_n, PT, nout, nh, PT).then_inc(sN["out"], 1)

            def hot(s, u):
                g = s * 2 + u
                if not first(s):
                    v.wait_ge(s_hot_used, g - 1)
                for t in range(GT):
                    at = g * GT + t
                    nc.vector.tensor_scalar(hot_lo[:, u, t, :], iota_h[:, 0:P], lo_f[:, bass.ds(at, 1)], None, ALU.is_equal)
                    ins = nc.vector.tensor_scalar(hot_hi[:, u, t, :], iota_h[:, :], hi_f[:, bass.ds(at, 1)], None, ALU.is_equal)
                ins.then_inc(s_hot, 1)

            chain = Chain(v, sem("s_chain_h"), share=18)

            def step_h(s):
                chain.begin(s)
                hot(s, 0)
                hot(s, 1)
                nodes(s, first(s))
                chain.end()

            step_h(0)
            step_h(1)
            with v.Fori(2, STEPS) as s:
                step_h(s)

            v.wait_ge(s_pe0, 4)
            link(nc.vector.tensor_copy(tab[:, 0, :], bank[7][:, 0:HI]))
            mark["counts"] = prep.used
            nc.vector.tensor_scalar(tab[:, 4, :], tab[:, 0, :], 1.0, None, ALU.max)
            link(nc.vector.tensor_scalar(tab[:, 7, :], node_i[:, :], float(SLOTS), None, ALU.add))
            inv_sqrt(prep, tab[:, 5, :], tab[:, 4, :], tab[:, 8, :], tab[:, 6, :])
            v.wait_ge(s_pe0, 5)
            link(nc.vector.tensor_copy(tab[:, 1, :], bank[6][:, 0:HI]))
            link(nc.vector.tensor_tensor_scan(tab[:, 2, :], ones[:, 0:HI], tab[:, 1, :], 0.0, ALU.mult, ALU.add))
            link(nc.vector.tensor_tensor(tab[:, 3, :], tab[:, 2, :], tab[:, 1, :], ALU.subtract))
            link(nc.vector.tensor_tensor(tab[:, 3, :], tab[:, 3, :], bank[5][:, 0:HI], ALU.add))
            link(nc.vector.tensor_scalar(tab_i[:, :], tab[:, 3, :], 0.5 - K / 2, 1.0 / K, ALU.add, ALU.mult))
            link(nc.vector.tensor_copy(tab[:, 6, :], tab_i[:, :]))
            link(nc.vector.scalar_tensor_tensor(tab[:, 3, :], tab[:, 6, :], float(P - K), tab[:, 3, :], ALU.mult, ALU.add))
            link(nc.vector.tensor_tensor(tab[:, 6, :], tab[:, 3, :], tab[:, 7, :], ALU.subtract))
            link(nc.vector.scalar_tensor_tensor(tab[:, 6, :], tab[:, 0, :], 0.0, tab[:, 6, :], ALU.is_gt, ALU.mult))
            link(nc.vector.tensor_tensor(tab[:, 6, :], tab[:, 6, :], tab[:, 7, :], ALU.add))
            mark["tab"] = prep.used
            v.wait_ge(s_pe0, 6)
            full = HC - 1
            rest = HI - full * P
            for w in range(2):
                nc.vector.tensor_copy(tab_out[:, 0:full, :, w], bank[4 + w][:, 0:full * P].rearrange("p (c l) -> p c l", c=full))
                ins = nc.vector.tensor_copy(tab_out[0:rest, full, :, w], bank[4 + w][0:rest, full * P:HC * P])
            link(ins)
            mark["tabout"] = prep.used


            chain = Chain(v, sem("s_chain_a"), share=20)

            def step_a(s):
                chain.begin(s)
                nodes(s + STEPS, False, isinstance(s, int) and s == STEPS - 1)
                for u in range(2):
                    g = s * 2 + u
                    v.wait_ge(sA_tab[u], 64 * (s + 1))
                    if not first(s):
                        v.wait_ge(sA["part"], g - 1)
                    nc.vector.tensor_copy(idx_x1[:, bass.ds(g * GT, GT)], tabs[:, u, :, 1])
                    chain.link(nc.vector.tensor_tensor(weight0[0:K, bass.ds(g * GT, GT)], tabs[0:K, u, :, 0],
                                                       rdst[0:K, bass.ds(g * GT, GT)], ALU.mult))
                    nc.vector.tensor_tensor(flw[:, u, :, :], firstlast[:, bass.ds(g * GT, GT), :],
                                            weight0[:, bass.ds(g * GT, GT)].unsqueeze(2).to_broadcast([P, GT, 2]),
                                            ALU.mult).then_inc(sA["flw"], 1)
                chain.end()

            steps(v, step_a)

            def carries(s_partev, s_cpe, s_carry):
                v.wait_ge(s_partev, G)
                lk, wh = linked[:, 1:T], whole
                nc.vector.tensor_tensor(chain_a[:, 0, 1:T], lk, wh[:, 0:T - 1], ALU.mult)
                nc.vector.tensor_tensor(chain_b[:, 0, 1:T], lk, part[:, 1, 0:T - 1], ALU.mult)
                nc.vector.tensor_tensor(chain_a[:, 1, 0:T - 1], lk, wh[:, 1:T], ALU.mult)
                link(nc.vector.tensor_tensor(chain_b[:, 1, 0:T - 1], lk, part[:, 0, 1:T], ALU.mult))
                nc.vector.tensor_tensor_scan(carry[:, 0, 1:T], chain_a[:, 0, 1:T], chain_b[:, 0, 1:T], 0.0, ALU.mult, ALU.add)
                link(nc.vector.tensor_tensor_scan(carry[:, 1, 0:T - 1][:, ::-1], chain_a[:, 1, 0:T - 1][:, ::-1],
                                                  chain_b[:, 1, 0:T - 1][:, ::-1], 0.0, ALU.mult, ALU.add))
                v.sem_inc(s_cpe, 1)
                v.wait_ge(s_cpe, 2)
                nc.vector.tensor_copy(carry_rows[:, :, :, :].rearrange("p a c d -> p (a c d)"), bank[6][:, :]).then_inc(s_carry, 1)

            carries(sA["partev"], s_cpe0, s_carry0)

            def select(S, keys, weights, s, u, s_key, s_used, s_out):
                g = s * R + u
                v.wait_ge(s_key[u], 16 * (s + 1))
                free(v, s_used, g, R)
                for t in range(GT):
                    at = g * GT + t
                    ins = nc.vector.tensor_scalar(S[:, u, t, :], keys[:, u, t * P:(t + 1) * P], cols[:, QK, bass.ds(at, 1)],
                                                  weights[:, bass.ds(at, 1)], ALU.is_equal, ALU.mult)
                ins.then_inc(s_out, 1)

            def edge_layer(keys, S, weights, xd, h, z, dest, sem_of, s_key, s_xd, xd_count, s_st, st_count, s_done):
                def residual(s, u):
                    g = s * R + u
                    v.wait_ge(s_xd[u], xd_count * (s + 1))
                    v.wait_ge(sem_of["h"], g + 1)
                    free(v, s_done, g, R)
                    nc.vector.tensor_tensor(z[:, u, :, :], xd[:, u, :, :], h[:, u, :, :], ALU.add).then_inc(sem_of["z"], 1)

                def statistics(s, u):
                    v.wait_ge(sem_of["z"], s * R + u + 1)
                    return stats(norm_e, u * GT, z[:, u, :, :], GT)

                def step(s, ahead=True):
                    chain.begin(s)
                    behind = not first(s)
                    for u in range(R):
                        if ahead:
                            select(S, keys, weights, s, u, s_key, sem_of["A"], sem_of["S"])
                        if behind:
                            if u:
                                statistics(s - 1, u - 1)
                            residual(s - 1, u)
                    if behind:
                        chain.link(statistics(s - 1, R - 1))
                        sums(norm_e, 0, R * GT)
                        for u in range(R):
                            if not (isinstance(s, int) and s == 1):
                                v.wait_ge(s_st[u], st_count * (s - 1))
                            normalize(norm_e, u * GT, dest[:, u, :, :], z[:, u, :, :], GT).then_inc(s_done, 1)
                    chain.end()

                step(0)
                step(1)
                with v.Fori(2, RSTEPS) as s:
                    step(s)
                step(RSTEPS, False)

            chain = Chain(v, sem("s_chain_b"), share=16)
            edge_layer(bkey, bS, weight0, bxd, bh, bz, bx1, sB, sB_key, sB_xd, 64, sB_st, 16, sB["x1"])

            def product_c(g, u, n):
                v.wait_ge(sC["M"], g + 1)
                v.wait_ge(sC["g"], g + 1)
                if n is not None:
                    v.wait_ge(sC_st[u], 16 * n)
                nc.vector.scalar_tensor_tensor(cm[:, u, :, :].rearrange("p t d -> p (t d)"), cg[:, u, :, :].rearrange("p t d -> p (t d)"),
                                               1.0, bank[5][:, :], ALU.add, ALU.mult).then_inc(sC["m"], 1)

            def step_c(s):
                for u in range(2):
                    g = s * 2 + u
                    if not first(s):
                        v.wait_ge(sC["part"], g - 1)
                    nc.vector.tensor_tensor(cfl[:, u, :, :], firstlast[:, bass.ds(g * GT, GT), :],
                                            weight1[:, bass.ds(g * GT, GT)].unsqueeze(2).to_broadcast([P, GT, 2]),
                                            ALU.mult).then_inc(sC["cfl"], 1)
                    v.wait_ge(sC["T"], g + 1)
                    if not first(s):
                        v.wait_ge(sC["G"], g - 1)
                    nc.vector.tensor_copy(cdT[:, u, :], bank[1][:, :]).then_inc(sC["dT"], 1)
                    if not (first(s) and u == 0):
                        n = s if u == 1 else s - 1
                        early = first(s) or (isinstance(s, int) and s == 1 and u == 0)
                        product_c(g - 1, 1 - u, None if early else n)

            step_c(0)
            step_c(1)
            with v.Fori(2, STEPS) as s:
                step_c(s)
            product_c(G - 1, 1, STEPS - 1)
            carries(sC["partev"], s_cpe1, s_carry1)

            chain = Chain(v, sem("s_chain_d"), share=16)
            edge_layer(dkey, dS, weight1, dxd, dh, dz, dout, sD, sD_key, sD_xd, 16, sD_st, 64, sD["out"])

        @block.scalar
        def _(act):
            def turn():
                act.sem_inc(s_act_turn, 1)

            act.wait_ge(s_load, 16 * 15)
            nc.scalar.activation(plain_h[:, :], bias_in[:, B_B, :], ACT.Tanh).then_inc(s_act0, 1)

            def keep_part(g, u, s_part, s_partev, b0):
                act.wait_ge(s_part, g + 1)
                turn()
                nc.scalar.activation(part[:, :, bass.ds(g * GT, GT)].rearrange("p a t -> p t a"),
                                     bank[b0 + u][:, 0:2 * GT].rearrange("p (t a) -> p t a", a=2), ACT.Copy).then_inc(s_partev, 1)

            def nodes(k, k_first=False):
                for w in range(2):
                    act.wait_ge(sN["T"], 2 * k + w + 1)
                    if not k_first:
                        act.wait_ge(sN["O"], 2 * k + w - 1)
                    nc.scalar.activation(nx1T[:, w, :], bank[w][:, :], ACT.Copy).then_inc(sN["Tev"], 1)
                for w in range(2):
                    if w == 0 and not k_first:
                        act.wait_ge(sN["out"], k)
                    act.wait_ge(sN["O"], 2 * k + w + 1)
                    nc.scalar.activation(nh[:, w * GT:(w + 1) * GT, :].rearrange("p t d -> p (t d)"), bank[2 + w][:, :],
                                         ACT.Silu).then_inc(sN["h"], 1)

            nodes(0, True)
            with act.Fori(1, STEPS) as k:
                nodes(k)

            def step_a(s):
                if not (isinstance(s, int) and s == STEPS - 1):
                    nodes(s + STEPS)
                for u in range(2):
                    keep_part(s * 2 + u, u, sA["part"], sA["partev"], 4)

            steps(act, step_a)

            def tanh_b(g, u):
                act.wait_ge(sB["O"], g + 1)
                free(act, sB["z"], g, R)
                nc.scalar.activation(bh[:, u, :, :].rearrange("p t d -> p (t d)"), bank[3 + AT[u]][:, :], ACT.Tanh).then_inc(sB["h"], 1)

            def step_b(s):
                for u in range(R):
                    g = s * R + u
                    act.wait_ge(sB["A"], g + 1)
                    free(act, sB["O"], g, back3(u))
                    nc.scalar.activation(baT[:, AT[u], :], bank[AT[u]][:, :], ACT.Copy).then_inc(sB["Aev"], 1)
                    if not (first(s) and u == 0):
                        tanh_b(g - 1, (u - 1) % R)

            step_b(0)
            step_b(1)
            with act.Fori(2, RSTEPS) as s:
                step_b(s)
            tanh_b(G - 1, R - 1)

            def gates_c(g, u):
                early = isinstance(g, int) and g < 2
                act.wait_ge(sC["H"], g + 1)
                if not early:
                    act.wait_ge(sC["M"], g - 1)
                nc.scalar.activation(chT[:, u, :], bank[3][:, :], ACT.Silu, bias=b1c[:, 0:1]).then_inc(sC["h"], 1)
                act.wait_ge(sC["G"], g + 1)
                if not early:
                    act.wait_ge(sC["m"], g - 1)
                nc.scalar.activation(cg[:, u, :, :].rearrange("p t d -> p (t d)"), bank[4][:, :], ACT.Tanh, scale=0.5).then_inc(sC["g"], 1)

            def step_c(s):
                for u in range(2):
                    g = s * 2 + u
                    act.wait_ge(sC["T"], g + 1)
                    if not first(s):
                        act.wait_ge(sC["G"], g - 1)
                    nc.scalar.activation(csT[:, u, :], bank[0][:, :], ACT.Copy).then_inc(sC["sT"], 1)
                    nc.scalar.activation(ceT[:, u, :], bank[2][0:DE, :], ACT.Copy).then_inc(sC["eT"], 1)
                    if not (first(s) and u == 0):
                        gates_c(g - 1, 1 - u)
                    if not first(s):
                        keep_part(g - 2, u, sC["part"], sC["partev"], 6)

            step_c(0)
            step_c(1)
            with act.Fori(2, STEPS) as s:
                step_c(s)
            gates_c(G - 1, 1)
            for u in range(2):
                keep_part(G - 2 + u, u, sC["part"], sC["partev"], 6)

            def silu_d(g, u):
                act.wait_ge(sD["O"], g + 1)
                free(act, sD["z"], g, R)
                nc.scalar.activation(dh[:, u, :, :].rearrange("p t d -> p (t d)"), bank[6 + u % 2][:, :], ACT.Silu).then_inc(sD["h"], 1)

            def step_d(s):
                for u in range(R):
                    g = s * R + u
                    free(act, sD["O"], g, back3(u))
                    act.wait_ge(sD["T"], g + 1)
                    nc.scalar.activation(dxT[:, AT[u], :], bank[3 + AT[u]][:, :], ACT.Copy).then_inc(sD["Tev"], 1)
                    act.wait_ge(sD["A"], g + 1)
                    nc.scalar.activation(daT[:, AT[u], :], bank[AT[u]][:, :], ACT.Copy).then_inc(sD["Aev"], 1)
                    if not (first(s) and u == 0):
                        silu_d(g - 1, (u - 1) % R)

            step_d(0)
            step_d(1)
            with act.Fori(2, RSTEPS) as s:
                step_d(s)
            silu_d(G - 1, R - 1)

        @block.tensor
        def _(pe):
            mm = nc.tensor.matmul

            def transpose(dest, src_, parts=P):
                return nc.tensor.transpose(dest, src_, ident[0:parts, 0:parts])

            pe.wait_ge(s_consts, 1)
            pe.wait_ge(s_load, 16 * 15)
            transpose(bank[6][:, 0:P], Wsb[:, :]).then_inc(s_wt, 1)
            pe.wait_ge(s_chain, mark["scans"])
            for c in range(2):
                for n, col in enumerate((scan_lo[:, c, K - 1:K], scan_hi[:, c, 0:1], tile_flags[:, c, 0:1], tile_flags[:, c, 1:2])):
                    at = (n % 2) * 2 * P + c * P
                    ins = transpose(bank[n // 2][0:1, at:at + P], col)
            ins.then_inc(s_pe0, 1)
            pe.wait_ge(s_chain, mark["lines"])
            for a in range(2):
                for c in range(2):
                    transpose(bank[2][:, 2 * a + c:2 * a + c + 1], line_ex[0:1, a, c * P:(c + 1) * P], 1)
            mm(bank[3][:, :], ones[0:1, 0:P], line[0:1, 2:4, :].rearrange("o a b -> o (a b)"), start=True, stop=True).then_inc(s_pe0, 1)
            pe.wait_ge(s_chain, mark["rows"])
            for n in range(6):
                transpose(bank[n][:, 0:P], rows[:, n, 0, :])
                ins = transpose(bank[n][:, P:T], rows[0:T - P, n, 1, :], T - P)
            ins.then_inc(s_pe0, 1)

            mm(bank[7][:, 0:HI], zerosb[:, 0:P], zerosb[:, 0:HI], start=True, stop=False)

            pe.wait_ge(s_chain, mark["weights"])

            def bias_mm(dest, n):
                return mm(dest, onesb[:, :], bias3[:, n, :].unsqueeze(1).to_broadcast([P, GT, D]), start=True, stop=False)

            def tile_at(t):
                return slice(t * P, (t + 1) * P)

            def nodes(k, k_first=False):
                pe.wait_ge(sN["x1"], k + 1)
                for w in range(2):
                    if not k_first:
                        pe.wait_ge(sN["Tev"], 2 * k + w - 1)
                    for t in range(GT):
                        ins = transpose(bank[w][:, tile_at(t)], nx1[:, w * GT + t, :])
                    ins.then_inc(sN["T"], 1)
                for w in range(2):
                    pe.wait_ge(sN["Tev"], 2 * k + w + 1)
                    if not k_first:
                        pe.wait_ge(sN["h"], 2 * k + w - 1)
                    bias_mm(bank[2 + w][:, :], B_BU)
                    for t in range(GT):
                        ins = mm(bank[2 + w][:, tile_at(t)], nx1T[:, w, tile_at(t)], wux[:, :], start=False, stop=t == GT - 1)
                    ins.then_inc(sN["O"], 1)

            def step_h(s):
                for u in range(2):
                    pe.wait_ge(s_hot, s * 2 + u + 1)
                    for t in range(GT):
                        ins = mm(bank[7][:, 0:HI], hot_lo[0:K, u, t, :], hot_hi[0:K, u, t, :], start=False, stop=False)
                    ins.then_inc(s_hot_used, 1)
                nodes(s, first(s))

            steps(pe, step_h)
            mm(bank[7][:, 0:HI], zerosb[:, 0:P], zerosb[:, 0:HI], start=False, stop=True).then_inc(s_pe0, 1)
            pe.wait_ge(s_chain, mark["counts"])
            mm(bank[5][:, 0:HI], before[:, :], tab[:, 0, :], start=True, stop=True)
            mm(bank[6][:, 0:HI], ones[:, 0:P], tab[:, 0, :], start=True, stop=True).then_inc(s_pe0, 1)
            pe.wait_ge(s_chain, mark["tab"])
            for c in range(HC):
                n = min(P, HI - c * P)
                for w, q in enumerate((5, 6)):
                    ins = transpose(bank[4 + w][0:n, c * P:(c + 1) * P], tab[:, q, c * P:c * P + n])
            ins.then_inc(s_pe0, 1)
            pe.wait_ge(s_chain, mark["tabout"])

            def step_a(s):
                if not (isinstance(s, int) and s == STEPS - 1):
                    nodes(s + STEPS)
                for u in range(2):
                    g = s * 2 + u
                    pe.wait_ge(sA_xs[u], 16 * (s + 1))
                    pe.wait_ge(sA["flw"], g + 1)
                    if not first(s):
                        pe.wait_ge(sA["partev"], g - 1)
                    for t in range(GT):
                        ins = mm(bank[4 + u][:, 2 * t:2 * t + 2], axs[:, u, t, :], flw[:, u, t, :], start=t == 0, stop=t == GT - 1)
                    ins.then_inc(sA["part"], 1)

            steps(pe, step_a)

            def carry_mm(s_cpe):
                pe.wait_ge(s_cpe, 1)
                for a in range(2):
                    for c in range(2):
                        ins = transpose(bank[6][:, (2 * a + c) * P:(2 * a + c + 1) * P], carry[:, a, c * P:(c + 1) * P])
                ins.then_inc(s_cpe, 1)

            carry_mm(s_cpe0)

            def out_b(g, u):
                pe.wait_ge(sB["Aev"], g + 1)
                free(pe, sB["h"], g, back3(u))
                o = bank[3 + AT[u]]
                bias_mm(o[:, :], B_B)
                for t in range(GT):
                    ins = mm(o[:, tile_at(t)], baT[:, AT[u], tile_at(t)], WT[:, :], start=False, stop=t == GT - 1)
                ins.then_inc(sB["O"], 1)

            def step_b(s):
                for u in range(R):
                    g = s * R + u
                    pe.wait_ge(sB_xs[u], 16 * (s + 1))
                    pe.wait_ge(sB["S"], g + 1)
                    free(pe, sB["Aev"], g, back3(u))
                    for t in range(GT):
                        ins = mm(bank[AT[u]][:, tile_at(t)], bxs[:, u, t, :], bS[:, u, t, :], start=t == 0, stop=t == GT - 1)
                    ins.then_inc(sB["A"], 1)
                    if not (first(s) and u == 0):
                        out_b(g - 1, (u - 1) % R)

            step_b(0)
            step_b(1)
            with pe.Fori(2, RSTEPS) as s:
                step_b(s)
            out_b(G - 1, R - 1)
            pe.wait_ge(sB["h"], G)
            pe.wait_ge(s_carry0, 1)

            def transposes_c(s, u):
                g = s * 2 + u
                pe.wait_ge(sC_xd[u], 16 * (s + 1))
                short = isinstance(g, int) and g == G - 1
                pe.wait_ge(sC_ea[u], 16 * (s + 1) + (16 if short else 0))
                pe.wait_ge(sC_xs[u], 64 * (s + 1))
                if not (first(s) and u == 0):
                    for n in ("sT", "dT", "eT"):
                        pe.wait_ge(sC[n], g)
                for t in range(GT):
                    transpose(bank[0][:, tile_at(t)], cxs[:, u, t, :])
                for t in range(GT):
                    transpose(bank[1][:, tile_at(t)], cxd[:, u, t, :])
                for t in range(GT):
                    ins = transpose(bank[2][0:DE, tile_at(t)], cea[:, u, t, :])
                ins.then_inc(sC["T"], 1)

            def messages_c(g, u):
                for n in ("sT", "dT", "eT"):
                    pe.wait_ge(sC[n], g + 1)
                later = not (isinstance(g, int) and g == 0)
                if later:
                    pe.wait_ge(sC["h"], g)
                mm(bank[3][:, :], w1s[:, :], csT[:, u, :], start=True, stop=False)
                mm(bank[3][:, :], w1d[:, :], cdT[:, u, :], start=False, stop=False)
                mm(bank[3][:, :], w1e[:, :], ceT[:, u, :], start=False, stop=True).then_inc(sC["H"], 1)
                if later:
                    pe.wait_ge(sC["g"], g)
                bias_mm(bank[4][:, :], B_BG)
                for t in range(GT):
                    mm(bank[4][:, tile_at(t)], csT[:, u, tile_at(t)], wgs[:, :], start=False, stop=False)
                    mm(bank[4][:, tile_at(t)], cdT[:, u, tile_at(t)], wgd[:, :], start=False, stop=False)
                    ins = mm(bank[4][:, tile_at(t)], ceT[:, u, tile_at(t)], wge[:, :], start=False, stop=t == GT - 1)
                ins.then_inc(sC["G"], 1)
                if later:
                    pe.wait_ge(sC["m"], g)
                pe.wait_ge(sC["h"], g + 1)
                bias_mm(bank[5][:, :], B_B2)
                for t in range(GT):
                    ins = mm(bank[5][:, tile_at(t)], chT[:, u, tile_at(t)], w2sb[:, :], start=False, stop=t == GT - 1)
                ins.then_inc(sC["M"], 1)

            def part_c(g, u):
                pe.wait_ge(sC["m"], g + 1)
                pe.wait_ge(sC["cfl"], g + 1)
                if not (isinstance(g, int) and g < 2):
                    pe.wait_ge(sC["partev"], g - 1)
                for t in range(GT):
                    ins = mm(bank[6 + u][:, 2 * t:2 * t + 2], cm[:, u, t, :], cfl[:, u, t, :], start=t == 0, stop=t == GT - 1)
                ins.then_inc(sC["part"], 1)

            def step_c(s):
                for u in range(2):
                    g = s * 2 + u
                    transposes_c(s, u)
                    if not first(s):
                        part_c(g - 2, u)
                    if not (first(s) and u == 0):
                        messages_c(g - 1, 1 - u)

            step_c(0)
            step_c(1)
            with pe.Fori(2, STEPS - 1) as s:
                step_c(s)
            step_c(STEPS - 1)
            part_c(G - 2, 0)
            messages_c(G - 1, 1)
            part_c(G - 1, 1)
            pe.wait_ge(sC["partev"], G)
            carry_mm(s_cpe1)

            def out_d(g, u):
                pe.wait_ge(sD["Tev"], g + 1)
                pe.wait_ge(sD["Aev"], g + 1)
                free(pe, sD["h"], g, 2 if u else 1)
                o = bank[6 + u % 2]
                bias_mm(o[:, :], B_BU)
                for t in range(GT):
                    mm(o[:, tile_at(t)], dxT[:, AT[u], tile_at(t)], wux[:, :], start=False, stop=False)
                    ins = mm(o[:, tile_at(t)], daT[:, AT[u], tile_at(t)], wua[:, :], start=False, stop=t == GT - 1)
                ins.then_inc(sD["O"], 1)

            def step_d(s):
                for u in range(R):
                    g = s * R + u
                    pe.wait_ge(sD_xd[u], 16 * (s + 1))
                    free(pe, sD["Tev"], g, back3(u))
                    for t in range(GT):
                        ins = transpose(bank[3 + AT[u]][:, tile_at(t)], dxd[:, u, t, :])
                    ins.then_inc(sD["T"], 1)
                    pe.wait_ge(sD_ms[u], 16 * (s + 1))
                    pe.wait_ge(sD["S"], g + 1)
                    free(pe, sD["Aev"], g, back3(u))
                    for t in range(GT):
                        ins = mm(bank[AT[u]][:, tile_at(t)], dms[:, u, t, :], dS[:, u, t, :], start=t == 0, stop=t == GT - 1)
                    ins.then_inc(sD["A"], 1)
                    if not (first(s) and u == 0):
                        out_d(g - 1, (u - 1) % R)

            step_d(0)
            step_d(1)
            with pe.Fori(2, RSTEPS) as s:
                step_d(s)
            out_d(G - 1, R - 1)

        @block.sync
        def _(sp):
            sp.wait_ge(s_prefill, 1)
            for lst, tile in ((dst, dst_i), (src, src_i)):
                sp.dma_start(tile[:, 0, :], lst[0:P * K].rearrange("(t i) -> t i", i=K)).then_inc(s_idx_ld, 16)
                sp.dma_start(tile[0:C1_TILES - 1, 1, :],
                             lst[P * K:(T_REAL - 1) * K].rearrange("(t i) -> t i", i=K)).then_inc(s_idx_ld, 16)
                sp.dma_start(tile[C1_TILES - 1:C1_TILES, 1, 0:LAST_ROWS],
                             lst[(T_REAL - 1) * K:E].rearrange("(t i) -> t i", t=1)).then_inc(s_idx_ld, 16)
            with nc.allow_non_contiguous_dma(reason="one key per tile"):
                pairs = ((prev_i[1:P, 0:1], K - 1, P - 1), (prev_i[0:C1_TILES, 1:2], P * K - 1, C1_TILES),
                         (next_i[:, 0:1], K, P), (next_i[0:C1_TILES - 1, 1:2], (P + 1) * K, C1_TILES - 1))
                for tile, at, n in pairs:
                    sp.dma_start(tile, dst[at:at + (n - 1) * K + 1].unsqueeze(1)[::K, :]).then_inc(s_idx_ld, 16)
            for tile, ap in ((Wsb[:, :], W), (w1s[:, :], w1[0:D, :]), (w1d[:, :], w1[D:2 * D, :]), (w1e[:, :], w1[2 * D:, :]),
                             (wgs[:, :], wg[0:D, :]), (wgd[:, :], wg[D:2 * D, :]), (wge[:, :], wg[2 * D:, :]),
                             (w2sb[:, :], w2), (wux[:, :], wu[0:D, :]), (wua[:, :], wu[D:, :]),
                             (b1c[:, :], b1.unsqueeze(1))):
                sp.dma_start(tile, ap).then_inc(s_load, 16)
            for n, ap in ((B_B, b), (B_B2, b2), (B_BG, bg), (B_BU, bu)):
                sp.dma_start(bias_in[:, n, :], ap.unsqueeze(0).to_broadcast([P, D])).then_inc(s_load, 16)
            sp.wait_ge(s_chain, mark["keys"])
            sp.dma_start(key_rows[0:P, :], rows[:, QK, 0, :]).then_inc(s_keys, 16)
            sp.dma_start(key_rows[P:T, :], rows[0:T - P, QK, 1, :]).then_inc(s_keys, 16)

            def load_nodes(k):
                for w in range(2):
                    g = k * 2 + w
                    parts = NG_LAST_P if isinstance(g, int) and g == NG - 1 else P
                    sp.dma_start(nx[0:parts, w * GT:(w + 1) * GT, :].rearrange("p j d -> p (j d)"),
                                 nodes_of(x, g, 0, parts)).then_inc(sN["nx"], 16)

            def store_nodes(k, tile, table, base, s_done):
                for w in range(2):
                    g = k * 2 + w
                    parts = NG_LAST_P if isinstance(g, int) and g == NG - 1 else P
                    sp.dma_start(nodes_of(table, g, base, parts),
                                 tile[0:parts, w * GT:(w + 1) * GT, :].rearrange("p j d -> p (j d)")).then_inc(s_done, 16)

            def nodes(k, k_first=False, k_last=False, k_next=True):
                if k_next:
                    sp.wait_ge(sN["z1"], k + 1)
                    load_nodes(k + 1)
                if not k_last:
                    sp.wait_ge(sN["x1"], k + 1)
                    store_nodes(k, nx1, x1_tab, SLOTS, sN["x1st"])
                if not k_first:
                    sp.wait_ge(sN["out"], k)
                    store_nodes(k - 1, nout, out, 0, sN["outst"])

            load_nodes(0)

            def step_h(s):
                for u in range(2):
                    sp.wait_ge(sH_xs[u], 64 * (s + 1))
                    sp.dma_start(slots_of(src_feat, s * 2 + u), xs[:, u, :, :]).then_inc(sH_st[u], 16)
                nodes(s, first(s))

            steps(sp, step_h)
            sp.wait_ge(s_chain, mark["tabout"])
            full = HC - 1
            sp.dma_start(node_tab[0:full * P * P, :].rearrange("(c p l) w -> p c (l w)", p=P, l=P),
                         tab_out[:, 0:full, :, :].rearrange("p c l w -> p c (l w)")).then_inc(s_tab, 16)
            sp.dma_start(node_tab[full * P * P:HI * P, :].rearrange("(p l) w -> p (l w)", l=P),
                         tab_out[0:HI - full * P, full, :, :].rearrange("p l w -> p (l w)")).then_inc(s_tab, 16)

            for u in range(2):
                sp.wait_ge(sH_st[u], 16 * STEPS)

            def load_a(s, u):
                if not first(s):
                    sp.wait_ge(sA["part"], s * 2 + u - 1)
                sp.dma_start(axs[:, u, :, :], slots_of(src_feat, s * 2 + u)).then_inc(sA_xs[u], 16)

            def step_a(s):
                k = s + STEPS
                end = isinstance(s, int)
                nodes(k, False, end and k == PAIRS, not (end and k >= PAIRS - 1))
                if not (end and s == STEPS - 1):
                    for u in range(2):
                        load_a(s + 1, u)

            for u in range(2):
                load_a(0, u)
            step_a(0)
            with sp.Fori(1, STEPS - 3) as s:
                step_a(s)
            for s in range(STEPS - 3, STEPS):
                step_a(s)

            sp.wait_ge(s_carry0, 1)
            for side in range(2):
                for c, n in ((0, P), (1, T - P)):
                    sp.dma_start(src_feat.rearrange("(t s) d -> t s d", s=P)[c * P:c * P + n, K + side, :],
                                 carry_rows[0:n, side, c, :]).then_inc(s_cst0, 16)
            sp.wait_ge(s_cst0, 64)
            sp.wait_ge(s_keys, 32)

            def load_b(s, u):
                g = s * R + u
                free(sp, sB["S"], g, R)
                sp.dma_start(bkey[:, u, :], key_rows[bass.ds(g * GT, GT), :].rearrange("t s -> (t s)").unsqueeze(0)
                             .to_broadcast([P, GT * P])).then_inc(sB_key[u], 16)
                free(sp, sB["A"], g, R)
                sp.dma_start(bxs[:, u, :, :], slots_of(src_feat, g)).then_inc(sB_xs[u], 16)

            def store_b(s, u):
                g = s * R + u
                sp.wait_ge(sB["x1"], g + 1)
                sp.dma_start(slots_of(x1_tab, g), bx1[:, u, :, :]).then_inc(sB_st[u], 16)

            def step_b(s):
                if not (isinstance(s, int) and s == RSTEPS - 1):
                    for u in range(R):
                        load_b(s + 1, u)
                if not first(s):
                    for u in range(R):
                        store_b(s - 1, u)

            for u in range(R):
                load_b(0, u)
            steps(sp, step_b, RSTEPS)
            for u in range(R):
                store_b(RSTEPS - 1, u)

            for u in range(R):
                sp.wait_ge(sB_st[u], 16 * RSTEPS)

            def load_c(s, u):
                g = s * 2 + u
                if not first(s):
                    sp.wait_ge(sC["T"], g - 1)
                sp.dma_start(cxd[:, u, :, :], slots_of(x1_tab, g)).then_inc(sC_xd[u], 16)
                at = g * (GT * K)
                if isinstance(g, int) and g == G - 1:
                    full = T_REAL - 1 - g * GT
                    sp.dma_start(cea[0:K, u, 0:full, :],
                                 edge_attr[at:at + full * K, :].rearrange("(t i) d -> i t d", i=K)).then_inc(sC_ea[u], 16)
                    sp.dma_start(cea[0:LAST_ROWS, u, full, :], edge_attr[at + full * K:E, :]).then_inc(sC_ea[u], 16)
                else:
                    sp.dma_start(cea[0:K, u, :, :],
                                 edge_attr[bass.ds(at, GT * K), :].rearrange("(t i) d -> i t d", i=K)).then_inc(sC_ea[u], 16)

            def store_c(g, u):
                sp.wait_ge(sC["m"], g + 1)
                sp.dma_start(slots_of(messages, g), cm[:, u, :, :]).then_inc(sC_st[u], 16)

            def step_c(s):
                for u in range(2):
                    if not (isinstance(s, int) and s == STEPS - 1):
                        load_c(s + 1, u)
                    if not (first(s) and u == 0):
                        store_c(s * 2 + u - 1, 1 - u)

            for u in range(2):
                load_c(0, u)
            step_c(0)
            with sp.Fori(1, STEPS - 2) as s:
                step_c(s)
            step_c(STEPS - 2)
            step_c(STEPS - 1)
            store_c(G - 1, 1)

            for u in range(2):
                sp.wait_ge(sC_st[u], 16 * STEPS)
            sp.wait_ge(s_carry1, 1)
            for side in range(2):
                for c, n in ((0, P), (1, T - P)):
                    sp.dma_start(messages.rearrange("(t s) d -> t s d", s=P)[c * P:c * P + n, K + side, :],
                                 carry_rows[0:n, side, c, :]).then_inc(s_cst1, 16)
            sp.wait_ge(s_cst1, 64)

            def load_d(s, u):
                g = s * R + u
                free(sp, sD["S"], g, R)
                sp.dma_start(dkey[:, u, :], key_rows[bass.ds(g * GT, GT), :].rearrange("t s -> (t s)").unsqueeze(0)
                             .to_broadcast([P, GT * P])).then_inc(sD_key[u], 16)
                free(sp, sD["A"], g, R)
                sp.dma_start(dms[:, u, :, :], slots_of(messages, g)).then_inc(sD_ms[u], 16)

            def load_residual_d(s, u):
                g = s * R + u
                free(sp, sD["z"], g, R)
                sp.dma_start(dxd[:, u, :, :], slots_of(x1_tab, g)).then_inc(sD_xd[u], 16)

            for u in range(R):
                load_d(0, u)
                load_residual_d(0, u)

            def step_d(s):
                for u in range(R):
                    load_d(s + 1, u)
                for u in range(R):
                    load_residual_d(s + 1, u)

            step_d(0)
            with sp.Fori(1, RSTEPS - 1) as s:
                step_d(s)
            for u in range(R):
                sp.wait_ge(sD_st[u], 64 * RSTEPS)

        @block.gpsimd
        def _(pool):
            nc.gpsimd.iota(iota_i[:, :], pattern=[[1, HI]], base=0, channel_multiplier=0)
            nc.gpsimd.iota(node_i[:, :], pattern=[[P, HI]], base=0, channel_multiplier=1)
            nc.gpsimd.iota(edge_i[:, :, :], pattern=[[P * K, 2], [1, K]], base=0, channel_multiplier=K)
            nc.gpsimd.memset(ones[:, :], 1.0).then_inc(s_mask0, 1)
            pool.wait_ge(s_mask0, 1)
            nc.gpsimd.affine_select(out=ident[:, :], in_=ones[:, 0:P], pattern=[[-1, P]], compare_op=ALU.is_equal,
                                    fill=0.0, base=0, channel_multiplier=1)
            nc.gpsimd.affine_select(out=third_m[:, :], in_=ones[:, 0:3], pattern=[[-1, 3]], compare_op=ALU.is_equal,
                                    fill=0.0, base=0, channel_multiplier=1)
            nc.gpsimd.affine_select(out=before[:, :], in_=ones[:, 0:P], pattern=[[1, P]], compare_op=ALU.is_gt,
                                    fill=0.0, base=0, channel_multiplier=-1).then_inc(s_consts, 1)
            def turn():
                pool.sem_inc(s_pool_turn, 1)

            def take_ids(ids, idx, s, u, s_ids, n=2):
                g = s * n + u
                nc.gpsimd.tensor_copy(ids[:, u, :], idx[:, bass.ds(g * GT, GT)]).then_inc(s_ids, 1)
                pool.wait_ge(s_ids, g + 1)
                turn()

            def gather(dest, table, ids, u, t, s_done):
                nc.gpsimd.indirect_dma_start(dest, None, table, bass.IndirectOffsetOnAxis(ap=ids[:, u, t:t + 1], axis=0)
                                             ).then_inc(s_done, 16)

            pool.wait_ge(s_chain, mark["deg"])

            def step_h(s):
                for u in range(2):
                    if not first(s):
                        pool.wait_ge(sH_st[u], 16 * s)
                        turn()
                    take_ids(ids_h, idx_src, s, u, s_hids)
                    for t in range(GT):
                        gather(xs[:, u, t, :], x[:, :], ids_h, u, t, sH_xs[u])

            steps(pool, step_h)

            pool.wait_ge(s_tab, 32)

            def step_a(s):
                for u in range(2):
                    if not first(s):
                        pool.wait_ge(sA["flw"], s * 2 + u - 1)
                        turn()
                    take_ids(ids_a, idx_src, s, u, sA["ids"])
                    for t in range(GT):
                        gather(tabs[:, u, t, :], node_tab[:, :], ids_a, u, t, sA_tab[u])

            steps(pool, step_a)

            def step_b(s):
                for u in range(R):
                    if not first(s):
                        pool.wait_ge(sB["z"], s * R + u - R + 1)
                        turn()
                    take_ids(ids_b, idx_dst, s, u, sB["ids"], R)
                    for t in range(GT):
                        gather(bxd[:, u, t, :], x[:, :], ids_b, u, t, sB_xd[u])

            steps(pool, step_b, RSTEPS)

            for u in range(R):
                pool.wait_ge(sB_st[u], 16 * RSTEPS)
            pool.wait_ge(sN["x1st"], 32 * PAIRS)

            def step_c(s):
                for u in range(2):
                    if not first(s):
                        pool.wait_ge(sC["T"], s * 2 + u - 1)
                        turn()
                    take_ids(ids_c, idx_x1, s, u, sC["ids"])
                    for t in range(GT):
                        gather(cxs[:, u, t, :], x1_tab[:, :], ids_c, u, t, sC_xs[u])

            steps(pool, step_c)

            pool.wait_ge(sN["outst"], 32 * PAIRS)

            def step_d(s):
                for u in range(R):
                    if not first(s):
                        pool.wait_ge(sD_st[u], 64 * s)
                        turn()
                    take_ids(ids_d, idx_out, s, u, sD["ids"], R)
                    pool.wait_ge(sD["out"], s * R + u + 1)
                    turn()
                    for t in range(GT):
                        nc.gpsimd.indirect_dma_start(out[:, :], bass.IndirectOffsetOnAxis(ap=ids_d[:, u, t:t + 1], axis=0),
                                                     dout[:, u, t, :], None, bounds_check=N - 1, oob_is_err=False
                                                     ).then_inc(sD_st[u], 16)

            steps(pool, step_d, RSTEPS)


_INS = ["x", "src", "dst", "edge_attr_64", "L0_gnn_W", "L0_gnn_b", "L1_gnn_w1", "L1_gnn_b1", "L1_gnn_w2", "L1_gnn_b2",
        "L1_gnn_wg", "L1_gnn_bg", "L1_gnn_wu", "L1_gnn_bu"]


def kernel(**inputs):
    import concourse.bacc as _bacc
    from concourse.bass_utils import run_bass_kernel_spmd as _run

    nc = _bacc.Bacc("TRN2", target_bir_lowering=False, num_devices=1)
    arrays, args = {}, []
    for name in _INS:
        a = np.ascontiguousarray(inputs[name])
        arrays[f"in_{name}_dram"] = a
        args.append(nc.dram_tensor(f"in_{name}_dram", a.shape, mybir.dt.from_np(a.dtype), kind="ExternalInput").ap())
    shape = inputs["x"].shape
    args.append(nc.dram_tensor("out_dram", shape, F32, kind="ExternalOutput").ap())
    gnn_kernel(nc, *args)
    r = _run(nc, [arrays], core_ids=[0])
    return r.results[0]["out_dram"]
```

```python
import numpy as np
import concourse.bass as bass
from concourse import mybir
from contextlib import ExitStack

F32, I32, F16, BF16 = mybir.dt.float32, mybir.dt.int32, mybir.dt.float16, mybir.dt.bfloat16
ALU, ACT = mybir.AluOpType, mybir.ActivationFunctionType


def gnn_kernel(nc, x, src, dst, edge_attr, W, b, w1, b1, w2, b2, wg, bg, wu, bu, out):
    P = 128
    N, D = x.shape
    E = src.shape[0]
    DE = edge_attr.shape[1]
    K = P - 2
    GT = 4
    T_REAL = -(-E // K)
    T = -(-T_REAL // (2 * GT)) * 2 * GT
    G = T // GT
    STEPS = G // 2
    R = 5
    RSTEPS = G // R
    assert RSTEPS * R == G
    SLOTS = T * P
    LAST_ROWS = E - (T_REAL - 1) * K
    NODE_GROUP = GT * P
    NG = -(-N // NODE_GROUP)
    NG_LAST_P = (N - (NG - 1) * NODE_GROUP) // GT
    PAIRS = NG // 2
    assert NG % 2 == 0 and 2 * STEPS == PAIRS + 1 and (N - (NG - 1) * NODE_GROUP) % GT == 0
    HI = -(-N // P)
    HC = -(-HI // P)
    NO_KEY = 65535.0
    SKIP = 70000.0
    FAR = 1.0e6
    EPS = 1e-5
    C1_TILES = T_REAL - P

    def dram(name, shape, dt):
        return nc.dram_tensor(name, shape, dt, kind="Internal").ap()

    key_rows = dram("key_rows", (T, P), F32)
    node_tab = dram("node_tab", (HI * P, 2), F32)
    src_feat = dram("src_feat", (SLOTS, D), F32)
    messages = dram("messages", (SLOTS, D), F32)
    x1_tab = dram("x1_tab", (SLOTS + N, D), F32)

    def slots_of(tab, g):
        return tab[bass.ds(g * (GT * P), GT * P), :].rearrange("(t s) d -> s t d", s=P)

    def nodes_of(tab, g, base=0, parts=P):
        return tab[bass.ds(g * NODE_GROUP + base, parts * GT), :].rearrange("(p j) d -> p (j d)", j=GT)

    ctx = ExitStack()
    with ctx:
        def sb(name, shape, dt=F32):
            return ctx.enter_context(nc.sbuf_tensor(name, shape, dt))

        def sem(name):
            return ctx.enter_context(nc.semaphore(name))

        bank = [ctx.enter_context(nc.psum_tensor(f"bank{i}", [P, 512], F32)) for i in range(8)]

        ident = sb("ident", [P, P])
        before = sb("before", [P, P])
        ones = sb("ones", [P, 512])
        onesb = sb("onesb", [P, P], BF16)
        zerosb = sb("zerosb", [P, 512], BF16)
        iota_i = sb("iota_i", [P, HI], I32)
        iota_h = sb("iota_h", [P, HI], F16)
        node_i = sb("node_i", [P, HI], I32)
        edge_i = sb("edge_i", [P, 2, K], I32)
        third_m = sb("third_m", [P, 3])
        Wsb, WT = sb("Wsb", [P, D]), sb("WT", [P, D])
        w1s, w1d, w1e = sb("w1s", [P, D]), sb("w1d", [P, D]), sb("w1e", [DE, D])
        wgs, wgd, wge = sb("wgs", [P, D]), sb("wgd", [P, D]), sb("wge", [P, D])
        w2sb, wux, wua = sb("w2sb", [P, D]), sb("wux", [P, D]), sb("wua", [P, D])
        b1c = sb("b1c", [P, 1])
        bias_in = sb("bias_in", [P, 4, D])
        bias_rest = sb("bias_rest", [P, 4, D])
        bias_part = sb("bias_part", [P, 4, D], BF16)
        bias3 = sb("bias3", [P, 4, D], BF16)
        plain_h = sb("plain_h", [P, D])
        B_B, B_B2, B_BG, B_BU = range(4)

        dst_i, src_i = sb("dst_i", [P, 2, K], I32), sb("src_i", [P, 2, K], I32)
        prev_i, next_i = sb("prev_i", [P, 2], I32), sb("next_i", [P, 2], I32)
        prev_f, next_f = sb("prev_f", [P, 2]), sb("next_f", [P, 2])
        QK, QS, QD, QB, QF, QL = range(6)
        rows = sb("rows", [P, 6, 2, P])
        edge_f = sb("edge_f", [P, 2, K])
        run_last = sb("run_last", [P, 2, K])
        scan_in, scan_lo, scan_hi = sb("scan_in", [P, 2, K]), sb("scan_lo", [P, 2, K]), sb("scan_hi", [P, 2, K])
        scan_in2 = sb("scan_in2", [P, 2, K])
        tile_flags = sb("tile_flags", [P, 2, 2])
        line = sb("line", [1, 4, 2 * P])
        line_sc, line_ex = sb("line_sc", [1, 2, 2 * P]), sb("line_ex", [1, 2, 2 * P])
        run_carry = sb("run_carry", [P, 2, 2])
        linked, whole = sb("linked", [P, 2 * P]), sb("whole", [P, 2 * P])
        cols = sb("cols", [P, 4, T])
        firstlast = sb("firstlast", [P, T, 2])
        valid, tmp_c = sb("valid", [P, T]), sb("tmp_c", [P, T])
        idx_src, idx_dst = sb("idx_src", [P, T], I32), sb("idx_dst", [P, T], I32)
        idx_out, idx_x1 = sb("idx_out", [P, T], I32), sb("idx_x1", [P, T], I32)
        rdst, weight0, weight1 = sb("rdst", [P, T]), sb("weight0", [P, T]), sb("weight1", [P, T])
        half_c, scr_c = sb("half_c", [P, T]), sb("scr_c", [P, T])
        hi_i, hi_f, lo_f = sb("hi_i", [P, T], I32), sb("hi_f", [P, T]), sb("lo_f", [P, T])
        hot_lo, hot_hi = sb("hot_lo", [P, 2, GT, P], F16), sb("hot_hi", [P, 2, GT, HI], F16)
        tab_flat = sb("tab_flat", [P, 9 * HI])
        tab = tab_flat[:, :].rearrange("p (a h) -> p a h", a=9)
        tab_i = sb("tab_i", [P, HI], I32)
        tab_out = sb("tab_out", [P, HC, P, 2])
        part = sb("part", [P, 2, T])
        chain_a, chain_b = sb("chain_a", [P, 2, T]), sb("chain_b", [P, 2, T])
        carry = sb("carry", [P, 2, 2 * P])
        carry_rows = sb("carry_rows", [P, 2, 2, P])

        s_consts, s_mask0, s_load, s_idx_ld, s_chain = (sem(n) for n in ("s_consts", "s_mask0", "s_load", "s_idx_ld", "s_chain"))
        s_prefill, s_pe0, s_act0 = (sem(n) for n in ("s_prefill", "s_pe0", "s_act0"))
        s_wt = sem("s_wt")
        s_keys, s_tab = sem("s_keys"), sem("s_tab")
        s_hot, s_hot_used = sem("s_hot"), sem("s_hot_used")
        s_pool_turn = sem("s_pool_turn")
        s_act_turn = sem("s_act_turn")

        mark = {}

        room = sb("room", [P, 38 * GT * D])
        taken = [0, 0]

        def view(area, slots, *shape):
            lo = taken[area]
            taken[area] += slots
            assert taken[area] <= 38
            v_ = room[:, lo * GT * D:(lo + slots) * GT * D]
            if shape[0] == "rows":
                return v_.rearrange("p (u e) -> p u e", u=slots)
            if shape[0] == "tiles":
                return v_.rearrange("p (t d) -> p t d", d=D)
            return v_.rearrange("p (u t d) -> p u t d", u=slots, t=GT)

        axs = view(0, 4, "groups")
        tabs = sb("tabs", [P, 4, GT, 2])
        ids_h, ids_a = (sb(f"ids_{n}", [P, 4, GT], I32) for n in "ha")
        ids_c = sb("ids_c", [P, 2, GT], I32)
        ids_b, ids_d = (sb(f"ids_{n}", [P, R, GT], I32) for n in "bd")
        flw = sb("flw", [P, 4, GT, 2])
        PT = 2 * GT
        ACT_TILES = 6
        nx, nz, nx1, nh, nz2, nout = ([view(0, 2, "tiles") for _ in range(2)] for _ in range(6))
        nx1T = [view(0, 2, "rows") for _ in range(2)]
        xs = view(0, 4, "groups")

        class Norm:
            def __init__(self, name, n):
                self.st = sb(name + "_st", [P, n, 6])
                self.tmp = sb(name + "_tmp", [P, 4, n])
                self.mean, self.var, self.mhalf, self.rstd = (sb(name + t, [P, n]) for t in ("_mean", "_var", "_mhalf", "_rstd"))

        shift_n = [sb(f"shift_n{q}", [P, 2 * PT]) for q in range(2)]
        rstd_n = [sb(f"rstd_n{q}", [P, 2 * PT]) for q in range(2)]
        norm_n, norm_e = Norm("norm_n", 2 * PT), Norm("norm_e", R * GT)

        sN = {n: sem("n_" + n) for n in ("z1", "st1", "norm", "x1", "T", "Tev", "O", "h", "z2", "out", "out_v")}
        sN_x, sN_x1st, sN_outst = ([sem(f"n_{n}_{q}") for q in range(2)] for n in ("x", "x1st", "outst"))
        sH_xs, sH_st = ([sem(f"h_{n}{u}") for u in range(4)] for n in ("xs", "st"))
        s_hids = sem("h_ids")
        sA = {n: sem("a_" + n) for n in ("ids", "w", "flw", "part", "partev")}
        sA_xs, sA_tab = ([sem(f"a_{n}{u}") for u in range(4)] for n in ("xs", "tab"))
        s_carry0, s_carry1, s_cst0, s_cst1, s_cpe0, s_cpe1 = (sem(n) for n in ("s_carry0", "s_carry1", "s_cst0", "s_cst1", "s_cpe0", "s_cpe1"))

        AT = (0, 1, 0, 1, 2)
        bx1, bz, bh = view(1, R, "groups"), view(1, R, "groups"), view(1, R, "groups")
        baT = view(1, 3, "rows")
        bS, bxs = view(1, R, "groups"), view(1, R, "groups")
        bkey, bxd = view(1, R, "rows"), view(1, R, "groups")
        sB = {n: sem("b_" + n) for n in ("ids", "S", "A", "Aev", "O", "h", "z", "x1")}
        sB_xs, sB_key, sB_xd, sB_st = ([sem(f"b_{n}{u}") for u in range(R)] for n in ("xs", "key", "xd", "st"))

        cxs, cxd, cea = sb("cxs", [P, 2, GT, D]), sb("cxd", [P, 2, GT, D]), sb("cea", [P, 2, GT, DE])
        turned = sb("turned", [P, 4, GT * P])
        csT, cdT, ceT = turned[:, 0:2, :], turned[:, 2:4, :], sb("ceT", [P, 2, GT * P])
        per = 2 * GT * P
        chT = tab_flat[:, 0:per].rearrange("p (u e) -> p u e", u=2)
        cg, cm = (tab_flat[:, n * per:(n + 1) * per].rearrange("p (u t d) -> p u t d", u=2, t=GT) for n in (1, 2))
        cfl = sb("cfl", [P, 2, GT, 2])
        sC = {n: sem("c_" + n) for n in ("ids", "cfl", "T", "sT", "dT", "eT", "H", "h", "G", "g", "M", "mb", "m", "part", "partev")}
        sC_xs, sC_xd, sC_ea, sC_st = ([sem(f"c_{n}{u}") for u in range(2)] for n in ("xs", "xd", "ea", "st"))

        dms, dkey, dS, dxd, daT, dh, dz, dout = bxs, bkey, bS, bxd, baT, bh, bz, bx1
        dxT = turned[:, 0:3, :]
        sD = {n: sem("d_" + n) for n in ("ids", "S", "A", "Aev", "T", "Tev", "O", "h", "z", "out")}
        sD_ms, sD_key, sD_xd, sD_st = ([sem(f"d_{n}{u}") for u in range(R)] for n in ("ms", "key", "xd", "st"))

        block = ctx.enter_context(nc.Block())

        def steps(eng, body, count=STEPS):
            body(0)
            with eng.Fori(1, count - 1) as s:
                body(s)
            body(count - 1)

        assert STEPS % 2 == 1 and PAIRS == 2 * STEPS - 1
        HALF = STEPS // 2

        def steps_h(eng, body):
            body(0, 0, 0)
            body(1, 0, 1)
            body(2, 1, 0)
            with eng.Fori(1, HALF) as i:
                body(i * 2 + 1, i, 1)
                body(i * 2 + 2, i + 1, 0)

        def turns_a(j, q):
            return j - HALF - (1 - q)

        def steps_a(eng, body, start=0):
            for s in range(start, 5):
                body(s, (s + STEPS) // 2, (s + STEPS) % 2)
            with eng.Fori(2, HALF - 1) as i:
                body(i * 2 + 1, i + HALF + 1, 0)
                body(i * 2 + 2, i + HALF + 1, 1)
            body(STEPS - 2, 2 * HALF, 0)
            body(STEPS - 1, 2 * HALF, 1)

        def first(s):
            return isinstance(s, int) and s == 0

        def before_pair(k, n):
            return isinstance(k, int) and k < n

        def free(eng, semaphore, g, back):
            if not (isinstance(g, int) and g < back):
                eng.wait_ge(semaphore, g - back + 1)

        def back3(u):
            return next(d for d in range(1, R + 1) if AT[(u - d) % R] == AT[u])

        class Chain:

            def __init__(self, eng, semaphore, share=0):
                self.eng, self.semaphore, self.share, self.base, self.used = eng, semaphore, share, 0, 0

            def begin(self, s):
                self.base, self.used = s * self.share, 0

            def link(self, ins, beside=None, n=0):
                self.used += 1
                ins.then_inc(self.semaphore, 1)
                if beside is not None:
                    beside(n)
                self.eng.wait_ge(self.semaphore, self.base + self.used)

            def end(self):
                assert self.used <= self.share, self.used
                if self.used < self.share:
                    self.eng.sem_inc(self.semaphore, self.share - self.used)

        def inv_sqrt(chain, y, v_, mhalf, tmp, beside=None, n=0):
            nc.vector.tensor_scalar(mhalf, v_, -0.5, None, ALU.mult)
            chain.link(nc.vector.tensor_scalar(y.bitcast(I32), v_.bitcast(I32), -0.5, float(0x5F3759DF), ALU.mult, ALU.add), beside, n)
            for i in range(3):
                chain.link(nc.vector.tensor_tensor(tmp, y, y, ALU.mult), beside, n + 3 * i + 1)
                chain.link(nc.vector.tensor_tensor(tmp, tmp, mhalf, ALU.mult), beside, n + 3 * i + 2)
                chain.link(nc.vector.scalar_tensor_tensor(y, tmp, 1.5, y, ALU.add, ALU.mult), beside, n + 3 * i + 3)

        @block.vector
        def _(v):
            prep = Chain(v, s_chain)
            link = prep.link
            nc.vector.memset(dst_i[:, :, :], int(NO_KEY))
            nc.vector.memset(src_i[:, :, :], 0)
            nc.vector.memset(next_i[:, :], int(NO_KEY))
            link(nc.vector.memset(prev_i[:, :], int(NO_KEY)))
            nc.vector.memset(prev_i[0:1, 0:1], -1).then_inc(s_prefill, 1)
            nc.vector.memset(cea[:, :, :, :], 0.0)
            nc.vector.memset(ceT[:, :, :], 0.0)
            nc.vector.memset(wge[:, :], 0.0).then_inc(s_prefill, 1)
            nc.vector.memset(onesb[:, :], 1.0)
            nc.vector.memset(zerosb[:, :], 0.0)
            nc.vector.memset(weight0[:, :], 1.0)
            nc.vector.memset(carry[:, :, :], 0.0)
            link(nc.vector.memset(rows[:, :, :, :], 0.0))
            link(nc.vector.memset(ceT[DE:DE + 1, :, :], 1.0))
            mark["fills"] = prep.used
            v.wait_ge(s_idx_ld, 16 * 10)
            key = rows[:, QK, :, :]
            nc.vector.tensor_copy(rows[:, QS, :, 0:K], src_i[:, :, :])
            nc.vector.tensor_copy(prev_f[:, :], prev_i[:, :])
            nc.vector.tensor_copy(next_f[:, :], next_i[:, :])
            link(nc.vector.tensor_copy(key[:, :, 0:K], dst_i[:, :, :]))
            nc.vector.tensor_copy(key[:, :, K:K + 1], key[:, :, 0:1])
            link(nc.vector.tensor_copy(key[:, :, K + 1:P], key[:, :, K - 1:K]))
            mark["keys"] = prep.used
            v.wait_ge(s_consts, 1)
            nc.vector.tensor_copy(iota_h[:, :], iota_i[:, :])
            link(nc.vector.tensor_copy(edge_f[:, :, :], edge_i[:, :, :]))
            nc.vector.tensor_tensor(rows[:, QB, :, 0:1], key[:, :, 0:1], prev_f[:, :].unsqueeze(2), ALU.not_equal)
            nc.vector.tensor_tensor(rows[:, QB, :, 1:K], key[:, :, 1:K], key[:, :, 0:K - 1], ALU.not_equal)
            nc.vector.tensor_tensor(run_last[:, :, K - 1:K], key[:, :, K - 1:K], next_f[:, :].unsqueeze(2), ALU.not_equal)
            link(nc.vector.tensor_tensor(run_last[:, :, 0:K - 1], key[:, :, 0:K - 1], key[:, :, 1:K], ALU.not_equal))
            nc.vector.tensor_tensor(scan_in[:, :, :], rows[:, QB, :, 0:K], edge_f[:, :, :], ALU.mult)
            link(nc.vector.scalar_tensor_tensor(scan_in2[:, :, :], edge_f[:, :, :], 1.0 - FAR, run_last[:, :, :], ALU.add, ALU.mult))
            link(nc.vector.tensor_scalar(scan_in2[:, :, :], scan_in2[:, :, :], FAR, None, ALU.add))
            for c in range(2):
                nc.vector.tensor_tensor_scan(scan_lo[:, c, :], scan_in[:, c, :], scan_in[:, c, :], 0.0, ALU.max, ALU.max)
                nc.vector.tensor_tensor_scan(scan_hi[:, c, ::-1], scan_in2[:, c, ::-1], scan_in2[:, c, ::-1], FAR, ALU.min, ALU.min)
                nc.vector.tensor_scalar(rows[:, QF, c, 0:K], key[:, c, 0:K], key[:, c, 0:1], None, ALU.is_equal)
                nc.vector.tensor_scalar(rows[:, QL, c, 0:K], key[:, c, 0:K], key[:, c, K - 1:K], None, ALU.is_equal)
            nc.vector.tensor_tensor(tile_flags[:, :, 0:1], key[:, :, 0:1], prev_f[:, :].unsqueeze(2), ALU.is_equal)
            link(nc.vector.tensor_tensor(tile_flags[:, :, 1:2], key[:, :, 0:1], key[:, :, K - 1:K], ALU.is_equal))
            mark["scans"] = prep.used
            v.wait_ge(s_pe0, 1)
            nc.vector.tensor_copy(line[0:1, 0:2, :], bank[0][0:1, 0:512].rearrange("o (a b) -> o a b", a=2))
            link(nc.vector.tensor_copy(line[0:1, 2:4, :], bank[1][0:1, 0:512].rearrange("o (a b) -> o a b", a=2)))
            nc.vector.tensor_tensor_scan(line_sc[:, 0, :], line[:, 0, :], line[:, 0, :], 0.0, ALU.max, ALU.max)
            nc.vector.memset(line_ex[:, 0, 0:1], 0.0)
            nc.vector.memset(line_ex[:, 1, 2 * P - 1:2 * P], FAR)
            link(nc.vector.tensor_tensor_scan(line_sc[:, 1, ::-1], line[:, 1, ::-1], line[:, 1, ::-1], FAR, ALU.min, ALU.min))
            nc.vector.tensor_copy(line_ex[:, 0, 1:2 * P], line_sc[:, 0, 0:2 * P - 1])
            link(nc.vector.tensor_copy(line_ex[:, 1, 0:2 * P - 1], line_sc[:, 1, 1:2 * P]))
            mark["lines"] = prep.used
            v.wait_ge(s_pe0, 2)
            nc.vector.tensor_copy(linked[:, :], bank[3][:, 0:2 * P])
            nc.vector.tensor_copy(whole[:, :], bank[3][:, 2 * P:4 * P])
            link(nc.vector.tensor_copy(run_carry[:, :, :], bank[2][:, 0:4].rearrange("p (a c) -> p a c", a=2)))
            for c in range(2):
                nc.vector.tensor_scalar(scan_lo[:, c, :], scan_lo[:, c, :], run_carry[:, 0, c:c + 1], None, ALU.max)
                ins = nc.vector.tensor_scalar(scan_hi[:, c, :], scan_hi[:, c, :], run_carry[:, 1, c:c + 1], None, ALU.min)
            link(ins)
            nc.vector.memset(rows[:, QD, :, K:P], 0.5)
            link(nc.vector.tensor_tensor(rows[:, QD, :, 0:K], scan_hi[:, :, :], scan_lo[:, :, :], ALU.subtract))
            mark["rows"] = prep.used
            v.wait_ge(s_pe0, 3)
            for n in (QK, QS, QD, QB):
                nc.vector.tensor_copy(cols[:, n, :], bank[n][:, 0:T])
            nc.vector.tensor_copy(firstlast[:, :, 0], bank[QF][:, 0:T])
            link(nc.vector.tensor_copy(firstlast[:, :, 1], bank[QL][:, 0:T]))
            mark["cols"] = prep.used
            ckey = cols[:, QK, :]
            nc.vector.tensor_copy(idx_src[:, :], cols[:, QS, :])
            nc.vector.tensor_scalar(hi_i[:, :], ckey, 0.5 - P / 2, 1.0 / P, ALU.add, ALU.mult)
            nc.vector.reciprocal(weight1[:, :], cols[:, QD, :])
            nc.vector.tensor_scalar(tmp_c[:, :], cols[:, QD, :], 1.0, None, ALU.max)
            link(nc.vector.tensor_scalar(valid[:, :], ckey, NO_KEY, None, ALU.is_lt))
            mark["deg"] = prep.used
            nc.vector.tensor_tensor(idx_dst[:, :], ckey, valid[:, :], ALU.mult)
            nc.vector.tensor_tensor(cols[:, QB, :], cols[:, QB, :], valid[:, :], ALU.mult)
            nc.vector.tensor_copy(hi_f[:, :], hi_i[:, :])
            link(nc.vector.scalar_tensor_tensor(weight1[:, :], weight1[:, :], 0.5, valid[:, :], ALU.mult, ALU.mult))
            link(nc.vector.scalar_tensor_tensor(lo_f[:, :], hi_f[:, :], -float(P), ckey, ALU.mult, ALU.add))
            link(nc.vector.scalar_tensor_tensor(cols[:, QB, :], ckey, -SKIP, cols[:, QB, :], ALU.add, ALU.mult))
            nc.vector.tensor_scalar(idx_out[:, :], cols[:, QB, :], SKIP, None, ALU.add)
            inv_sqrt(prep, rdst[:, :], tmp_c[:, :], half_c[:, :], scr_c[:, :])
            link(nc.vector.tensor_tensor(rdst[:, :], rdst[:, :], valid[:, :], ALU.mult))
            mark["idx"] = prep.used

            v.wait_ge(s_load, 16 * 16)
            link(nc.vector.tensor_copy(bias_part[:, :, :], bias_in[:, :, :]))
            nc.vector.tensor_scalar(bias3[:, :, :], bias_part[:, :, :], third_m[:, 0:1], None, ALU.mult)
            link(nc.vector.tensor_tensor(bias_rest[:, :, :], bias_in[:, :, :], bias_part[:, :, :], ALU.subtract))
            for n in (1, 2):
                link(nc.vector.tensor_copy(bias_part[:, :, :], bias_rest[:, :, :]))
                for w in range(4):
                    nc.vector.scalar_tensor_tensor(bias3[:, w, :], bias_part[:, w, :], third_m[:, n:n + 1], bias3[:, w, :], ALU.mult, ALU.add)
                link(nc.vector.tensor_tensor(bias_rest[:, :, :], bias_rest[:, :, :], bias_part[:, :, :], ALU.subtract))
            v.wait_ge(s_wt, 1)
            link(nc.vector.tensor_copy(WT[:, :], bank[6][:, 0:P]))
            mark["weights"] = prep.used
            v.wait_ge(s_act0, 1)

            def sums(nm, lo, hi, beside=lambda i: None):
                tmp, st = nm.tmp, nm.st
                nc.vector.tensor_tensor(tmp[:, 0, lo:hi], st[:, lo:hi, 1], st[:, lo:hi, 4], ALU.add)
                nc.vector.tensor_tensor(tmp[:, 1, lo:hi], st[:, lo:hi, 1], st[:, lo:hi, 4], ALU.subtract)
                chain.link(nc.vector.tensor_tensor(tmp[:, 2, lo:hi], st[:, lo:hi, 2], st[:, lo:hi, 5], ALU.add), beside, 0)
                nc.vector.tensor_scalar(nm.mean[:, lo:hi], tmp[:, 0, lo:hi], 0.5, None, ALU.mult)
                chain.link(nc.vector.scalar_tensor_tensor(tmp[:, 3, lo:hi], tmp[:, 1, lo:hi], D / 4.0, tmp[:, 1, lo:hi], ALU.mult, ALU.mult), beside, 1)
                chain.link(nc.vector.tensor_tensor(tmp[:, 3, lo:hi], tmp[:, 3, lo:hi], tmp[:, 2, lo:hi], ALU.add), beside, 2)
                chain.link(nc.vector.tensor_scalar(nm.var[:, lo:hi], tmp[:, 3, lo:hi], 1.0 / D, EPS, ALU.mult, ALU.add), beside, 3)
                inv_sqrt(chain, nm.rstd[:, lo:hi], nm.var[:, lo:hi], nm.mhalf[:, lo:hi], tmp[:, 0, lo:hi], beside, 4)

            def stats(nm, at, z, n):
                for t in range(n):
                    ins = nc.vector.bn_stats(nm.st[:, at + t, :], z[:, t, :])
                return ins

            def normalize(nm, at, dest, z, n):
                for t in range(n):
                    ins = nc.vector.tensor_scalar(dest[:, t, :], z[:, t, :], nm.mean[:, at + t:at + t + 1],
                                                  nm.rstd[:, at + t:at + t + 1], ALU.subtract, ALU.mult)
                return ins

            def first_sum(j, q):
                k = j * 2 + q
                v.wait_ge(sN_x[q], 32 * (j + 1))
                if not before_pair(k, 2):
                    v.wait_ge(sN["x1"], 2 * (k - 1))
                nc.vector.tensor_tensor(nz[q], nx[q], plain_h[:, :].unsqueeze(1).to_broadcast([P, PT, D]),
                                        ALU.add).then_inc(sN["z1"], 1)

            def first_stat(k, q, t):
                if t == 0:
                    v.wait_ge(sN["z1"], k + 1)
                ins = nc.vector.bn_stats(norm_n.st[:, t, :], nz[q][:, t, :])
                if t == PT - 1:
                    ins.then_inc(sN["st1"], 1)

            def nodes(j, q, here=True, ahead=True, beside=lambda i: None, shared=False):
                k = j * 2 + q
                there = not before_pair(k, 2)
                if there:
                    v.wait_ge(sN["h"], 2 * (k - 1))
                    if not before_pair(k, 4):
                        v.wait_ge(sN["out"], k - 3)
                    if shared and not before_pair(k, STEPS + 2):
                        v.wait_ge(sN["out_v"], k - 1 - STEPS)
                    nc.vector.tensor_tensor(nz2[q], nx1[q], nh[q], ALU.add).then_inc(sN["z2"], 1)
                    v.wait_ge(sN["z2"], k - 1)
                    chain.link(stats(norm_n, PT, nz2[q], PT))
                if here:
                    v.wait_ge(sN["st1"], k + 1)
                lo, hi = 0 if here else PT, 2 * PT if there else PT
                if not before_pair(k, 2):
                    v.wait_ge(sN["x1"], 2 * (k - 1))
                if not before_pair(k, 4):
                    v.wait_ge(sN["out"], k - 3)

                if shared and not before_pair(k, STEPS + 1):
                    v.wait_ge(sN["out_v"], k - STEPS)

                def beside_sums(i):
                    if ahead:
                        if i == 3:
                            first_sum(j + q, 1 - q)
                        if 5 <= i < 5 + PT:
                            first_stat(k + 1, 1 - q, i - 5)
                    beside(i)

                norm_n.rstd = rstd_n[q]
                sums(norm_n, lo, hi, beside_sums)
                nc.vector.scalar_tensor_tensor(shift_n[q][:, lo:hi], norm_n.mean[:, lo:hi], -1.0, norm_n.rstd[:, lo:hi],
                                               ALU.mult, ALU.mult).then_inc(sN["norm"], 1)
                if shared:
                    v.wait_ge(sN_outst[q], 32 * (j - 1))
                    normalize(norm_n, PT + ACT_TILES, nout[q][:, ACT_TILES:PT, :], nz2[q][:, ACT_TILES:PT, :],
                              PT - ACT_TILES).then_inc(sN["out_v"], 1)

            for u in range(R):
                nc.vector.tensor_copy(ids_b[:, u, :], idx_dst[:, u * GT:(u + 1) * GT]).then_inc(sB["ids"], 1)

            def hot(s, u, t):
                g = s * 2 + u
                if t == 0 and not first(s):
                    v.wait_ge(s_hot_used, g - 1)
                at = g * GT + t
                nc.vector.tensor_scalar(hot_lo[:, u, t, :], iota_h[:, 0:P], lo_f[:, bass.ds(at, 1)], None, ALU.is_equal)
                ins = nc.vector.tensor_scalar(hot_hi[:, u, t, :], iota_h[:, :], hi_f[:, bass.ds(at, 1)], None, ALU.is_equal)
                if t == GT - 1:
                    ins.then_inc(s_hot, 1)

            chain = Chain(v, sem("s_chain_h"), share=16)

            def step_h(s, j, q):
                def beside(i):
                    if 1 <= i <= 2 * GT:
                        hot(s, (i - 1) // GT, (i - 1) % GT)

                chain.begin(s)
                nodes(j, q, True, True, beside)
                chain.end()

            first_sum(0, 0)
            for t in range(PT):
                first_stat(0, 0, t)

            steps_h(v, step_h)

            chain = Chain(v, sem("s_chain_a"), share=18)

            def edge_weights(s, turn_, q):
                for u in range(2):
                    g = s * 2 + u
                    slot = 2 * q + u
                    v.wait_ge(sA_tab[slot], 64 * (turn_ + 1))
                    free(v, sA["part"], g, 4)
                    nc.vector.tensor_copy(idx_x1[:, bass.ds(g * GT, GT)], tabs[:, slot, :, 1])
                    nc.vector.tensor_tensor(weight0[0:K, bass.ds(g * GT, GT)], tabs[0:K, slot, :, 0],
                                            rdst[0:K, bass.ds(g * GT, GT)], ALU.mult).then_inc(sA["w"], 1)
                for u in range(2):
                    g = s * 2 + u
                    v.wait_ge(sA["w"], g + 1)
                    nc.vector.tensor_tensor(flw[:, 2 * q + u, :, :], firstlast[:, bass.ds(g * GT, GT), :],
                                            weight0[:, bass.ds(g * GT, GT)].unsqueeze(2).to_broadcast([P, GT, 2]),
                                            ALU.mult).then_inc(sA["flw"], 1)

            def step_a(s, j, q):
                chain.begin(s)
                end = isinstance(s, int)
                nodes(j, q, not (end and s == STEPS - 1), not (end and s >= STEPS - 2), shared=True)
                if not (end and s < 2):
                    edge_weights(s - 2, turns_a(j, q) - 1, q)
                chain.end()

            step_a(0, HALF, 1)

            v.wait_ge(s_pe0, 4)
            link(nc.vector.tensor_copy(tab[:, 0, :], bank[7][:, 0:HI]))
            mark["counts"] = prep.used
            nc.vector.tensor_scalar(tab[:, 4, :], tab[:, 0, :], 1.0, None, ALU.max)
            link(nc.vector.tensor_scalar(tab[:, 7, :], node_i[:, :], float(SLOTS), None, ALU.add))
            inv_sqrt(prep, tab[:, 5, :], tab[:, 4, :], tab[:, 8, :], tab[:, 6, :])
            v.wait_ge(s_pe0, 5)
            link(nc.vector.tensor_copy(tab[:, 1, :], bank[6][:, 0:HI]))
            link(nc.vector.tensor_tensor_scan(tab[:, 2, :], ones[:, 0:HI], tab[:, 1, :], 0.0, ALU.mult, ALU.add))
            link(nc.vector.tensor_tensor(tab[:, 3, :], tab[:, 2, :], tab[:, 1, :], ALU.subtract))
            link(nc.vector.tensor_tensor(tab[:, 3, :], tab[:, 3, :], bank[5][:, 0:HI], ALU.add))
            link(nc.vector.tensor_scalar(tab_i[:, :], tab[:, 3, :], 0.5 - K / 2, 1.0 / K, ALU.add, ALU.mult))
            link(nc.vector.tensor_copy(tab[:, 6, :], tab_i[:, :]))
            link(nc.vector.scalar_tensor_tensor(tab[:, 3, :], tab[:, 6, :], float(P - K), tab[:, 3, :], ALU.mult, ALU.add))
            link(nc.vector.tensor_tensor(tab[:, 6, :], tab[:, 3, :], tab[:, 7, :], ALU.subtract))
            link(nc.vector.scalar_tensor_tensor(tab[:, 6, :], tab[:, 0, :], 0.0, tab[:, 6, :], ALU.is_gt, ALU.mult))
            link(nc.vector.tensor_tensor(tab[:, 6, :], tab[:, 6, :], tab[:, 7, :], ALU.add))
            mark["tab"] = prep.used
            v.wait_ge(s_pe0, 6)
            full = HC - 1
            rest = HI - full * P
            for w in range(2):
                nc.vector.tensor_copy(tab_out[:, 0:full, :, w], bank[4 + w][:, 0:full * P].rearrange("p (c l) -> p c l", c=full))
                ins = nc.vector.tensor_copy(tab_out[0:rest, full, :, w], bank[4 + w][0:rest, full * P:HC * P])
            link(ins)
            mark["tabout"] = prep.used

            steps_a(v, step_a, 1)
            chain.begin(STEPS)
            nodes(STEPS, 0, False, False, shared=True)
            edge_weights(STEPS - 2, HALF - 1, 0)
            edge_weights(STEPS - 1, HALF, 1)

            def select(S, keys, weights, s, u, s_key, s_used, s_out):
                g = s * R + u
                v.wait_ge(s_key[u], 16 * (s + 1))
                free(v, s_used, g, R)
                for t in range(GT):
                    at = g * GT + t
                    ins = nc.vector.tensor_scalar(S[:, u, t, :], keys[:, u, t * P:(t + 1) * P], cols[:, QK, bass.ds(at, 1)],
                                                  weights[:, bass.ds(at, 1)], ALU.is_equal, ALU.mult)
                ins.then_inc(s_out, 1)

            def take_ids_b(s, u):
                nc.vector.tensor_copy(ids_b[:, u, :], idx_dst[:, bass.ds((s * R + u) * GT, GT)]).then_inc(sB["ids"], 1)

            def take_ids_d(s, u):
                nc.vector.tensor_copy(ids_d[:, u, :], idx_out[:, bass.ds((s * R + u) * GT, GT)]).then_inc(sD["ids"], 1)

            def edge_layer(begin, early, late, after_residual, before_norm, keys, S, weights, xd, h, z, dest, sem_of, s_key, s_xd, xd_count, s_st, st_count, s_done):
                def residual(s, u):
                    g = s * R + u
                    v.wait_ge(s_xd[u], xd_count * (s + 1))
                    v.wait_ge(sem_of["h"], g + 1)
                    free(v, s_done, g, R)
                    nc.vector.tensor_tensor(z[:, u, :, :], xd[:, u, :, :], h[:, u, :, :], ALU.add).then_inc(sem_of["z"], 1)
                    after_residual(s, u)

                def statistics(s, u):
                    v.wait_ge(sem_of["z"], s * R + u + 1)
                    return stats(norm_e, u * GT, z[:, u, :, :], GT)

                def norms(s, u, count):
                    for w in range(u, u + count):
                        if not (isinstance(s, int) and s == 0):
                            v.wait_ge(s_st[w], st_count * s)
                        before_norm(s, w)
                        normalize(norm_e, w * GT, dest[:, w, :, :], z[:, w, :, :], GT).then_inc(s_done, 1)

                def step(s, batches=((0, R),), ahead=True):
                    chain.begin(s)
                    behind = not first(s)
                    for u in range(R):
                        if ahead:
                            select(S, keys, weights, s, u, s_key, sem_of["A"], sem_of["S"])
                        if not behind:
                            continue
                        starts = any(u == lo for lo, n in batches)
                        if not starts:
                            statistics(s - 1, u - 1)
                        residual(s - 1, u)
                        for lo, n in batches:
                            if u == lo + n - 1:
                                chain.link(statistics(s - 1, u))
                                sums(norm_e, lo * GT, (lo + n) * GT)
                                norms(s - 1, lo, n)
                    chain.end()

                if begin:
                    step(0)
                    return
                step(1, early)
                with v.Fori(2, RSTEPS) as s:
                    step(s)
                step(RSTEPS, late, False)

            def carries(s_partev, s_cpe, s_carry):
                v.wait_ge(s_partev, G)
                lk, wh = linked[:, 1:T], whole
                nc.vector.tensor_tensor(chain_a[:, 0, 1:T], lk, wh[:, 0:T - 1], ALU.mult)
                nc.vector.tensor_tensor(chain_b[:, 0, 1:T], lk, part[:, 1, 0:T - 1], ALU.mult)
                nc.vector.tensor_tensor(chain_a[:, 1, 0:T - 1], lk, wh[:, 1:T], ALU.mult)
                link(nc.vector.tensor_tensor(chain_b[:, 1, 0:T - 1], lk, part[:, 0, 1:T], ALU.mult))
                nc.vector.tensor_tensor_scan(carry[:, 0, 1:T], chain_a[:, 0, 1:T], chain_b[:, 0, 1:T], 0.0, ALU.mult, ALU.add)
                link(nc.vector.tensor_tensor_scan(carry[:, 1, 0:T - 1][:, ::-1], chain_a[:, 1, 0:T - 1][:, ::-1],
                                                  chain_b[:, 1, 0:T - 1][:, ::-1], 0.0, ALU.mult, ALU.add))
                v.sem_inc(s_cpe, 1)
                v.wait_ge(s_cpe, 2)
                nc.vector.tensor_copy(carry_rows[:, :, :, :].rearrange("p a c d -> p (a c d)"), bank[6][:, :]).then_inc(s_carry, 1)

            layer_b = (bkey, bS, weight0, bxd, bh, bz, bx1, sB, sB_key, sB_xd, 64, sB_st, 16, sB["x1"])
            chain = Chain(v, sem("s_chain_b"), share=32)
            v.wait_ge(sN["out"], PAIRS)
            edge_layer(True, None, None, None, None, *layer_b)
            carries(sA["partev"], s_cpe0, s_carry0)

            def next_ids_b(s, u):
                if not (isinstance(s, int) and s == RSTEPS - 1):
                    take_ids_b(s + 1, u)

            edge_layer(False, ((0, R),), ((0, 3), (3, R - 3)), next_ids_b, lambda s, u: None, *layer_b)

            def product_c(g, u, n):
                v.wait_ge(sC["M"], g + 1)
                if n is not None:
                    v.wait_ge(sC_st[u], 16 * n)
                nc.vector.tensor_tensor(cm[:, u, :, :], bank[5][:, :].rearrange("p (t d) -> p t d", t=GT),
                                        bias_in[:, B_B2, :].unsqueeze(1).to_broadcast([P, GT, D]), ALU.add).then_inc(sC["mb"], 1)
                v.wait_ge(sC["mb"], g + 1)
                v.wait_ge(sC["g"], g + 1)
                nc.vector.scalar_tensor_tensor(cm[:, u, :, :], cg[:, u, :, :], 1.0, cm[:, u, :, :], ALU.add, ALU.mult).then_inc(sC["m"], 1)

            def step_c(s):
                for u in range(2):
                    g = s * 2 + u
                    v.wait_ge(sC["T"], g + 1)
                    if not first(s):
                        v.wait_ge(sC["G"], g - 1)
                    nc.vector.tensor_copy(cdT[:, u, :], bank[1][:, :]).then_inc(sC["dT"], 1)
                    if not (first(s) and u == 0):
                        n = s if u == 1 else s - 1
                        early = first(s) or (isinstance(s, int) and s == 1 and u == 0)
                        product_c(g - 1, 1 - u, None if early else n)
                    if not first(s):
                        v.wait_ge(sC["part"], g - 1)
                    nc.vector.tensor_tensor(cfl[:, u, :, :], firstlast[:, bass.ds(g * GT, GT), :],
                                            weight1[:, bass.ds(g * GT, GT)].unsqueeze(2).to_broadcast([P, GT, 2]),
                                            ALU.mult).then_inc(sC["cfl"], 1)

            step_c(0)
            step_c(1)
            with v.Fori(2, STEPS) as s:
                step_c(s)
            product_c(G - 1, 1, STEPS - 1)
            layer_d = (dkey, dS, weight1, dxd, dh, dz, dout, sD, sD_key, sD_xd, 16, sD_st, 64, sD["out"])
            chain = Chain(v, sem("s_chain_d"), share=32)
            edge_layer(True, None, None, None, None, *layer_d)
            carries(sC["partev"], s_cpe1, s_carry1)

            edge_layer(False, ((0, 2), (2, R - 2)), ((0, 2), (2, R - 2)), lambda s, u: None, take_ids_d, *layer_d)

        @block.scalar
        def _(act):
            def turn():
                act.sem_inc(s_act_turn, 1)

            act.wait_ge(s_load, 16 * 16)
            nc.scalar.activation(plain_h[:, :], bias_in[:, B_B, :], ACT.Tanh).then_inc(s_act0, 1)

            def keep_part(g, u, s_part, s_partev, b0):
                act.wait_ge(s_part, g + 1)
                turn()
                nc.scalar.activation(part[:, :, bass.ds(g * GT, GT)].rearrange("p a t -> p t a"),
                                     bank[b0 + u][:, 0:2 * GT].rearrange("p (t a) -> p t a", a=2), ACT.Copy).then_inc(s_partev, 1)

            def nodes(j, q, here=True, shared=False):
                k = j * 2 + q
                act.wait_ge(sN["norm"], k + 1)
                if here:
                    if not before_pair(k, 2):
                        act.wait_ge(sN_x1st[q], 32 * j)
                    turn()
                    for t in range(PT):
                        ins = nc.scalar.activation(nx1[q][:, t, :], nz[q][:, t, :], ACT.Identity, bias=shift_n[q][:, t:t + 1],
                                                   scale=rstd_n[q][:, t:t + 1])
                        if t % GT == GT - 1:
                            ins.then_inc(sN["x1"], 1)

                def keep_turned(w):
                    act.wait_ge(sN["T"], 2 * k + w + 1)
                    if not before_pair(k, 2):
                        act.wait_ge(sN["O"], 2 * k + w - 3)
                    nc.scalar.activation(nx1T[q][:, w, :], bank[w][:, :], ACT.Copy).then_inc(sN["Tev"], 1)

                def second_norm(lo, hi):
                    for t in range(lo, hi):
                        ins = nc.scalar.activation(nout[q][:, t, :], nz2[q][:, t, :], ACT.Identity,
                                                   bias=shift_n[q][:, PT + t:PT + t + 1], scale=rstd_n[q][:, PT + t:PT + t + 1])
                    return ins

                there = not before_pair(k, 2)
                if here:
                    keep_turned(0)
                if there:
                    if not before_pair(k, 4):
                        act.wait_ge(sN_outst[q], 32 * (j - 1))
                    turn()
                    second_norm(0, GT)
                if here:
                    keep_turned(1)
                if there:
                    second_norm(GT, ACT_TILES if shared else PT).then_inc(sN["out"], 1)
                if here:
                    if there:
                        act.wait_ge(sN["z2"], k - 1)
                    for w in range(2):
                        act.wait_ge(sN["O"], 2 * k + w + 1)
                        nc.scalar.activation(nh[q][:, w * GT:(w + 1) * GT, :].rearrange("p t d -> p (t d)"), bank[2 + w][:, :],
                                             ACT.Silu).then_inc(sN["h"], 1)

            steps_h(act, lambda s, j, q: nodes(j, q))

            def step_a(s, j, q):
                nodes(j, q, not (isinstance(s, int) and s == STEPS - 1), True)
                for u in range(2):
                    if not (isinstance(s, int) and s < 3):
                        keep_part(s * 2 - 6 + u, u, sA["part"], sA["partev"], 4)

            steps_a(act, step_a)
            nodes(STEPS, 0, False, True)
            for g in range(G - 6, G):
                keep_part(g, g % 2, sA["part"], sA["partev"], 4)

            def tanh_b(g, u):
                act.wait_ge(sB["O"], g + 1)
                free(act, sB["z"], g, R)
                nc.scalar.activation(bh[:, u, :, :].rearrange("p t d -> p (t d)"), bank[3 + AT[u]][:, :], ACT.Tanh).then_inc(sB["h"], 1)

            def step_b(s):
                for u in range(R):
                    g = s * R + u
                    act.wait_ge(sB["A"], g + 1)
                    free(act, sB["O"], g, back3(u))
                    nc.scalar.activation(baT[:, AT[u], :], bank[AT[u]][:, :], ACT.Copy).then_inc(sB["Aev"], 1)
                    if not (first(s) and u == 0):
                        tanh_b(g - 1, (u - 1) % R)

            step_b(0)
            step_b(1)
            with act.Fori(2, RSTEPS) as s:
                step_b(s)
            tanh_b(G - 1, R - 1)

            def gates_c(g, u):
                early = isinstance(g, int) and g < 2
                act.wait_ge(sC["H"], g + 1)
                if not early:
                    act.wait_ge(sC["M"], g - 1)
                nc.scalar.activation(chT[:, u, :], bank[3][:, :], ACT.Silu, bias=b1c[:, 0:1]).then_inc(sC["h"], 1)
                act.wait_ge(sC["G"], g + 1)
                if not early:
                    act.wait_ge(sC["m"], g - 1)
                nc.scalar.activation(cg[:, u, :, :].rearrange("p t d -> p (t d)"), bank[4][:, :], ACT.Tanh, scale=0.5).then_inc(sC["g"], 1)

            def step_c(s):
                for u in range(2):
                    g = s * 2 + u
                    act.wait_ge(sC["T"], g + 1)
                    if not first(s):
                        act.wait_ge(sC["G"], g - 1)
                    nc.scalar.activation(csT[:, u, :], bank[0][:, :], ACT.Copy).then_inc(sC["sT"], 1)
                    nc.scalar.activation(ceT[0:DE, u, :], bank[2][0:DE, :], ACT.Copy).then_inc(sC["eT"], 1)
                    if not (first(s) and u == 0):
                        gates_c(g - 1, 1 - u)
                    if not first(s):
                        keep_part(g - 2, u, sC["part"], sC["partev"], 6)

            step_c(0)
            step_c(1)
            with act.Fori(2, STEPS) as s:
                step_c(s)
            gates_c(G - 1, 1)
            for u in range(2):
                keep_part(G - 2 + u, u, sC["part"], sC["partev"], 6)

            def silu_d(g, u):
                act.wait_ge(sD["O"], g + 1)
                free(act, sD["z"], g, R)
                nc.scalar.activation(dh[:, u, :, :].rearrange("p t d -> p (t d)"), bank[6 + u % 2][:, :], ACT.Silu).then_inc(sD["h"], 1)

            def step_d(s):
                for u in range(R):
                    g = s * R + u
                    free(act, sD["O"], g, back3(u))
                    act.wait_ge(sD["T"], g + 1)
                    nc.scalar.activation(dxT[:, AT[u], :], bank[3 + AT[u]][:, :], ACT.Copy).then_inc(sD["Tev"], 1)
                    act.wait_ge(sD["A"], g + 1)
                    nc.scalar.activation(daT[:, AT[u], :], bank[AT[u]][:, :], ACT.Copy).then_inc(sD["Aev"], 1)
                    if not (first(s) and u == 0):
                        silu_d(g - 1, (u - 1) % R)

            step_d(0)
            step_d(1)
            with act.Fori(2, RSTEPS) as s:
                step_d(s)
            silu_d(G - 1, R - 1)

        @block.tensor
        def _(pe):
            mm = nc.tensor.matmul

            def transpose(dest, src_, parts=P):
                return nc.tensor.transpose(dest, src_, ident[0:parts, 0:parts])

            pe.wait_ge(s_consts, 1)
            pe.wait_ge(s_load, 16 * 16)
            transpose(bank[6][:, 0:P], Wsb[:, :]).then_inc(s_wt, 1)
            pe.wait_ge(s_chain, mark["scans"])
            for c in range(2):
                for n, col in enumerate((scan_lo[:, c, K - 1:K], scan_hi[:, c, 0:1], tile_flags[:, c, 0:1], tile_flags[:, c, 1:2])):
                    at = (n % 2) * 2 * P + c * P
                    ins = transpose(bank[n // 2][0:1, at:at + P], col)
            ins.then_inc(s_pe0, 1)
            pe.wait_ge(s_chain, mark["lines"])
            for a in range(2):
                for c in range(2):
                    transpose(bank[2][:, 2 * a + c:2 * a + c + 1], line_ex[0:1, a, c * P:(c + 1) * P], 1)
            mm(bank[3][:, :], ones[0:1, 0:P], line[0:1, 2:4, :].rearrange("o a b -> o (a b)"), start=True, stop=True).then_inc(s_pe0, 1)
            pe.wait_ge(s_chain, mark["rows"])
            for n in range(6):
                transpose(bank[n][:, 0:P], rows[:, n, 0, :])
                ins = transpose(bank[n][:, P:T], rows[0:T - P, n, 1, :], T - P)
            ins.then_inc(s_pe0, 1)

            mm(bank[7][:, 0:HI], zerosb[:, 0:P], zerosb[:, 0:HI], start=True, stop=False)

            pe.wait_ge(s_chain, mark["weights"])

            def bias_mm(dest, n):
                return mm(dest, onesb[:, :], bias3[:, n, :].unsqueeze(1).to_broadcast([P, GT, D]), start=True, stop=False)

            def tile_at(t):
                return slice(t * P, (t + 1) * P)

            def nodes(j, q):
                k = j * 2 + q
                for w in range(2):
                    pe.wait_ge(sN["x1"], 2 * k + w + 1)
                    if not before_pair(k, 1):
                        pe.wait_ge(sN["Tev"], 2 * k + w - 1)
                    for t in range(GT):
                        ins = transpose(bank[w][:, tile_at(t)], nx1[q][:, w * GT + t, :])
                    ins.then_inc(sN["T"], 1)
                for w in range(2):
                    pe.wait_ge(sN["Tev"], 2 * k + w + 1)
                    if not before_pair(k, 1):
                        pe.wait_ge(sN["h"], 2 * k + w - 1)
                    bias_mm(bank[2 + w][:, :], B_BU)
                    for t in range(GT):
                        ins = mm(bank[2 + w][:, tile_at(t)], nx1T[q][:, w, tile_at(t)], wux[:, :], start=False, stop=t == GT - 1)
                    ins.then_inc(sN["O"], 1)

            def step_h(s, j, q):
                for u in range(2):
                    pe.wait_ge(s_hot, s * 2 + u + 1)
                    for t in range(GT):
                        ins = mm(bank[7][:, 0:HI], hot_lo[0:K, u, t, :], hot_hi[0:K, u, t, :], start=False, stop=False)
                    ins.then_inc(s_hot_used, 1)
                nodes(j, q)

            steps_h(pe, step_h)
            mm(bank[7][:, 0:HI], zerosb[:, 0:P], zerosb[:, 0:HI], start=False, stop=True).then_inc(s_pe0, 1)
            pe.wait_ge(s_chain, mark["counts"])
            mm(bank[5][:, 0:HI], before[:, :], tab[:, 0, :], start=True, stop=True)
            mm(bank[6][:, 0:HI], ones[:, 0:P], tab[:, 0, :], start=True, stop=True).then_inc(s_pe0, 1)
            pe.wait_ge(s_chain, mark["tab"])
            for c in range(HC):
                n = min(P, HI - c * P)
                for w, q in enumerate((5, 6)):
                    ins = transpose(bank[4 + w][0:n, c * P:(c + 1) * P], tab[:, q, c * P:c * P + n])
            ins.then_inc(s_pe0, 1)
            pe.wait_ge(s_chain, mark["tabout"])

            def parts_a(s, turn_, q):
                for u in range(2):
                    g = s * 2 + u
                    slot = 2 * q + u
                    pe.wait_ge(sA_xs[slot], 16 * (turn_ + 1))
                    pe.wait_ge(sA["flw"], g + 1)
                    if not first(s):
                        pe.wait_ge(sA["partev"], g - 1)
                    for t in range(GT):
                        ins = mm(bank[4 + u][:, 2 * t:2 * t + 2], axs[:, slot, t, :], flw[:, slot, t, :], start=t == 0, stop=t == GT - 1)
                    ins.then_inc(sA["part"], 1)

            def step_a(s, j, q):
                if not (isinstance(s, int) and s < 3):
                    parts_a(s - 3, turns_a(j, 1 - q) - (1 if q else 2), 1 - q)
                if not (isinstance(s, int) and s == STEPS - 1):
                    nodes(j, q)

            steps_a(pe, step_a)
            parts_a(STEPS - 3, HALF - 1, 1)
            parts_a(STEPS - 2, HALF - 1, 0)
            parts_a(STEPS - 1, HALF, 1)

            def carry_mm(s_cpe):
                pe.wait_ge(s_cpe, 1)
                for a in range(2):
                    for c in range(2):
                        ins = transpose(bank[6][:, (2 * a + c) * P:(2 * a + c + 1) * P], carry[:, a, c * P:(c + 1) * P])
                ins.then_inc(s_cpe, 1)

            carry_mm(s_cpe0)

            def out_b(g, u):
                pe.wait_ge(sB["Aev"], g + 1)
                free(pe, sB["h"], g, back3(u))
                o = bank[3 + AT[u]]
                bias_mm(o[:, :], B_B)
                for t in range(GT):
                    ins = mm(o[:, tile_at(t)], baT[:, AT[u], tile_at(t)], WT[:, :], start=False, stop=t == GT - 1)
                ins.then_inc(sB["O"], 1)

            def step_b(s):
                for u in range(R):
                    g = s * R + u
                    pe.wait_ge(sB_xs[u], 16 * (s + 1))
                    pe.wait_ge(sB["S"], g + 1)
                    free(pe, sB["Aev"], g, back3(u))
                    for t in range(GT):
                        ins = mm(bank[AT[u]][:, tile_at(t)], bxs[:, u, t, :], bS[:, u, t, :], start=t == 0, stop=t == GT - 1)
                    ins.then_inc(sB["A"], 1)
                    if not (first(s) and u == 0):
                        out_b(g - 1, (u - 1) % R)

            step_b(0)
            step_b(1)
            with pe.Fori(2, RSTEPS) as s:
                step_b(s)
            out_b(G - 1, R - 1)
            pe.wait_ge(sB["h"], G)
            pe.wait_ge(s_carry0, 1)

            def transposes_c(s, u):
                g = s * 2 + u
                pe.wait_ge(sC_xd[u], 16 * (s + 1))
                short = isinstance(g, int) and g == G - 1
                pe.wait_ge(sC_ea[u], 16 * (s + 1) + (16 if short else 0))
                pe.wait_ge(sC_xs[u], 64 * (s + 1))
                if not (first(s) and u == 0):
                    for n in ("sT", "dT", "eT"):
                        pe.wait_ge(sC[n], g)
                for t in range(GT):
                    transpose(bank[0][:, tile_at(t)], cxs[:, u, t, :])
                for t in range(GT):
                    transpose(bank[1][:, tile_at(t)], cxd[:, u, t, :])
                for t in range(GT):
                    ins = transpose(bank[2][0:DE, tile_at(t)], cea[:, u, t, :])
                ins.then_inc(sC["T"], 1)

            def part_c(g, u):
                pe.wait_ge(sC["m"], g + 1)
                pe.wait_ge(sC["cfl"], g + 1)
                if not (isinstance(g, int) and g < 2):
                    pe.wait_ge(sC["partev"], g - 1)
                for t in range(GT):
                    ins = mm(bank[6 + u][:, 2 * t:2 * t + 2], cm[:, u, t, :], cfl[:, u, t, :], start=t == 0, stop=t == GT - 1)
                ins.then_inc(sC["part"], 1)

            def messages_c(g, u):
                for n in ("sT", "dT", "eT"):
                    pe.wait_ge(sC[n], g + 1)
                later = not (isinstance(g, int) and g == 0)
                if later:
                    pe.wait_ge(sC["h"], g)
                mm(bank[3][:, :], w1s[:, :], csT[:, u, :], start=True, stop=False)
                mm(bank[3][:, :], w1d[:, :], cdT[:, u, :], start=False, stop=False)
                mm(bank[3][:, :], w1e[:, :], ceT[0:DE, u, :], start=False, stop=True).then_inc(sC["H"], 1)
                if later:
                    pe.wait_ge(sC["g"], g)
                for t in range(GT):
                    mm(bank[4][:, tile_at(t)], csT[:, u, tile_at(t)], wgs[:, :], start=t == 0, stop=False)
                    mm(bank[4][:, tile_at(t)], cdT[:, u, tile_at(t)], wgd[:, :], start=False, stop=False)
                    ins = mm(bank[4][:, tile_at(t)], ceT[:, u, tile_at(t)], wge[:, :], start=False, stop=t == GT - 1)
                ins.then_inc(sC["G"], 1)
                if later:
                    part_c(g - 1, 1 - u)
                    pe.wait_ge(sC["m"], g)
                pe.wait_ge(sC["h"], g + 1)
                for t in range(GT):
                    ins = mm(bank[5][:, tile_at(t)], chT[:, u, tile_at(t)], w2sb[:, :], start=t == 0, stop=t == GT - 1)
                ins.then_inc(sC["M"], 1)

            def step_c(s):
                for u in range(2):
                    g = s * 2 + u
                    transposes_c(s, u)
                    if not (first(s) and u == 0):
                        messages_c(g - 1, 1 - u)

            step_c(0)
            step_c(1)
            with pe.Fori(2, STEPS - 1) as s:
                step_c(s)
            step_c(STEPS - 1)
            messages_c(G - 1, 1)
            part_c(G - 1, 1)
            pe.wait_ge(sC["partev"], G)
            carry_mm(s_cpe1)

            def out_d(g, u):
                pe.wait_ge(sD["Tev"], g + 1)
                pe.wait_ge(sD["Aev"], g + 1)
                free(pe, sD["h"], g, 2 if u else 1)
                o = bank[6 + u % 2]
                bias_mm(o[:, :], B_BU)
                for t in range(GT):
                    mm(o[:, tile_at(t)], dxT[:, AT[u], tile_at(t)], wux[:, :], start=False, stop=False)
                    ins = mm(o[:, tile_at(t)], daT[:, AT[u], tile_at(t)], wua[:, :], start=False, stop=t == GT - 1)
                ins.then_inc(sD["O"], 1)

            def step_d(s):
                for u in range(R):
                    g = s * R + u
                    pe.wait_ge(sD_xd[u], 16 * (s + 1))
                    free(pe, sD["Tev"], g, back3(u))
                    for t in range(GT):
                        ins = transpose(bank[3 + AT[u]][:, tile_at(t)], dxd[:, u, t, :])
                    ins.then_inc(sD["T"], 1)
                    pe.wait_ge(sD_ms[u], 16 * (s + 1))
                    pe.wait_ge(sD["S"], g + 1)
                    free(pe, sD["Aev"], g, back3(u))
                    for t in range(GT):
                        ins = mm(bank[AT[u]][:, tile_at(t)], dms[:, u, t, :], dS[:, u, t, :], start=t == 0, stop=t == GT - 1)
                    ins.then_inc(sD["A"], 1)
                    if not (first(s) and u == 0):
                        out_d(g - 1, (u - 1) % R)

            step_d(0)
            step_d(1)
            with pe.Fori(2, RSTEPS) as s:
                step_d(s)
            out_d(G - 1, R - 1)

        @block.sync
        def _(sp):
            sp.wait_ge(s_prefill, 1)
            for lst, tile in ((dst, dst_i), (src, src_i)):
                sp.dma_start(tile[:, 0, :], lst[0:P * K].rearrange("(t i) -> t i", i=K)).then_inc(s_idx_ld, 16)
                sp.dma_start(tile[0:C1_TILES - 1, 1, :],
                             lst[P * K:(T_REAL - 1) * K].rearrange("(t i) -> t i", i=K)).then_inc(s_idx_ld, 16)
                sp.dma_start(tile[C1_TILES - 1:C1_TILES, 1, 0:LAST_ROWS],
                             lst[(T_REAL - 1) * K:E].rearrange("(t i) -> t i", t=1)).then_inc(s_idx_ld, 16)
            with nc.allow_non_contiguous_dma(reason="one key per tile"):
                pairs = ((prev_i[1:P, 0:1], K - 1, P - 1), (prev_i[0:C1_TILES, 1:2], P * K - 1, C1_TILES),
                         (next_i[:, 0:1], K, P), (next_i[0:C1_TILES - 1, 1:2], (P + 1) * K, C1_TILES - 1))
                for tile, at, n in pairs:
                    sp.dma_start(tile, dst[at:at + (n - 1) * K + 1].unsqueeze(1)[::K, :]).then_inc(s_idx_ld, 16)
            sp.wait_ge(s_prefill, 2)
            for tile, ap in ((Wsb[:, :], W), (w1s[:, :], w1[0:D, :]), (w1d[:, :], w1[D:2 * D, :]), (w1e[:, :], w1[2 * D:, :]),
                             (wgs[:, :], wg[0:D, :]), (wgd[:, :], wg[D:2 * D, :]), (wge[0:DE, :], wg[2 * D:, :]), (wge[DE:DE + 1, :], bg.unsqueeze(0)),
                             (w2sb[:, :], w2), (wux[:, :], wu[0:D, :]), (wua[:, :], wu[D:, :]),
                             (b1c[:, :], b1.unsqueeze(1))):
                sp.dma_start(tile, ap).then_inc(s_load, 16)
            for n, ap in ((B_B, b), (B_B2, b2), (B_BG, bg), (B_BU, bu)):
                sp.dma_start(bias_in[:, n, :], ap.unsqueeze(0).to_broadcast([P, D])).then_inc(s_load, 16)
            sp.wait_ge(s_chain, mark["keys"])
            sp.dma_start(key_rows[0:P, :], rows[:, QK, 0, :]).then_inc(s_keys, 16)
            sp.dma_start(key_rows[P:T, :], rows[0:T - P, QK, 1, :]).then_inc(s_keys, 16)

            def load_nodes(j, q):
                for w in range(2):
                    g = (j * 2 + q) * 2 + w
                    parts = NG_LAST_P if isinstance(g, int) and g == NG - 1 else P
                    sp.dma_start(nx[q][0:parts, w * GT:(w + 1) * GT, :].rearrange("p j d -> p (j d)"),
                                 nodes_of(x, g, 0, parts)).then_inc(sN_x[q], 16)

            def store_nodes(j, q, tile, table, base, s_done, groups=(0, 1)):
                for w in groups:
                    g = (j * 2 + q) * 2 + w
                    parts = NG_LAST_P if isinstance(g, int) and g == NG - 1 else P
                    sp.dma_start(nodes_of(table, g, base, parts),
                                 tile[0:parts, w * GT:(w + 1) * GT, :].rearrange("p j d -> p (j d)")).then_inc(s_done, 16)

            def nodes(j, q, here=True, ahead=True, shared=False):
                k = j * 2 + q
                if ahead:
                    sp.wait_ge(sN["z1"], k + 1)
                    load_nodes(j + 1, q)
                if here:
                    sp.wait_ge(sN["x1"], 2 * (k + 1))
                    store_nodes(j, q, nx1[q], x1_tab, SLOTS, sN_x1st[q])
                if not before_pair(k, 2):
                    sp.wait_ge(sN["out"], k - 1)
                    store_nodes(j - 1, q, nout[q], out, 0, sN_outst[q], (0,))
                    if shared:
                        sp.wait_ge(sN["out_v"], k + 1 - STEPS)
                    store_nodes(j - 1, q, nout[q], out, 0, sN_outst[q], (1,))

            load_nodes(0, 0)
            load_nodes(0, 1)

            def step_h(s, j, q):
                for u in range(2):
                    slot = 2 * q + u
                    sp.wait_ge(sH_xs[slot], 64 * (j + 1))
                    sp.dma_start(slots_of(src_feat, s * 2 + u), xs[:, slot, :, :]).then_inc(sH_st[slot], 16)
                nodes(j, q)

            steps_h(sp, step_h)
            sp.wait_ge(s_chain, mark["tabout"])
            full = HC - 1
            sp.dma_start(node_tab[0:full * P * P, :].rearrange("(c p l) w -> p c (l w)", p=P, l=P),
                         tab_out[:, 0:full, :, :].rearrange("p c l w -> p c (l w)")).then_inc(s_tab, 16)
            sp.dma_start(node_tab[full * P * P:HI * P, :].rearrange("(p l) w -> p (l w)", l=P),
                         tab_out[0:HI - full * P, full, :, :].rearrange("p l w -> p (l w)")).then_inc(s_tab, 16)

            for q in range(2):
                for u in range(2):
                    sp.wait_ge(sH_st[2 * q + u], 16 * (HALF + 1 - q))

            def load_a(s, u, slot):
                free(sp, sA["part"], s * 2 + u, 4)
                sp.dma_start(axs[:, slot, :, :], slots_of(src_feat, s * 2 + u)).then_inc(sA_xs[slot], 16)

            def step_a(s, j, q):
                end = isinstance(s, int)
                if not (end and s < 1):
                    for u in range(2):
                        load_a(s - 1, u, 2 * (1 - q) + u)
                nodes(j, q, not (end and s == STEPS - 1), not (end and s >= STEPS - 3), True)

            for s in range(3):
                step_a(s, (s + STEPS) // 2, (s + STEPS) % 2)
            with sp.Fori(1, HALF - 2) as i:
                step_a(i * 2 + 1, i + HALF + 1, 0)
                step_a(i * 2 + 2, i + HALF + 1, 1)
            for s in range(STEPS - 4, STEPS):
                step_a(s, (s + STEPS) // 2, (s + STEPS) % 2)
            nodes(STEPS, 0, False, False, True)
            for u in range(2):
                load_a(STEPS - 1, u, 2 + u)

            def load_keys_b(s, u):
                g = s * R + u
                free(sp, sB["S"], g, R)
                sp.dma_start(bkey[:, u, :], key_rows[bass.ds(g * GT, GT), :].rearrange("t s -> (t s)").unsqueeze(0)
                             .to_broadcast([P, GT * P])).then_inc(sB_key[u], 16)

            sp.wait_ge(s_keys, 32)
            for u in range(R):
                load_keys_b(0, u)

            sp.wait_ge(s_carry0, 1)
            for side in range(2):
                for c, n in ((0, P), (1, T - P)):
                    sp.dma_start(src_feat.rearrange("(t s) d -> t s d", s=P)[c * P:c * P + n, K + side, :],
                                 carry_rows[0:n, side, c, :]).then_inc(s_cst0, 16)
            sp.wait_ge(s_cst0, 64)

            def load_b(s, u):
                g = s * R + u
                if not first(s):
                    load_keys_b(s, u)
                free(sp, sB["A"], g, R)
                sp.dma_start(bxs[:, u, :, :], slots_of(src_feat, g)).then_inc(sB_xs[u], 16)

            def store_b(s, u):
                g = s * R + u
                sp.wait_ge(sB["x1"], g + 1)
                sp.dma_start(slots_of(x1_tab, g), bx1[:, u, :, :]).then_inc(sB_st[u], 16)

            def step_b(s):
                if not (isinstance(s, int) and s == RSTEPS - 1):
                    for u in range(R):
                        load_b(s + 1, u)
                if not first(s):
                    for u in range(R):
                        store_b(s - 1, u)

            for u in range(R):
                load_b(0, u)
            steps(sp, step_b, RSTEPS)
            for u in range(R):
                store_b(RSTEPS - 1, u)

            for u in range(R):
                sp.wait_ge(sB_st[u], 16 * RSTEPS)

            def load_c(s, u):
                g = s * 2 + u
                if not first(s):
                    sp.wait_ge(sC["T"], g - 1)
                sp.dma_start(cxd[:, u, :, :], slots_of(x1_tab, g)).then_inc(sC_xd[u], 16)
                at = g * (GT * K)
                if isinstance(g, int) and g == G - 1:
                    full = T_REAL - 1 - g * GT
                    sp.dma_start(cea[0:K, u, 0:full, :],
                                 edge_attr[at:at + full * K, :].rearrange("(t i) d -> i t d", i=K)).then_inc(sC_ea[u], 16)
                    sp.dma_start(cea[0:LAST_ROWS, u, full, :], edge_attr[at + full * K:E, :]).then_inc(sC_ea[u], 16)
                else:
                    sp.dma_start(cea[0:K, u, :, :],
                                 edge_attr[bass.ds(at, GT * K), :].rearrange("(t i) d -> i t d", i=K)).then_inc(sC_ea[u], 16)

            def store_c(g, u):
                sp.wait_ge(sC["m"], g + 1)
                sp.dma_start(slots_of(messages, g), cm[:, u, :, :]).then_inc(sC_st[u], 16)

            def step_c(s):
                for u in range(2):
                    if not (isinstance(s, int) and s == STEPS - 1):
                        load_c(s + 1, u)
                    if not (first(s) and u == 0):
                        store_c(s * 2 + u - 1, 1 - u)

            for u in range(2):
                load_c(0, u)

            def load_keys_d(s, u):
                g = s * R + u
                free(sp, sD["S"], g, R)
                sp.dma_start(dkey[:, u, :], key_rows[bass.ds(g * GT, GT), :].rearrange("t s -> (t s)").unsqueeze(0)
                             .to_broadcast([P, GT * P])).then_inc(sD_key[u], 16)

            def load_residual_d(s, u):
                g = s * R + u
                free(sp, sD["z"], g, R)
                sp.dma_start(dxd[:, u, :, :], slots_of(x1_tab, g)).then_inc(sD_xd[u], 16)

            step_c(0)
            for u in range(R):
                load_keys_d(0, u)
                load_residual_d(0, u)
            with sp.Fori(1, STEPS - 2) as s:
                step_c(s)
            step_c(STEPS - 2)
            step_c(STEPS - 1)
            store_c(G - 1, 1)

            for u in range(2):
                sp.wait_ge(sC_st[u], 16 * STEPS)
            sp.wait_ge(s_carry1, 1)
            for side in range(2):
                for c, n in ((0, P), (1, T - P)):
                    sp.dma_start(messages.rearrange("(t s) d -> t s d", s=P)[c * P:c * P + n, K + side, :],
                                 carry_rows[0:n, side, c, :]).then_inc(s_cst1, 16)
            sp.wait_ge(s_cst1, 64)

            def load_d(s, u):
                g = s * R + u
                if not first(s):
                    load_keys_d(s, u)
                free(sp, sD["A"], g, R)
                sp.dma_start(dms[:, u, :, :], slots_of(messages, g)).then_inc(sD_ms[u], 16)

            for u in range(R):
                load_d(0, u)

            def step_d(s):
                for u in range(R):
                    load_d(s + 1, u)
                for u in range(R):
                    load_residual_d(s + 1, u)

            step_d(0)
            with sp.Fori(1, RSTEPS - 1) as s:
                step_d(s)
            for u in range(R):
                sp.wait_ge(sD_st[u], 64 * RSTEPS)

        @block.gpsimd
        def _(pool):
            nc.gpsimd.iota(iota_i[:, :], pattern=[[1, HI]], base=0, channel_multiplier=0)
            nc.gpsimd.iota(node_i[:, :], pattern=[[P, HI]], base=0, channel_multiplier=1)
            nc.gpsimd.iota(edge_i[:, :, :], pattern=[[P * K, 2], [1, K]], base=0, channel_multiplier=K)
            nc.gpsimd.memset(ones[:, :], 1.0).then_inc(s_mask0, 1)
            pool.wait_ge(s_mask0, 1)
            nc.gpsimd.affine_select(out=ident[:, :], in_=ones[:, 0:P], pattern=[[-1, P]], compare_op=ALU.is_equal,
                                    fill=0.0, base=0, channel_multiplier=1)
            nc.gpsimd.affine_select(out=third_m[:, :], in_=ones[:, 0:3], pattern=[[-1, 3]], compare_op=ALU.is_equal,
                                    fill=0.0, base=0, channel_multiplier=1)
            nc.gpsimd.affine_select(out=before[:, :], in_=ones[:, 0:P], pattern=[[1, P]], compare_op=ALU.is_gt,
                                    fill=0.0, base=0, channel_multiplier=-1).then_inc(s_consts, 1)
            def turn():
                pool.sem_inc(s_pool_turn, 1)

            def take_ids(ids, idx, s, u, s_ids, slot=None):
                g = s * 2 + u
                nc.gpsimd.tensor_copy(ids[:, u if slot is None else slot, :], idx[:, bass.ds(g * GT, GT)]).then_inc(s_ids, 1)
                pool.wait_ge(s_ids, g + 1)
                turn()

            def gather(dest, table, ids, u, t, s_done):
                nc.gpsimd.indirect_dma_start(dest, None, table, bass.IndirectOffsetOnAxis(ap=ids[:, u, t:t + 1], axis=0)
                                             ).then_inc(s_done, 16)

            pool.wait_ge(s_chain, mark["deg"])

            def step_h(s, j, q):
                for u in range(2):
                    slot = 2 * q + u
                    if not before_pair(s, 2):
                        pool.wait_ge(sH_st[slot], 16 * j)
                        turn()
                    take_ids(ids_h, idx_src, s, u, s_hids, slot)
                    for t in range(GT):
                        gather(xs[:, slot, t, :], x[:, :], ids_h, slot, t, sH_xs[slot])

            steps_h(pool, step_h)

            pool.wait_ge(s_tab, 32)

            def step_a(s, j, q):
                for u in range(2):
                    slot = 2 * q + u
                    if not before_pair(s, 2):
                        pool.wait_ge(sA["flw"], s * 2 + u - 3)
                        turn()
                    take_ids(ids_a, idx_src, s, u, sA["ids"], slot)
                    for t in range(GT):
                        gather(tabs[:, slot, t, :], node_tab[:, :], ids_a, slot, t, sA_tab[slot])

            steps_a(pool, step_a)

            for q in range(2):
                for u in range(2):
                    pool.wait_ge(sH_st[2 * q + u], 16 * (HALF + 1 - q))

            def step_b(s):
                for u in range(R):
                    if not first(s):
                        pool.wait_ge(sB["z"], s * R + u - R + 1)
                        turn()
                    pool.wait_ge(sB["ids"], s * R + u + 1)
                    turn()
                    for t in range(GT):
                        gather(bxd[:, u, t, :], x[:, :], ids_b, u, t, sB_xd[u])

            steps(pool, step_b, RSTEPS)

            for u in range(R):
                pool.wait_ge(sB_st[u], 16 * RSTEPS)
            for q in range(2):
                pool.wait_ge(sN_x1st[q], 32 * (STEPS - q))

            def step_c(s):
                for u in range(2):
                    if not first(s):
                        pool.wait_ge(sC["T"], s * 2 + u - 1)
                        turn()
                    take_ids(ids_c, idx_x1, s, u, sC["ids"])
                    for t in range(GT):
                        gather(cxs[:, u, t, :], x1_tab[:, :], ids_c, u, t, sC_xs[u])

            steps(pool, step_c)

            for q in range(2):
                pool.wait_ge(sN_outst[q], 32 * (STEPS - q))

            def step_d(s):
                for u in range(R):
                    pool.wait_ge(sD["ids"], s * R + u + 1)
                    turn()
                    pool.wait_ge(sD["out"], s * R + u + 1)
                    turn()
                    for t in range(GT):
                        nc.gpsimd.indirect_dma_start(out[:, :], bass.IndirectOffsetOnAxis(ap=ids_d[:, u, t:t + 1], axis=0),
                                                     dout[:, u, t, :], None, bounds_check=N - 1, oob_is_err=False
                                                     ).then_inc(sD_st[u], 16)

            steps(pool, step_d, RSTEPS)


_INS = ["x", "src", "dst", "edge_attr_64", "L0_gnn_W", "L0_gnn_b", "L1_gnn_w1", "L1_gnn_b1", "L1_gnn_w2", "L1_gnn_b2",
        "L1_gnn_wg", "L1_gnn_bg", "L1_gnn_wu", "L1_gnn_bu"]


def kernel(**inputs):
    import concourse.bacc as _bacc
    from concourse.bass_utils import run_bass_kernel_spmd as _run

    nc = _bacc.Bacc("TRN2", target_bir_lowering=False, num_devices=1)
    arrays, args = {}, []
    for name in _INS:
        a = np.ascontiguousarray(inputs[name])
        arrays[f"in_{name}_dram"] = a
        args.append(nc.dram_tensor(f"in_{name}_dram", a.shape, mybir.dt.from_np(a.dtype), kind="ExternalInput").ap())
    shape = inputs["x"].shape
    args.append(nc.dram_tensor("out_dram", shape, F32, kind="ExternalOutput").ap())
    gnn_kernel(nc, *args)
    r = _run(nc, [arrays], core_ids=[0])
    return r.results[0]["out_dram"]
```
